# Optimizing a Trainium2 kernel written in Bass

```python
import numpy as np
import jax
import jax.numpy as jnp

def _softmax(x, axis=-1):
    return jax.nn.softmax(x, axis=axis)

def _gelu(x):
    return jax.nn.gelu(x, approximate=True)

def _silu(x):
    return jax.nn.silu(x)

def _sigmoid(x):
    return jax.nn.sigmoid(x)

def _layernorm(x, axis=-1, eps=1e-05):
    m = jnp.mean(x, axis=axis, keepdims=True)
    v = jnp.var(x, axis=axis, keepdims=True)
    return (x - m) / jnp.sqrt(v + eps)

def _scatter_add(tgt, idx, src, axis=0):
    return tgt.at[idx].add(src)

def _segment_sum(src, seg, n):
    return jax.ops.segment_sum(src, seg, n)
kernel_name = 'mk_decoder_preln_d2_seqx_r8_a1cbea'

def setup_inputs(seed: int=0):
    np.random.seed(seed)
    _w = jnp.asarray

    def _rec_inputs():
        import jax
        import jax.numpy as jnp
        _rk = jax.random.key(seed)
        x = -0.0002928 + 1 * jax.random.normal(jax.random.fold_in(_rk, 1), (8, 128, 256), jnp.float32)
        _lenS = 128 - jax.random.randint(jax.random.fold_in(_rk, 7), (8,), 0, max(1, 128 // 4) + 1, jnp.int32)
        _lenS2 = 128 - jax.random.randint(jax.random.fold_in(_rk, 8), (8,), 0, max(1, 128 // 4) + 1, jnp.int32)
        fside_S2_0 = -0.00337071 + 1.01897 * jax.random.normal(jax.random.fold_in(_rk, 11), (128,), jnp.float32)
        _ctx_2048P = jax.random.normal(jax.random.fold_in(_rk, 12), (8, 16, 256), jnp.float32)
        _ctx_2048c = jax.random.dirichlet(jax.random.fold_in(_rk, 512), 0.3 * jnp.ones((16,), jnp.float32), (8, 128))
        _ctx_2048t = jnp.einsum('bsk,bkd->bsd', _ctx_2048c, _ctx_2048P)
        _ctx_2048t = _ctx_2048t * jax.lax.rsqrt(jnp.mean(jnp.square(_ctx_2048t)) + 1e-12) * 0.953939
        ctx_2048 = 0.000675642 + 1.00031 * (_ctx_2048t + 0.3 * jax.random.normal(jax.random.fold_in(_rk, 612), (8, 128, 256), jnp.float32))
        return (x, fside_S2_0, ctx_2048)
    x, fside_S2_0, ctx_2048 = _rec_inputs()

    def _L0_attn_setup():
        import jax, jax.numpy as jnp
        import numpy as np
        NUM_HEADS = 16

        def _l2_normalize_complex(z):
            n = jnp.sqrt(jnp.sum(jnp.abs(z) ** 2, axis=-1, keepdims=True))
            return z / n
        key = jax.random.key(seed)
        k1, k2, k3, k4 = jax.random.split(key, 4)
        B, S, D = (4, 512, 256)
        scale = 1.0 / np.sqrt(D)
        return {'x': jax.random.normal(k1, (B, S, D), dtype=jnp.float32), 'W_q': jax.random.normal(k2, (D, D), dtype=jnp.float32) * scale, 'W_kv': jax.random.normal(k3, (D, D), dtype=jnp.float32) * scale, 'W_o': jax.random.normal(k4, (D, D), dtype=jnp.float32) * scale}
    _L0_attn_all = _L0_attn_setup()
    _L0_attn_in = {k: v for k, v in _L0_attn_all.items() if k in ('W_q', 'W_kv', 'W_o')}
    del _L0_attn_all

    def _L0_xattn_setup():
        import jax, jax.numpy as jnp
        import numpy as np
        key = jax.random.key(seed)
        ks = jax.random.split(key, 5)
        B, D, L, NH = (2, 128, 256, 8)
        H = D // NH
        return {'v': jax.random.normal(ks[0], (B, D, L), jnp.float32), 'k': jax.random.normal(ks[1], (H, L), jnp.float32) * 0.1, 'bias': jax.random.normal(ks[2], (D,), jnp.float32), 'x1': jax.random.normal(ks[3], (B, D, L), jnp.float32), 'x2': jax.random.normal(ks[4], (B, D, L), jnp.float32), 'num_heads': NH}
    _L0_xattn_all = _L0_xattn_setup()
    _L0_xattn_in = {k: v for k, v in _L0_xattn_all.items() if k in ('k',)}
    del _L0_xattn_all

    def _L0_ffn_setup():
        import jax, jax.numpy as jnp
        import numpy as np
        B, S, D = (4, 128, 256)
        H = 512
        NE = 8
        TOPK = 2
        key = jax.random.key(seed)
        ks = jax.random.split(key, 9)
        s = lambda fan_in: 1.0 / np.sqrt(fan_in)
        return {'x': jax.random.normal(ks[0], (B, S, D), dtype=jnp.float32), 'W1': jax.random.normal(ks[1], (NE, D, H), dtype=jnp.float32) * s(D), 'b1': jnp.zeros((NE, H), dtype=jnp.float32), 'W2': jax.random.normal(ks[2], (NE, H, H), dtype=jnp.float32) * s(H), 'b2': jnp.zeros((NE, H), dtype=jnp.float32), 'W3': jax.random.normal(ks[3], (NE, H, D), dtype=jnp.float32) * s(H), 'b3': jnp.zeros((NE, D), dtype=jnp.float32), 'Wg': jax.random.normal(ks[4], (D, NE), dtype=jnp.float32) * s(D), 'bg': jnp.zeros((NE,), dtype=jnp.float32)}
    _L0_ffn_all = _L0_ffn_setup()
    _L0_ffn_in = {k: v for k, v in _L0_ffn_all.items() if k in ('W1', 'b1', 'W2', 'b2', 'W3', 'b3', 'Wg', 'bg')}
    del _L0_ffn_all

    def _L1_attn_setup():
        import jax, jax.numpy as jnp
        import numpy as np
        B, S, D = (2, 256, 256)
        H = 16
        Q_LORA, KV_LORA = (192, 64)
        ROPE_DIM, NOPE_DIM, V_DIM = (64, 64, 128)
        Q_HEAD_DIM = NOPE_DIM + ROPE_DIM
        ROPE_THETA, ROPE_RATIO = (10000.0, 1.0)

        def _rope_tables(seq_len):
            half = ROPE_DIM // 2
            inv_freq = ROPE_RATIO / ROPE_THETA ** (jnp.arange(half, dtype=jnp.float32) * 2.0 / ROPE_DIM)
            freqs = jnp.arange(seq_len, dtype=jnp.float32)[:, None] * inv_freq[None, :]
            return (jnp.cos(freqs), jnp.sin(freqs))

        def _apply_rope(x, cos, sin):
            x_even = x[..., 0::2]
            x_odd = x[..., 1::2]
            r_even = x_even * cos - x_odd * sin
            r_odd = x_odd * cos + x_even * sin
            return jnp.stack([r_even, r_odd], axis=-1).reshape(x.shape)
        key = jax.random.key(seed)
        ks = jax.random.split(key, 6)
        std = 0.02
        return {'hidden_states': jax.random.normal(ks[0], (B, S, D), jnp.float32), 'Wqa': jax.random.normal(ks[1], (D, Q_LORA), jnp.float32) * std, 'Wqb': jax.random.normal(ks[2], (Q_LORA, H * Q_HEAD_DIM), jnp.float32) * std, 'Wkva': jax.random.normal(ks[3], (D, KV_LORA + ROPE_DIM), jnp.float32) * std, 'Wkvb': jax.random.normal(ks[4], (KV_LORA, H * (NOPE_DIM + V_DIM)), jnp.float32) * std, 'Wo': jax.random.normal(ks[5], (H * V_DIM, D), jnp.float32) * std}
    _L1_attn_all = _L1_attn_setup()
    _L1_attn_in = {k: v for k, v in _L1_attn_all.items() if k in ('Wqa', 'Wqb', 'Wkva', 'Wkvb', 'Wo')}
    del _L1_attn_all

    def _L1_xattn_setup():
        import jax, jax.numpy as jnp
        import numpy as np
        NUM_HEADS = 16

        def _qdq(x):
            s = jnp.maximum(jnp.max(jnp.abs(x), axis=-1, keepdims=True) / 127.0, 1e-08)
            return jnp.clip(jnp.round(x / s), -127.0, 127.0) * s
        key = jax.random.key(seed)
        ks = jax.random.split(key, 8)
        B, N, M, D = (2, 512, 64, 256)
        w_std = 0.02
        return {'x': jax.random.normal(ks[0], (B, N, D), jnp.float32), 'cond': jax.random.normal(ks[1], (B, M, D), jnp.float32), 'wq': jax.random.normal(ks[2], (D, D), jnp.float32) * w_std, 'bq': jax.random.normal(ks[3], (D,), jnp.float32) * w_std, 'wkv': jax.random.normal(ks[4], (2 * D, D), jnp.float32) * w_std, 'bkv': jax.random.normal(ks[5], (2 * D,), jnp.float32) * w_std, 'wp': jax.random.normal(ks[6], (D, D), jnp.float32) * w_std, 'bp': jax.random.normal(ks[7], (D,), jnp.float32) * w_std}
    _L1_xattn_all = _L1_xattn_setup()
    _L1_xattn_in = {k: v for k, v in _L1_xattn_all.items() if k in ('wq', 'bq', 'wkv', 'bkv', 'wp', 'bp')}
    del _L1_xattn_all

    def _L1_ffn_setup():
        import jax, jax.numpy as jnp
        import numpy as np
        EPS = 1e-05

        def _quant_weight(w):
            scale = jnp.mean(jnp.abs(w)) + EPS
            wq = jnp.clip(jnp.round(w / scale), -1.0, 1.0)
            return (wq, scale)

        def _quant_act(x):
            s = jnp.max(jnp.abs(x), axis=-1, keepdims=True) / 127.0 + EPS
            xq = jnp.clip(jnp.round(x / s), -128.0, 127.0)
            return (xq, s)

        def _qlinear(x, w):
            wq, ws = _quant_weight(w)
            xq, xs = _quant_act(x)
            y = jnp.einsum('bsi,oi->bso', xq, wq)
            return y * xs * ws
        key = jax.random.key(seed)
        k1, k2, k3, k4 = jax.random.split(key, 4)
        H, I = (256, 1024)
        x = jax.random.normal(k1, (4, 512, H), dtype=jnp.float32)
        w_gate = jax.random.normal(k2, (I, H), dtype=jnp.float32) * (1.0 / np.sqrt(H))
        w_up = jax.random.normal(k3, (I, H), dtype=jnp.float32) * (1.0 / np.sqrt(H))
        w_down = jax.random.normal(k4, (H, I), dtype=jnp.float32) * (1.0 / np.sqrt(I))
        return {'x': x, 'w_gate': w_gate, 'w_up': w_up, 'w_down': w_down}
    _L1_ffn_all = _L1_ffn_setup()
    _L1_ffn_in = {k: v for k, v in _L1_ffn_all.items() if k in ('w_gate', 'w_up', 'w_down')}
    del _L1_ffn_all
    return {'x': x, 'fside_S2_0': fside_S2_0, 'ctx_2048': ctx_2048, 'L0_attn_W_q': _L0_attn_in['W_q'], 'L0_attn_W_kv': _L0_attn_in['W_kv'], 'L0_attn_W_o': _L0_attn_in['W_o'], 'L0_xattn_k': _L0_xattn_in['k'], 'L0_ffn_W1': _L0_ffn_in['W1'], 'L0_ffn_b1': _L0_ffn_in['b1'], 'L0_ffn_W2': _L0_ffn_in['W2'], 'L0_ffn_b2': _L0_ffn_in['b2'], 'L0_ffn_W3': _L0_ffn_in['W3'], 'L0_ffn_b3': _L0_ffn_in['b3'], 'L0_ffn_Wg': _L0_ffn_in['Wg'], 'L0_ffn_bg': _L0_ffn_in['bg'], 'L1_attn_Wqa': _L1_attn_in['Wqa'], 'L1_attn_Wqb': _L1_attn_in['Wqb'], 'L1_attn_Wkva': _L1_attn_in['Wkva'], 'L1_attn_Wkvb': _L1_attn_in['Wkvb'], 'L1_attn_Wo': _L1_attn_in['Wo'], 'L1_xattn_wq': _L1_xattn_in['wq'], 'L1_xattn_bq': _L1_xattn_in['bq'], 'L1_xattn_wkv': _L1_xattn_in['wkv'], 'L1_xattn_bkv': _L1_xattn_in['bkv'], 'L1_xattn_wp': _L1_xattn_in['wp'], 'L1_xattn_bp': _L1_xattn_in['bp'], 'L1_ffn_w_gate': _L1_ffn_in['w_gate'], 'L1_ffn_w_up': _L1_ffn_in['w_up'], 'L1_ffn_w_down': _L1_ffn_in['w_down']}

def reference(x, fside_S2_0, ctx_2048, L0_attn_W_q, L0_attn_W_kv, L0_attn_W_o, L0_xattn_k, L0_ffn_W1, L0_ffn_b1, L0_ffn_W2, L0_ffn_b2, L0_ffn_W3, L0_ffn_b3, L0_ffn_Wg, L0_ffn_bg, L1_attn_Wqa, L1_attn_Wqb, L1_attn_Wkva, L1_attn_Wkvb, L1_attn_Wo, L1_xattn_wq, L1_xattn_bq, L1_xattn_wkv, L1_xattn_bkv, L1_xattn_wp, L1_xattn_bp, L1_ffn_w_gate, L1_ffn_w_up, L1_ffn_w_down):
    import jax
    import jax.numpy as jnp

    def _L0_attn_ref(x, W_q, W_kv, W_o):
        import jax, jax.numpy as jnp
        import numpy as np
        NUM_HEADS = 16

        def _l2_normalize_complex(z):
            n = jnp.sqrt(jnp.sum(jnp.abs(z) ** 2, axis=-1, keepdims=True))
            return z / n
        B, S, D = x.shape
        H = NUM_HEADS
        hd = D // H
        q = (x @ W_q.T).reshape(B, S, H, hd)
        kv = (x @ W_kv.T).reshape(B, S, H, hd)
        qf = jnp.fft.fft(q, axis=-1)
        kvf = jnp.fft.fft(kv, axis=-1)
        qf = _l2_normalize_complex(qf)
        kvf = _l2_normalize_complex(kvf)
        kvf = jnp.cumsum(kvf, axis=1)
        qv = qf * kvf
        values_hat = jnp.fft.ifft(qv, axis=-1).real.astype(x.dtype)
        values_hat = values_hat.reshape(B, S, D)
        return values_hat @ W_o.T

    def _L0_xattn_ref(v, k, bias, x1, x2, num_heads):
        import jax, jax.numpy as jnp
        import numpy as np
        B, D, L = v.shape
        H = D // num_heads
        fft_size = 2 * L
        vr = v.reshape(B, H, num_heads, L)
        x1r = x1.reshape(B, H, num_heads, L)
        x2r = x2.reshape(B, H, num_heads, L)
        kv = vr[:, :, :, None, :] * x2r[:, :, None, :, :]
        k_f = jnp.fft.rfft(k.astype(jnp.float32), n=fft_size)
        y = jnp.fft.irfft(jnp.fft.rfft(kv, n=fft_size) * k_f[None, :, None, None, :], n=fft_size)[..., :L]
        skip = bias.astype(jnp.float32).reshape(H, num_heads)[None, :, :, None, None]
        y = y + kv * skip
        out = jnp.einsum('bhijl,bhil->bhjl', y, x1r)
        return out.reshape(B, D, L)

    def _L0_ffn_ref(x, W1, b1, W2, b2, W3, b3, Wg, bg):
        import jax, jax.numpy as jnp
        import numpy as np
        B, S, D = (4, 128, 256)
        H = 512
        NE = 8
        TOPK = 2
        gate_logits = jnp.einsum('bsd,dn->bsn', x, Wg) + bg
        gate_weights = jax.nn.softmax(gate_logits, axis=-1)
        topv, topi = jax.lax.top_k(gate_weights, TOPK)
        h = jax.nn.gelu(jnp.einsum('bsd,ndh->nbsh', x, W1) + b1[:, None, None, :], approximate=False)
        h = jax.nn.gelu(jnp.einsum('nbsh,nhf->nbsf', h, W2) + b2[:, None, None, :], approximate=False)
        eo = jnp.einsum('nbsf,nfd->nbsd', h, W3) + b3[:, None, None, :]
        comb = jnp.sum(jax.nn.one_hot(topi, NE, dtype=x.dtype) * topv[..., None], axis=-2)
        out = jnp.einsum('nbsd,bsn->bsd', eo, comb)
        return out

    def _L1_attn_ref(hidden_states, Wqa, Wqb, Wkva, Wkvb, Wo):
        import jax, jax.numpy as jnp
        import numpy as np
        B, S, D = (2, 256, 256)
        H = 16
        Q_LORA, KV_LORA = (192, 64)
        ROPE_DIM, NOPE_DIM, V_DIM = (64, 64, 128)
        Q_HEAD_DIM = NOPE_DIM + ROPE_DIM
        ROPE_THETA, ROPE_RATIO = (10000.0, 1.0)

        def _rope_tables(seq_len):
            half = ROPE_DIM // 2
            inv_freq = ROPE_RATIO / ROPE_THETA ** (jnp.arange(half, dtype=jnp.float32) * 2.0 / ROPE_DIM)
            freqs = jnp.arange(seq_len, dtype=jnp.float32)[:, None] * inv_freq[None, :]
            return (jnp.cos(freqs), jnp.sin(freqs))

        def _apply_rope(x, cos, sin):
            x_even = x[..., 0::2]
            x_odd = x[..., 1::2]
            r_even = x_even * cos - x_odd * sin
            r_odd = x_odd * cos + x_even * sin
            return jnp.stack([r_even, r_odd], axis=-1).reshape(x.shape)
        b, s, _ = hidden_states.shape
        scale = Q_HEAD_DIM ** (-0.5)
        q_latent = hidden_states @ Wqa
        q = (q_latent @ Wqb).reshape(b, s, H, Q_HEAD_DIM)
        q = jnp.transpose(q, (0, 2, 1, 3))
        q_nope, q_pe = (q[..., :NOPE_DIM], q[..., NOPE_DIM:])
        kv_comp = hidden_states @ Wkva
        c_kv, k_pe = (kv_comp[..., :KV_LORA], kv_comp[..., KV_LORA:])
        cos, sin = _rope_tables(s)
        q_pe = _apply_rope(q_pe, cos, sin)
        k_pe = _apply_rope(k_pe, cos, sin)
        kv = (c_kv @ Wkvb).reshape(b, s, H, NOPE_DIM + V_DIM)
        kv = jnp.transpose(kv, (0, 2, 1, 3))
        k_nope, v = (kv[..., :NOPE_DIM], kv[..., NOPE_DIM:])
        k_pe_b = jnp.broadcast_to(k_pe[:, None], (b, H, s, ROPE_DIM))
        q_full = jnp.concatenate([q_nope, q_pe], axis=-1)
        k_full = jnp.concatenate([k_nope, k_pe_b], axis=-1)
        scores = jnp.einsum('bhqd,bhkd->bhqk', q_full, k_full) * scale
        causal = jnp.tril(jnp.ones((s, s), dtype=bool))
        scores = jnp.where(causal[None, None], scores, jnp.finfo(scores.dtype).min)
        probs = jax.nn.softmax(scores, axis=-1)
        attn = jnp.einsum('bhqk,bhkd->bhqd', probs, v)
        out = jnp.transpose(attn, (0, 2, 1, 3)).reshape(b, s, H * V_DIM)
        return out @ Wo

    def _L1_xattn_ref(x, cond, wq, bq, wkv, bkv, wp, bp):
        import jax, jax.numpy as jnp
        import numpy as np
        NUM_HEADS = 16

        def _qdq(x):
            s = jnp.maximum(jnp.max(jnp.abs(x), axis=-1, keepdims=True) / 127.0, 1e-08)
            return jnp.clip(jnp.round(x / s), -127.0, 127.0) * s
        B, N, C = x.shape
        M = cond.shape[1]
        H = NUM_HEADS
        Dh = C // H
        q = _qdq(x) @ _qdq(wq).T + bq
        kv = cond @ wkv.T + bkv
        k, v = jnp.split(kv, 2, axis=-1)
        q = q.reshape(B, N, H, Dh)
        k = k.reshape(B, M, H, Dh)
        v = v.reshape(B, M, H, Dh)
        scale = 1.0 / np.sqrt(Dh)
        attn = jax.nn.softmax(jnp.einsum('bnhd,bmhd->bhnm', q, k) * scale, axis=-1)
        o = jnp.einsum('bhnm,bmhd->bnhd', attn, v).reshape(B, N, C)
        out = _qdq(o) @ _qdq(wp).T + bp
        return out

    def _L1_ffn_ref(x, w_gate, w_up, w_down):
        import jax, jax.numpy as jnp
        import numpy as np
        EPS = 1e-05

        def _quant_weight(w):
            scale = jnp.mean(jnp.abs(w)) + EPS
            wq = jnp.clip(jnp.round(w / scale), -1.0, 1.0)
            return (wq, scale)

        def _quant_act(x):
            s = jnp.max(jnp.abs(x), axis=-1, keepdims=True) / 127.0 + EPS
            xq = jnp.clip(jnp.round(x / s), -128.0, 127.0)
            return (xq, s)

        def _qlinear(x, w):
            wq, ws = _quant_weight(w)
            xq, xs = _quant_act(x)
            y = jnp.einsum('bsi,oi->bso', xq, wq)
            return y * xs * ws
        gate = jax.nn.silu(_qlinear(x, w_gate))
        up = _qlinear(x, w_up)
        return _qlinear(gate * up, w_down)
    x = x + _L0_attn_ref(_layernorm(x, axis=-1), L0_attn_W_q, L0_attn_W_kv, L0_attn_W_o)
    x = x + _L0_xattn_ref(_layernorm(x, axis=-1), L0_xattn_k, fside_S2_0, ctx_2048, ctx_2048, 8)
    x = x + _L0_ffn_ref(_layernorm(x, axis=-1), L0_ffn_W1, L0_ffn_b1, L0_ffn_W2, L0_ffn_b2, L0_ffn_W3, L0_ffn_b3, L0_ffn_Wg, L0_ffn_bg)
    x = x + _L1_attn_ref(_layernorm(x, axis=-1), L1_attn_Wqa, L1_attn_Wqb, L1_attn_Wkva, L1_attn_Wkvb, L1_attn_Wo)
    x = x + _L1_xattn_ref(_layernorm(x, axis=-1), ctx_2048, L1_xattn_wq, L1_xattn_bq, L1_xattn_wkv, L1_xattn_bkv, L1_xattn_wp, L1_xattn_bp)
    x = x + _L1_ffn_ref(_layernorm(x, axis=-1), L1_ffn_w_gate, L1_ffn_w_up, L1_ffn_w_down)
    return x

_drawn_inputs = setup_inputs


def setup_inputs(seed=0):
    import zlib

    import numpy as np

    out = dict(_drawn_inputs(seed))
    spreads = {'L0_ffn_b1': (0.0, 0.8),
     'L0_ffn_b2': (0.0, 0.8),
     'L0_ffn_b3': (0.0, 0.8),
     'L0_ffn_bg': (0.0, 0.8)}
    factors = {'L1_attn_Wqa': 8.0,
     'L1_attn_Wqb': 8.0,
     'L1_attn_Wkva': 8.0,
     'L1_attn_Wkvb': 8.0,
     'L1_attn_Wo': 8.0,
     'L1_xattn_wq': 8.0,
     'L1_xattn_bq': 43.634,
     'L1_xattn_wkv': 5.448,
     'L1_xattn_bkv': 38.257,
     'L1_xattn_wp': 5.553,
     'L1_xattn_bp': 64.0,
     'L1_ffn_w_gate': 8.0,
     'L1_ffn_w_up': 8.0,
     'L1_ffn_w_down': 8.0}
    for name, (base, spread) in spreads.items():
        noise = np.random.default_rng([zlib.crc32(name.encode()), seed]).standard_normal(out[name].shape)
        drawn = base * np.exp(spread * noise) if base else spread * noise
        out[name] = jnp.asarray(drawn.astype(out[name].dtype))
    for name, factor in factors.items():
        out[name] = (out[name] * factor).astype(out[name].dtype)
    return out
```

```python
from contextlib import ExitStack

import numpy as np

import concourse.bass as bass
from concourse import mybir

P = 128
NT = 8
D = 256
DC = D // P
NE = 8
FH = 512
FC = FH // P
CH = 8
HG = P // CH
H4 = 16
QL = 192
S4 = float(np.float32(P) ** np.float32(-0.5))
ROUND = 12582912.0
EPS = 1e-5
LAST_STAGE = 6

ALU = mybir.AluOpType
ACT = mybir.ActivationFunctionType
AX = mybir.AxisListType
F32 = mybir.dt.float32
F16 = mybir.dt.float16
BF16 = mybir.dt.bfloat16
U32 = mybir.dt.uint32


def shape_constants():
    n = np.arange(16)
    parts = {}
    parts["ident"] = np.eye(P)
    parts["upper"] = np.triu(np.ones((P, P)))
    parts["reverse"] = np.eye(P)[::-1]
    parts["group8"] = np.kron(np.eye(HG), np.ones((CH, CH)))
    parts["ones"] = np.ones((P, P))
    f = np.zeros((D, 2, 16, 8))
    c = np.zeros((3, 16, 8, D))
    for h in range(16):
        for k in range(8):
            s = slice(16 * h, 16 * h + 16)
            co, si = np.cos(2 * np.pi * k * n / 16), np.sin(2 * np.pi * k * n / 16)
            f[s, 0, h, k] = 0.25 if k == 0 else co * np.sqrt(2) / 4
            f[s, 1, h, k] = 0.25 * (-1.0) ** n if k == 0 else si * np.sqrt(2) / 4
            c[0, h, k, s] = co / 16
            c[1, h, k, s] = (-1.0) ** n / 16 if k == 0 else -co / 16
            c[2, h, k, s] = si / 16
    f = f.reshape(D, D)
    parts["fourier"] = np.concatenate([f[:P], f[P:]], 1)
    ct = c.reshape(3 * P, D).T
    parts["inverse"] = np.concatenate([ct[:P], ct[P:]], 1)
    inv = 1.0 / 10000.0 ** (np.arange(32, dtype=np.float32) * np.float32(2.0) / np.float32(64))
    ang = (np.arange(P, dtype=np.float32)[:, None] * inv.astype(np.float32)[None, :]).astype(np.float32)
    parts["cos"] = np.repeat(np.cos(ang), 2, axis=1)
    parts["sin"] = np.stack([-np.sin(ang), np.sin(ang)], axis=2).reshape(P, 64)
    parts["causal"] = np.where(np.tril(np.ones((P, P))) > 0, 0.0, -1e30)
    parts["head16"] = np.kron(np.eye(8), np.ones((16, 1))) * 0.25
    parts["iota8"] = np.tile(np.arange(8.0), (P, 1))
    at, cols = {}, 0
    for name, a in parts.items():
        at[name] = (cols, cols + a.shape[1])
        cols += a.shape[1]
    return np.concatenate(list(parts.values()), 1).astype(np.float32), at


CONST_AT = shape_constants()[1]


def decoder_kernel(nc, a, out):
    with ExitStack() as ctx:
        named = {}

        def sem(name):
            if name not in named:
                named[name] = ctx.enter_context(nc.semaphore(name))
            return named[name]

        def sb(name, shape, dt=F32, scope=ctx):
            return scope.enter_context(nc.sbuf_tensor(name, shape, dt))

        bank = [ctx.enter_context(nc.psum_tensor(f"bank{k}", [P, 512], F32)) for k in range(8)]

        ncol = max(hi for _, hi in CONST_AT.values())
        const = sb("const", [P, ncol])
        cst = {name: const[:, lo:hi] for name, (lo, hi) in CONST_AT.items()}
        x = sb("x", [P, NT, D])
        cx = sb("cx", [P, NT, D])
        cxT = sb("cxT", [P, DC, NT, P])
        xn = sb("xn", [P, NT, D])
        xnT = sb("xnT", [P, DC, NT, P])
        st = sb("st", [P, NT, 6])
        mv = sb("mv", [P, NT, 2])
        ve = sb("ve", [P, NT])
        sd = sb("sd", [P, NT])
        rs = sb("rs", [P, NT, 2])
        nw = sb("nw", [P, 2, NT])

        b12 = sb("b12", [2 * NE * FC, P], F32)
        identb = sb("identb", [P, P], BF16)
        xsc = sb("xsc", [P, 3, NT])
        fws = sb("fws", [P, 4, 3])
        fsg = sb("fsg", [P, NT, 2])
        fsn = sb("fsn", [P, 2, 2])
        fsd = sb("fsd", [P, 2, 4])
        be = sb("be", [P, 2, 2, FC])
        bT = sb("bT", [P, 2 * NE * FC], F32)
        b3 = sb("b3", [NE, D], F32)
        wg = sb("wg", [P, DC, NE], F32)
        bg = sb("bg", [P, NE], F32)
        lg = sb("lg", [P, NT, NE], F32)
        gm = sb("gm", [P, NT], F32)
        gs = sb("gs", [P, 2, NT], F32)
        gw = sb("gw", [P, NT, NE], F32)
        top = sb("top", [P, NT, 8], F32)
        topi = sb("topi", [P, NT, 8], U32)
        topf = sb("topf", [P, NT, 8], F32)
        pick = sb("pick", [P, 2, NT, NE], F32)
        comb = sb("comb", [P, NT, NE], F32)
        combT = sb("combT", [NE, NT, P], F32)
        s1, s2 = ExitStack(), ExitStack()
        wq = sb("wq", [P, DC, D], F32, s1)
        wkv = sb("wkv", [P, DC, D], F32, s1)
        wo = sb("wo", [P, DC, D], F32, s1)
        woT = sb("woT", [P, DC, D], F32, s1)
        toF = sb("toF", [P, DC, 2 * D], F32, s1)
        toO = sb("toO", [P, 3, D], F32, s1)
        sq = sb("sq", [P, 2, 512], F32, s1)
        ss = sb("ss", [P, NT * 32], F32, s1)
        sn = sb("sn", [P, NT * 32], F32, s1)
        rn = sb("rn", [P, 2, NT * 32], F32, s1)
        nn = sb("nn", [P, 2, NT * 32], F32, s1)
        qk = sb("qk", [P, NT, 512], F32, s1)
        kqT = sb("kqT", [P, NT, 512], F32, s1)
        pr = sb("pr", [P, NT, 4, P], F32, s1)
        tapR = sb("tapR", [P, HG, D], F32, s2)
        tap = sb("tap", [P, HG, D], F32, s2)
        skip = sb("skip", [P, 1], F32, s2)
        wsk = sb("wsk", [P, NT, D], F32, s2)
        sk2 = sb("sk2", [P, 2, 512], F32, s2)
        kvp = sb("kvp", [P, 2, DC, 512], F32, s2)
        yx = sb("yx", [P, 2, 512], F32, s2)
        yT = sb("yT", [P, DC, NT, P], F32, s2)

        s2.close()
        s1.close()
        s3 = ExitStack()
        xh = sb("xh", [P, DC, NT * P], F16, s3)
        xl = sb("xl", [P, DC, NT * P], F16, s3)
        WE = 2 * 2 * FH + FC * D + 2 * FH
        wraw = sb("wraw", [P, WE], F32, s3)
        whi = sb("whi", [P, 2, WE], F16, s3)
        wlo = sb("wlo", [P, 2, WE], F16, s3)
        hf = sb("hf", [P, FC, 512], F32, s3)
        h1 = sb("h1", [P, 2, 2, FC, 512], F16, s3)
        h2 = sb("h2", [P, 2, 2, FC, 512], F16, s3)


        s4w = ExitStack()
        wqa = sb("wqa", [P, DC, QL], F32, s4w)
        wkva = sb("wkva", [P, DC, P], F32, s4w)
        wqb = sb("wqb", [P, 2, H4, P], F32, s4w)
        wkvb = sb("wkvb", [64, H4, 192], F32, s4w)
        wo4 = sb("wo4", [P, H4, D], F32, s4w)
        s4w.close()
        s3.close()
        s4 = ExitStack()
        wvo = sb("wvo", [P, H4 // 2, D], F32, s4)
        s4p = ExitStack()
        wqbT = sb("wqbT", [64, H4, QL], F32, s4p)
        wkT = sb("wkT", [64, H4, 64], F32, s4p)
        wvT = sb("wvT", [P, H4, 64], F32, s4p)
        s4p.close()
        ql0 = sb("ql0", [P, 2, P], F32, s4)
        ql1 = sb("ql1", [64, 2, P], F32, s4)
        kvT = sb("kvT", [P, 2, P], F32, s4)
        kvr = sb("kvr", [P, 2, P], F32, s4)
        kT = sb("kT", [P, 2, P], F32, s4)
        rk = sb("rk", [P, 2, 64], F32, s4)
        rq = sb("rq", [P, 2, 2, 4, 64], F32, s4)
        qs = sb("qs", [P, 2, H4, P], F32, s4)
        qT = sb("qT", [P, 2, H4, P], F32, s4)
        sm = sb("sm", [P, 2, H4, P], F32, s4)
        nm = sb("nm", [P, 2, H4], F32, s4)
        rsum = sb("rsum", [P, 2, H4], F32, s4)
        rinv = sb("rinv", [P, 2, H4], F32, s4)
        pT = sb("pT", [P, 2, H4, P], F32, s4)
        oT = sb("oT", [P, 2, H4 // 2, P], F32, s4)
        s4.close()

        s56, s5 = ExitStack(), ExitStack()
        xi = sb("xi", [P, NT, D], BF16, s56)
        xiT = sb("xiT", [P, DC, NT, P], BF16, s56)
        fw = sb("fw", [P, 3, 2048], F32, s56)
        fi = sb("fi", [P, 3, 2048], BF16, s56)
        ew = sb("ew", [P, 2, DC, D], F32, s5)
        ewkv = sb("ewkv", [P, 4, D], F32, s5)
        bq5 = sb("bq5", [P, D], F32, s5)
        bp5 = sb("bp5", [P, D], F32, s5)
        bv5 = sb("bv5", [P, D], F32, s5)
        bk5 = sb("bk5", [P, DC], F32, s5)
        eqf = sb("eqf", [P, 4, D], F32, s5)
        eqi = sb("eqi", [P, 4, D], BF16, s5)
        esc = sb("esc", [P, 3, 4], F32, s5)
        ediag = sb("ediag", [P, 4, P], F32, s5)
        ewb = sb("ewb", [P, 2, D], F32, s5)
        ewT = sb("ewT", [P, 2, DC, D], BF16, s5)
        wkvT = sb("wkvT", [P, DC, 512], F32, s5)
        k5T = sb("k5T", [P, DC, NT, P], F32, s5)
        v5 = sb("v5", [P, NT, D], F32, s5)
        q5, q5T = xn, xnT
        q5s = sb("q5s", [P, 2, DC, P], F32, s5)
        kx = sb("kx", [P, 2, DC, 8, P], F32, s5)
        s5m = sb("s5m", [P, 2, H4, P], F32, s5)
        n5 = sb("n5", [P, 2, H4], F32, s5)
        r5 = sb("r5", [P, 2, H4], F32, s5)
        i5 = sb("i5", [P, 2, H4], F32, s5)
        p5T = sb("p5T", [P, 2, H4, P], F32, s5)
        o5 = sb("o5", [P, 2, D], F32, s5)
        oq = sb("oq", [P, 2, D], F32, s5)
        oi = sb("oi", [P, 2, D], BF16, s5)
        osc = sb("osc", [P, 2, 3], F32, s5)
        oiT = sb("oiT", [P, 2, DC, P], BF16, s5)
        ot = sb("ot", [P, 2, D], F32, s5)
        s5.close()
        s6 = ExitStack()
        fguT = sb("fguT", [P, DC, 2, 1024], BF16, s6)
        fdT = sb("fdT", [P, 8, D], BF16, s6)
        fg = sb("fg", [P, 2, 1024], F32, s6)
        fh = sb("fh", [P, 2, 1024], F32, s6)
        fq = sb("fq", [P, 2, 1024], F32, s6)
        fhi = sb("fhi", [P, 2, 1024], BF16, s6)
        fhT = sb("fhT", [P, 2, 8, P], BF16, s6)
        s6.close()
        s56.close()

        W1 = slice(0, 1024)
        W2 = slice(1024, 3072)
        W3 = slice(3072, 4096)
        CREDIT = 4
        XCREDIT = 8

        def x_done(eng, s, t):
            if s == 0:
                eng.wait_ge(sem("x_loaded"), 16)
            elif s == 1:
                eng.wait_ge(sem("x1_added"), t + 1)
            elif s == 2:
                eng.wait_ge(sem("x2_added"), t // 2 + 1)
            elif s == 3:
                eng.wait_ge(sem("expert_added"), XCREDIT + 8 * NT)
            else:
                eng.wait_ge(sem(f"x{s}_added"), t + 2)

        def prep4_moves():
            for k in range(2):
                yield wkT[:, 8 * k:8 * k + 8, :].rearrange("p h n -> p (h n)"), bank[k][0:64, :]
            for k in range(2):
                yield wvT[:, 8 * k:8 * k + 8, :].rearrange("p h n -> p (h n)"), bank[2 + k][:]
            for k in range(4):
                yield wqbT[:, 4 * k:4 * k + 4, 0:P], bank[4 + k][0:64, :].rearrange("p (h n) -> p h n", h=4)
            for k in range(2):
                yield wqbT[:, 8 * k:8 * k + 8, P:QL], bank[k][0:64, :].rearrange("p (h n) -> p h n", h=8)
            for k in range(2):
                yield wqb[:, 0, 8 * k:8 * k + 8, 0:64], bank[2 + k][:].rearrange("p (h n) -> p h n", h=8)
            for k in range(2):
                yield wqb[0:64, 1, 8 * k:8 * k + 8, 0:64], bank[4 + k][0:64, :].rearrange("p (h n) -> p h n", h=8)
            for k in range(4):
                yield wvo[:, 2 * k:2 * k + 2, :].rearrange("p j n -> p (j n)"), bank[(6, 7, 0, 1)[k]][:]

        block = ctx.enter_context(nc.Block())

        @block.sync
        def _(sp):
            sp.dma_start(x[:], a["x"].rearrange("b s d -> s b d")).then_inc(sem("x_loaded"), 16)
            sp.dma_start(const[:], a["consts"]).then_inc(sem("const_loaded"), 16)
            for dst, name in ((wq, "L0_attn_W_q"), (wkv, "L0_attn_W_kv"), (wo, "L0_attn_W_o")):
                sp.dma_start(dst[:], a[name].rearrange("(c p) n -> p c n", p=P)).then_inc(sem("w1_loaded"), 16)
            sp.dma_start(cx[:], a["ctx_2048"].rearrange("b s d -> s b d")).then_inc(sem("s2_loaded"), 16)
            for h in range(HG):
                pad = a["kpad"]
                src = bass.AP(tensor=pad.tensor, offset=pad.offset + h * (P + D) + 1, ap=[[1, P], [1, D]])
                sp.dma_start(tapR[:, h, :], src).then_inc(sem("s2_loaded"), 16)
            with nc.allow_non_contiguous_dma(reason="one value per partition"):
                sp.dma_start(skip[:], a["fside_S2_0"].rearrange("(p o) -> p o", o=1)).then_inc(sem("s2_loaded"), 16)
            sp.dma_start(wg[:], a["L0_ffn_Wg"].rearrange("(c p) e -> p c e", p=P)).then_inc(sem("gate_loaded"), 16)
            sp.dma_start(bg[:], a["L0_ffn_bg"].partition_broadcast(P)).then_inc(sem("gate_loaded"), 16)
            sp.dma_start(b3[:], a["L0_ffn_b3"]).then_inc(sem("gate_loaded"), 16)
            for i, name in enumerate(("L0_ffn_b1", "L0_ffn_b2")):
                sp.dma_start(b12[32 * i:32 * i + 32, :], a[name].rearrange("e (c p) -> (e c) p", p=P)).then_inc(sem("gate_loaded"), 16)
            x_done(sp, 2, NT - 1)
            sp.dma_start(wqa[:], a["L1_attn_Wqa"].rearrange("(c p) n -> p c n", p=P)).then_inc(sem("w4_loaded"), 16)
            sp.dma_start(wkva[:], a["L1_attn_Wkva"].rearrange("(c p) n -> p c n", p=P)).then_inc(sem("w4_loaded"), 16)
            sp.dma_start(wqb[:, 0].rearrange("p h n -> p (h n)"), a["L1_attn_Wqb"][0:P, :]).then_inc(sem("w4_loaded"), 16)
            sp.dma_start(wqb[0:64, 1].rearrange("p h n -> p (h n)"), a["L1_attn_Wqb"][P:QL, :]).then_inc(sem("w4_loaded"), 16)
            sp.dma_start(wkvb[:].rearrange("p h n -> p (h n)"), a["L1_attn_Wkvb"]).then_inc(sem("w4_loaded"), 16)
            sp.dma_start(wo4[:], a["L1_attn_Wo"].rearrange("(h v) n -> v h n", v=P)).then_inc(sem("w4_loaded"), 16)
            x_done(sp, 1, NT - 1)
            with sp.Fori(0, NE // 2) as i:
                for u in range(2):
                    e = i * 2 + u
                    sp.wait_ge(sem("w_split"), i * 2 + (u + 1))
                    for rows, where, name in ((DC, W1, "L0_ffn_W1"), (FC, W2, "L0_ffn_W2"), (FC, W3, "L0_ffn_W3")):
                        sp.dma_start(wraw[:, where].rearrange("p (c n) -> p c n", c=rows),
                                     a[name][bass.ds(e, 1)].rearrange("e (c p) n -> p (e c) n", p=P)).then_inc(sem("w_loaded"), 16)
            x_done(sp, 4, NT - 1)
            for i, name in enumerate(("L1_xattn_wq", "L1_xattn_wp")):
                sp.dma_start(ew[:, i], a[name].rearrange("(c p) n -> p c n", p=P)).then_inc(sem("w5_loaded"), 16)
            sp.dma_start(ewkv[:], a["L1_xattn_wkv"].rearrange("(c p) n -> p c n", p=P)).then_inc(sem("w5_loaded"), 16)
            sp.dma_start(bq5[:], a["L1_xattn_bq"].partition_broadcast(P)).then_inc(sem("w5_loaded"), 16)
            sp.dma_start(bp5[:], a["L1_xattn_bp"].partition_broadcast(P)).then_inc(sem("w5_loaded"), 16)
            sp.dma_start(bv5[:], a["L1_xattn_bkv"][D:2 * D].partition_broadcast(P)).then_inc(sem("w5_loaded"), 16)
            with nc.allow_non_contiguous_dma(reason="one value per partition"):
                sp.dma_start(bk5[:], a["L1_xattn_bkv"][0:D].rearrange("(c p) -> p c", p=P)).then_inc(sem("w5_loaded"), 16)
            for i, (name, c) in enumerate((("L1_ffn_w_gate", 8), ("L1_ffn_w_up", 8), ("L1_ffn_w_down", 2))):
                sp.dma_start(fw[:, i, :].rearrange("p (c n) -> p c n", c=c), a[name].rearrange("(c p) n -> p c n", p=P)).then_inc(sem("w6_loaded"), 16)
            if LAST_STAGE < 6:
                x_done(sp, LAST_STAGE, NT - 1)
                sp.dma_start(out.rearrange("b s d -> s b d"), x[:]).then_inc(sem("stored"), 16)
                sp.wait_ge(sem("stored"), 16)
            else:
                with sp.Fori(0, NT) as t:
                    sp.wait_ge(sem("x6_added"), t + 2)
                    sp.dma_start(out[bass.ds(t, 1)].rearrange("b s d -> s (b d)"), x[:, bass.ds(t, 1), :].rearrange("p t d -> p (t d)")).then_inc(sem("stored"), 16)
                sp.wait_ge(sem("stored"), 16 * NT)

        @block.gpsimd
        def _(pool):
            pool.sem_inc(sem("w_split"), 1)
            pool.wait_ge(sem("xnT_act"), 4)
            pool.wait_ge(sem("xnT_dve"), 4)
            pool.wait_ge(sem("cxT_act"), 2)
            pool.wait_ge(sem("cxT_dve"), 2)
            for h in range(HG):
                if h >= 2:
                    pool.wait_ge(sem("conv_psum"), 2 * (h - 1))
                for c in range(DC):
                    g = slice(CH * h, CH * h + CH)
                    nc.gpsimd.tensor_tensor(
                        kvp[:, h % 2, c, :].rearrange("p (b i j) -> p b i j", b=NT, i=CH),
                        xnT[:, c, :, g].unsqueeze(3).to_broadcast([P, NT, CH, CH]),
                        cxT[:, c, :, g].unsqueeze(2).to_broadcast([P, NT, CH, CH]),
                        ALU.mult).then_inc(sem("kvp_ready"), 1)
            with pool.Fori(0, NE // 2) as i:
                for u in range(2):
                    pool.wait_ge(sem("w_loaded"), i * 96 + (48 * u + 48))
                    pool.wait_ge(sem("expert_done"), i * 2 + u + 1)
                    pool.sem_inc(sem("slot_claimed"), 1)
                    nc.gpsimd.tensor_copy(whi[:, u, :], wraw[:]).then_inc(sem("w_hi"), 1)
                    pool.wait_ge(sem("w_hi"), i * 2 + u + 1)
                    nc.gpsimd.tensor_tensor(wlo[:, u, :], wraw[:], whi[:, u, :], ALU.subtract).then_inc(sem("w_split"), 1)
            own = [0]
            chain = sem("pool_own")

            def rope_q(i, u, g):
                v = qs[:, u, 4 * g:4 * g + 4, 64:128]
                pairs = v.rearrange("p h (f two) -> p h f two", two=2)
                cosb = cst["cos"].unsqueeze(1).to_broadcast([P, 4, 64])
                sinb = cst["sin"].rearrange("p (f two) -> p f two", two=2).unsqueeze(1).to_broadcast([P, 4, 32, 2])
                turned = rq[:, g % 2, 1].rearrange("p h (f two) -> p h f two", two=2)
                pool.wait_ge(sem("q4_copied"), i * 8 + (4 * u + g + 3))
                pool.sem_inc(sem("slot_claimed"), 1)
                nc.gpsimd.tensor_tensor(rq[:, g % 2, 0], v, cosb, ALU.mult).then_inc(chain, 1)
                for two in range(2):
                    nc.gpsimd.tensor_tensor(turned[:, :, :, two], pairs[:, :, :, 1 - two], sinb[:, :, :, two], ALU.mult).then_inc(chain, 1)
                pool.wait_ge(chain, i * 24 + (3 * (4 * u + g) + 3))
                nc.gpsimd.tensor_tensor(v, rq[:, g % 2, 0], rq[:, g % 2, 1], ALU.add).then_inc(sem("roped"), 1)

            with pool.Fori(0, NT // 2) as i:
                for u in range(2):
                    for g in range(4):
                        rope_q(i, u, g)
                for u in range(2):
                    for g in range(4):
                        hs = slice(4 * g, 4 * g + 4)
                        pool.wait_ge(sem("r4_ready"), i * 8 + (4 * u + g + 1))
                        nc.gpsimd.tensor_tensor(sm[:, u, hs, :], sm[:, u, hs, :],
                                                rinv[:, u, hs].unsqueeze(2).to_broadcast([P, 4, P]), ALU.mult).then_inc(sem("p4_ready"), 1)
            pool.wait_ge(sem("prep5_ready"), 6)

            def spread_keys(i, u):
                for c in range(DC):
                    pool.wait_ge(sem("s5_psum"), i * 8 + (4 * u + 4))
                    nc.gpsimd.tensor_tensor(kx[:, u, c], k5T[:, c, bass.ds(i * 2 + u, 1), :].to_broadcast([P, 8, P]),
                                            cst["head16"].unsqueeze(2).to_broadcast([P, 8, P]), ALU.mult).then_inc(sem("kx_ready"), 1)

            with pool.Fori(0, NT // 2) as i:
                for u in range(2):
                    spread_keys(i, u)
            pool.wait_ge(sem("w6_scale"), 1)
            for k in range(3):
                nc.gpsimd.tensor_scalar(fw[:, k, :], fw[:, k, :], fws[:, 3, k:k + 1], ROUND, ALU.mult, ALU.add).then_inc(sem("w6_step"), 1)
            for k in range(3):
                pool.wait_ge(sem("w6_step"), k + 1)
                nc.gpsimd.tensor_scalar(fw[:, k, :], fw[:, k, :], -ROUND, 1.0, ALU.add, ALU.min).then_inc(sem("w6_step"), 1)
            for k in range(3):
                pool.wait_ge(sem("w6_step"), k + 4)
                nc.gpsimd.tensor_scalar(fi[:, k, :], fw[:, k, :], -1.0, None, ALU.max).then_inc(sem("w6_int"), 1)


        @block.scalar
        def _(act):
            def deviation(s):
                act.wait_ge(sem("ln_var"), s)
                nc.scalar.activation(sd[:], ve[:], ACT.Sqrt).then_inc(sem("ln_sd"), 1)

            def xnT_copies(s):
                for half in range(2):
                    act.wait_ge(sem("xnT_psum"), 4 * (s - 1) + 2 * half + 1)
                    nc.scalar.copy(xnT[:, 0, 4 * half:4 * half + 4, :].rearrange("p t s -> p (t s)"), bank[2 * half][:]).then_inc(sem("xnT_act"), 1)

            act.wait_ge(sem("prep1_psum"), 1)
            nc.scalar.copy(woT[:].rearrange("p c n -> p (c n)"), bank[4][:]).then_inc(sem("prep1_ready"), 1)
            for c in range(DC):
                act.wait_ge(sem("prep1_psum"), c + 2)
                nc.scalar.copy(toF[:, c, :], bank[5 + c][:]).then_inc(sem("prep1_ready"), 1)
            act.wait_ge(sem("prep1_psum"), 4)
            nc.scalar.copy(toO[:, 0:2, :].rearrange("p c n -> p (c n)"), bank[7][:]).then_inc(sem("prep1_ready"), 1)
            act.wait_ge(sem("prep1_psum"), 5)
            nc.scalar.copy(toO[:, 2, :], bank[4][:, 0:D]).then_inc(sem("prep1_ready"), 1)
            deviation(1)
            xnT_copies(1)
            for t in range(NT):
                act.wait_ge(sem("qk_psum"), t + 1)
                if t >= 2:
                    act.wait_ge(sem("ss_done"), t - 1)
                nc.scalar.activation(sq[:, t % 2, :], bank[t % 4][:], ACT.Square).then_inc(sem("sq_ready"), 1)
                nc.scalar.copy(qk[:, t, :], bank[t % 4][:]).then_inc(sem("qk_ready"), 1)
            act.wait_ge(sem("ss_done"), NT)
            nc.scalar.activation(sn[:], ss[:], ACT.Sqrt).then_inc(sem("norm_ready"), 1)
            for t in range(NT):
                act.wait_ge(sem("kq_psum"), t + 1)
                nc.scalar.copy(kqT[:, t, :], bank[4 + t % 4][:]).then_inc(sem("kqT_ready"), 1)
            for k in range(8):
                act.wait_ge(sem("tap_psum"), k + 1)
                nc.scalar.copy(tap[:, 2 * k:2 * k + 2, :].rearrange("p h n -> p (h n)"), bank[4 + k % 2][:]).then_inc(sem("tap_ready"), 1)
            for half in range(2):
                act.wait_ge(sem("cxT_psum"), 2 * half + 1)
                nc.scalar.copy(cxT[:, 0, 4 * half:4 * half + 4, :].rearrange("p t s -> p (t s)"), bank[6][:]).then_inc(sem("cxT_act"), 1)
            deviation(2)
            xnT_copies(2)
            act.wait_ge(sem("bT_psum"), 1)
            nc.scalar.copy(bT[:], bank[4][:, 0:64]).then_inc(sem("bT_ready"), 1)
            deviation(3)
            xnT_copies(3)
            act.wait_ge(sem("xnT_dve"), 6)
            act.wait_ge(sem("xnT_act"), 6)
            nc.scalar.copy(xh[:].rearrange("p c n -> p (c n)"), xnT[:].rearrange("p c t s -> p (c t s)")).then_inc(sem("xh_ready"), 1)
            act.wait_ge(sem("gate_shifted"), 1)
            nc.scalar.activation(gw[:].rearrange("p t e -> p (t e)"), lg[:].rearrange("p t e -> p (t e)"), ACT.Exp).then_inc(sem("gate_exp"), 1)
            for k in range(2):
                act.wait_ge(sem("combT_psum"), k + 1)
                nc.scalar.copy(combT[:, 4 * k:4 * k + 4, :].rearrange("p t s -> p (t s)"), bank[5 + k][0:NE, :]).then_inc(sem("combT_ready"), 1)
            act.sem_inc(sem("h2_f32"), CREDIT)
            with act.Fori(0, NE // 2) as i:
                for u in range(2):
                    for layer in (1, 2):
                        nc.scalar.copy(be[:, layer - 1, u, :], bT[:, bass.ds(i * 8 + (32 * (layer - 1) + 4 * u), FC)]).then_inc(sem("bias_ready"), 1)
                    act.wait_ge(sem("bias_ready"), i * 4 + (2 * u + 2))
                    for half in range(2):
                        n4 = i * 16 + (8 * u + 4 * half)
                        for layer, h in ((1, h1), (2, h2)):
                            for f in range(FC):
                                bias = be[:, layer - 1, u, f:f + 1]
                                act.wait_ge(sem(f"l{layer}_psum"), n4 + (f + 1))
                                nc.scalar.activation(h[:, half, 0, f, :], bank[f][:], ACT.Gelu, bias=bias).then_inc(sem(f"h{layer}_hi"), 1)
                                act.wait_ge(sem("h2_lo" if layer == 1 else "h1_lo"), n4 + (f + 1))
                                nc.scalar.activation(hf[:, f, :], bank[f][:], ACT.Gelu, bias=bias).then_inc(sem(f"h{layer}_f32"), 1)
            def prep(k, dst, src):
                act.wait_ge(sem("prep4_psum"), k + 1)
                nc.scalar.copy(dst, src).then_inc(sem("prep4_act"), 1)

            for k, (dst, src) in enumerate(prep4_moves()):
                if k % 2 == 0:
                    prep(k, dst, src)
            deviation(4)
            xnT_copies(4)
            act.sem_inc(sem("q4_copied"), 2)
            act.sem_inc(sem("oT_ready"), 1)

            def latents(i, u):
                act.wait_ge(sem("lat_psum"), i * 2 + (u + 1))
                nc.scalar.copy(ql0[:, u, :], bank[0][:, 0:P])
                nc.scalar.copy(kvT[:, u, :], bank[0][:, P:2 * P])
                nc.scalar.copy(ql1[:, u, :], bank[0][0:64, 2 * P:3 * P]).then_inc(sem("lat_copied"), 1)

            def exps(i, u, g):
                act.wait_ge(sem("nm_ready"), i * 8 + (4 * u + g + 1))
                for h in range(4 * g, 4 * g + 4):
                    last = nc.scalar.activation(sm[:, u, h, :], sm[:, u, h, :], ACT.Exp, bias=nm[:, u, h:h + 1], accum_out=rsum[:, u, h:h + 1])
                last.then_inc(sem("exp_ready"), 1)

            with act.Fori(0, NT // 2) as i:
                for u in range(2):
                    latents(i, u)
                    for g in range(4):
                        act.wait_ge(sem("q4_psum"), i * 8 + (4 * u + g + 1))
                        nc.scalar.copy(qs[:, u, 4 * g:4 * g + 4, :].rearrange("p h n -> p (h n)"), bank[1 + g % 2][:]).then_inc(sem("q4_copied"), 1)
                    act.wait_ge(sem("kT_psum"), i * 2 + (u + 1))
                    nc.scalar.copy(kT[:, u, :], bank[0][:, 3 * P:4 * P]).then_inc(sem("kT_ready"), 1)
                steps = [(u, g) for u in range(2) for g in range(4)]
                for j, (u, g) in enumerate(steps):
                    act.wait_ge(sem("t4_psum"), i * 8 + (j + 1))
                    nc.scalar.copy(qT[:, u, 4 * g:4 * g + 4, :].rearrange("p h n -> p (h n)"), bank[3 + g % 2][:]).then_inc(sem("qT_ready"), 1)
                    if j >= 2:
                        exps(i, *steps[j - 2])
                exps(i, *steps[6])
                exps(i, *steps[7])
                for u in range(2):
                    for k in range(2):
                        act.wait_ge(sem("pv_psum"), i * 4 + (2 * u + k + 1))
                        nc.scalar.copy(oT[:, u, 4 * k:4 * k + 4, :].rearrange("p h n -> p (h n)"), bank[7 if k == 0 else 0][:]).then_inc(sem("oT_ready"), 1)
            act.wait_ge(sem("const_loaded"), 16)
            nc.scalar.copy(identb[:], cst["ident"]).then_inc(sem("identb_ready"), 1)
            deviation(5)
            for k in range(2):
                act.wait_ge(sem("prep5_psum"), k + 1)
                nc.scalar.copy(wkvT[:, k, :], bank[k][:]).then_inc(sem("prep5_ready"), 1)
            act.wait_ge(sem("w5_loaded"), 112)
            for k in range(4):
                act.wait_ge(sem("prep5_psum"), k + 3)
                nc.scalar.activation(k5T[:, k // 2, 4 * (k % 2):4 * (k % 2) + 4, :].rearrange("p t s -> p (t s)"), bank[2 + k][:], ACT.Identity,
                                     bias=bk5[:, k // 2:k // 2 + 1]).then_inc(sem("prep5_ready"), 1)
            act.wait_ge(sem("prep5_psum"), 7)
            nc.scalar.copy(ewT[:].rearrange("p w c n -> p (w c n)"), bank[6][:].bitcast(BF16)).then_inc(sem("prep5_ready"), 1)
            act.wait_ge(sem("prep5_psum"), 8)
            nc.scalar.copy(ewb[:].rearrange("p w n -> p (w n)"), bank[7][:]).then_inc(sem("prep5_ready"), 1)

            def xiT_copies(s):
                for c in range(DC):
                    act.wait_ge(sem("xiT_psum"), 2 * (s - 5) + c + 1)
                    nc.scalar.copy(xiT[:, c].rearrange("p t s -> p (t s)"), bank[c][:].bitcast(BF16)).then_inc(sem("xiT_ready"), 1)

            xiT_copies(5)
            for k in range(4):
                act.wait_ge(sem("q5T_psum"), k + 1)
                nc.scalar.copy(q5T[:, k % 2, 4 * (k // 2):4 * (k // 2) + 4, :].rearrange("p t s -> p (t s)"), bank[k][:]).then_inc(sem("q5T_ready"), 1)
            act.sem_inc(sem("exp5_ready"), 2)
            with act.Fori(0, NT // 2) as i:
                for u in range(2):
                    for g in range(4):
                        act.wait_ge(sem("n5_ready"), i * 8 + (4 * u + g + 1))
                        for k in range(4):
                            h = 4 * g + k
                            last = nc.scalar.activation(s5m[:, u, h, :], bank[5 + g % 2][:, P * k:P * k + P], ACT.Exp,
                                                        bias=n5[:, u, h:h + 1], accum_out=r5[:, u, h:h + 1])
                        last.then_inc(sem("exp5_ready"), 1)
                for u in range(2):
                    act.wait_ge(sem("oiT_psum"), i * 2 + (u + 1))
                    nc.scalar.copy(oiT[:, u].rearrange("p c s -> p (c s)"), bank[1][:, 0:P].bitcast(BF16)).then_inc(sem("oiT_ready"), 1)
            deviation(6)
            xiT_copies(6)
            for k in range(6):
                act.wait_ge(sem("w6T_psum"), k + 1)
                b16 = bank[2 + k][:].bitcast(BF16)
                if k < 4:
                    nc.scalar.copy(fguT[:, k % 2, k // 2, :], b16).then_inc(sem("w6T_ready"), 1)
                else:
                    nc.scalar.copy(fdT[:, 4 * (k - 4):4 * (k - 4) + 4, :].rearrange("p c n -> p (c n)"), b16).then_inc(sem("w6T_ready"), 1)
            act.sem_inc(sem("silu_ready"), 2)
            with act.Fori(0, NT // 2) as i:
                for u in range(2):
                    for k in range(2):
                        act.wait_ge(sem("gu_psum"), i * 2 + (u + 1))
                        nc.scalar.activation(fg[:, u, 512 * k:512 * k + 512], bank[4 * u + k][:], ACT.Silu, scale=fsn[:, u, 0:1]).then_inc(sem("silu_ready"), 1)
                for u in range(2):
                    act.wait_ge(sem("fhT_psum"), i * 2 + (u + 1))
                    nc.scalar.copy(fhT[:, u].rearrange("p c s -> p (c s)"), bank[4 * u][:].bitcast(BF16)).then_inc(sem("fhT_ready"), 1)

        @block.vector
        def _(dve):
            own = [0]

            def then(ins):
                own[0] += 1
                ins.then_inc(sem("dve_own"), 1)
                dve.wait_ge(sem("dve_own"), own[0])

            def rsqrt_refined(v, root, r, tmp):
                then(nc.vector.reciprocal(r[:, 0], root))
                then(nc.vector.tensor_tensor(tmp[:, 0], r[:, 0], r[:, 0], ALU.mult))
                then(nc.vector.tensor_tensor(tmp[:, 1], tmp[:, 0], v, ALU.mult))
                then(nc.vector.tensor_scalar(tmp[:, 0], tmp[:, 1], -0.5, 1.5, ALU.mult, ALU.add))
                then(nc.vector.tensor_tensor(r[:, 1], r[:, 0], tmp[:, 0], ALU.mult))

            def layernorm(s):
                for t in range(NT):
                    x_done(dve, s - 1, t)
                    nc.vector.bn_stats(st[:, t, :], x[:, t, :]).then_inc(sem("ln_stats"), 1)
                for t in range(NT):
                    dve.wait_ge(sem("ln_stats"), NT * (s - 1) + t + 1)
                    nc.vector.bn_aggr(mv[:, t, :], st[:, t, :]).then_inc(sem("ln_mean"), 1)
                dve.wait_ge(sem("ln_mean"), NT * s)
                nc.vector.tensor_scalar(ve[:], mv[:, :, 1], EPS, None, ALU.add).then_inc(sem("ln_var"), 1)
                dve.wait_ge(sem("ln_sd"), s)
                r2 = rs[:].rearrange("p t k -> p k t")
                rsqrt_refined(ve[:], sd[:], r2, nw)
                for t in range(NT):
                    nc.vector.tensor_scalar(xn[:, t, :], x[:, t, :], mv[:, t, 0:1], rs[:, t, 1:2], ALU.subtract, ALU.mult).then_inc(sem("xn_ready"), 1)

            def xnT_copies(s):
                for half in range(2):
                    dve.wait_ge(sem("xnT_psum"), 4 * (s - 1) + 2 * half + 2)
                    nc.vector.tensor_copy(xnT[:, 1, 4 * half:4 * half + 4, :].rearrange("p t s -> p (t s)"), bank[2 * half + 1][:]).then_inc(sem("xnT_dve"), 1)

            layernorm(1)
            xnT_copies(1)
            for t in range(NT):
                dve.wait_ge(sem("sq_ready"), t + 1)
                nc.vector.tensor_reduce(ss[:, 32 * t:32 * t + 32],
                                        sq[:, t % 2, :].rearrange("p (w a h k) -> p w h a k", w=2, a=2, k=8),
                                        AX.XY, ALU.add).then_inc(sem("ss_done"), 1)
            dve.wait_ge(sem("norm_ready"), 1)
            rsqrt_refined(ss[:], sn[:], rn, nn)
            for t in range(NT):
                dve.wait_ge(sem("qk_ready"), t + 1)
                for w in range(2):
                    v = qk[:, t, D * w:D * w + D].rearrange("p (a h k) -> p a h k", a=2, k=8)
                    r = rn[:, 1, 32 * t + 16 * w:32 * t + 16 * w + 16].unsqueeze(1).unsqueeze(3).to_broadcast([P, 2, 16, 8])
                    nc.vector.tensor_tensor(v, v, r, ALU.mult).then_inc(sem("qkn_ready"), 1)

            def add_attention(t):
                dve.wait_ge(sem("attn_psum"), t + 1)
                nc.vector.tensor_tensor(x[:, t, :], x[:, t, :], bank[t % 4][:, 0:D], ALU.add).then_inc(sem("x1_added"), 1)

            for t in range(NT):
                dve.wait_ge(sem("kqT_ready"), t + 1)
                nc.vector.tensor_tensor(pr[:, t, 0:2, :].rearrange("p a s -> p (a s)"), kqT[:, t, 0:256], kqT[:, t, 256:512], ALU.mult)
                nc.vector.tensor_tensor(pr[:, t, 2, :], kqT[:, t, 0:128], kqT[:, t, 384:512], ALU.mult)
                nc.vector.tensor_tensor(pr[:, t, 3, :], kqT[:, t, 128:256], kqT[:, t, 256:384], ALU.mult).then_inc(sem("products_ready"), 1)
                if t >= 1:
                    add_attention(t - 1)
            add_attention(NT - 1)
            for half in range(2):
                dve.wait_ge(sem("cxT_psum"), 2 * half + 2)
                nc.vector.tensor_copy(cxT[:, 1, 4 * half:4 * half + 4, :].rearrange("p t s -> p (t s)"), bank[7][:]).then_inc(sem("cxT_dve"), 1)
            layernorm(2)
            dve.wait_ge(sem("s2_loaded"), 16 * (HG + 2))
            for k in range(4):
                two = slice(2 * k, 2 * k + 2)
                dve.wait_ge(sem("xn_ready"), NT + 2 * k + 2)
                nc.vector.scalar_tensor_tensor(wsk[:, two, :], xn[:, two, :], skip[:, 0:1], cx[:, two, :],
                                               ALU.mult, ALU.mult).then_inc(sem("wsk_ready"), 1)
            xnT_copies(2)
            for k in range(4):
                two = slice(2 * k, 2 * k + 2)
                dve.wait_ge(sem("skip_psum"), k + 1)
                then(nc.vector.tensor_tensor(sk2[:, k % 2, :], bank[4 + k][:], cx[:, two, :].rearrange("p t d -> p (t d)"), ALU.mult))
                xt = x[:, two, :].rearrange("p t d -> p (t d)")
                nc.vector.tensor_tensor(xt, xt, sk2[:, k % 2, :], ALU.add).then_inc(sem("skip_added"), 1)
            for h in range(HG):
                g = slice(CH * h, CH * h + CH)
                for lc in range(DC):
                    dve.wait_ge(sem("conv_psum"), 2 * h + lc + 1)
                    b = 2 * (h % 2) + lc
                    if h >= 1:
                        dve.wait_ge(sem("yT_ready"), 2 * (h - 1) + lc + 1)
                    nc.vector.tensor_tensor(yx[:, lc, :].rearrange("p (b j i) -> p b j i", b=NT, j=CH),
                                            bank[b][:].rearrange("p (b i j) -> p b j i", b=NT, i=CH),
                                            cxT[:, lc, :, g].unsqueeze(2).to_broadcast([P, NT, CH, CH]),
                                            ALU.mult).then_inc(sem("yx_ready"), 1)
                for lc in range(DC):
                    dve.wait_ge(sem("yx_ready"), 2 * h + lc + 1)
                    nc.vector.tensor_reduce(yT[:, lc, :, g], yx[:, lc, :].rearrange("p (b j i) -> p b j i", b=NT, j=CH),
                                            AX.X, ALU.add).then_inc(sem("yT_ready"), 1)
            dve.wait_ge(sem("skip_added"), 4)
            for k in range(4):
                dve.wait_ge(sem("conv_out_psum"), k + 1)
                xt = x[:, 2 * k:2 * k + 2, :].rearrange("p t d -> p (t d)")
                nc.vector.tensor_tensor(xt, xt, bank[4 + k][:], ALU.add).then_inc(sem("x2_added"), 1)
            layernorm(3)
            xnT_copies(3)
            dve.wait_ge(sem("logits_psum"), 1)
            dve.wait_ge(sem("gate_loaded"), 80)
            bg8 = bg[:].unsqueeze(1).to_broadcast([P, NT, NE])
            then(nc.vector.tensor_tensor(lg[:], bank[7][:, 0:64].rearrange("p (t e) -> p t e", e=NE), bg8, ALU.add))
            then(nc.vector.tensor_reduce(gm[:], lg[:], AX.X, ALU.max))
            nc.vector.tensor_tensor(lg[:], lg[:], gm[:].unsqueeze(2).to_broadcast([P, NT, NE]), ALU.subtract).then_inc(sem("gate_shifted"), 1)
            dve.wait_ge(sem("xh_ready"), 1)
            nc.vector.tensor_tensor(xl[:].rearrange("p c n -> p (c n)"), xnT[:].rearrange("p c t s -> p (c t s)"),
                                    xh[:].rearrange("p c n -> p (c n)"), ALU.subtract).then_inc(sem("xl_ready"), 1)
            dve.wait_ge(sem("gate_exp"), 1)
            then(nc.vector.tensor_reduce(gs[:, 0, :], gw[:], AX.X, ALU.add))
            then(nc.vector.reciprocal(gs[:, 1, :], gs[:, 0, :]))
            then(nc.vector.tensor_tensor(gw[:], gw[:], gs[:, 1, :].unsqueeze(2).to_broadcast([P, NT, NE]), ALU.mult))
            for t in range(NT):
                then(nc.vector.max(top[:, t, :], gw[:, t, :]))
            for t in range(NT):
                then(nc.vector.max_index(topi[:, t, :], top[:, t, :], gw[:, t, :]))
            then(nc.vector.tensor_copy(topf[:], topi[:]))
            iota = cst["iota8"].unsqueeze(1).to_broadcast([P, NT, NE])
            for r in range(2):
                then(nc.vector.tensor_tensor(pick[:, r], iota, topf[:, :, r:r + 1].to_broadcast([P, NT, NE]), ALU.is_equal))
                then(nc.vector.tensor_tensor(pick[:, r], pick[:, r], top[:, :, r:r + 1].to_broadcast([P, NT, NE]), ALU.mult))
            nc.vector.tensor_tensor(comb[:], pick[:, 0], pick[:, 1], ALU.add).then_inc(sem("comb_ready"), 1)
            for k in range(4):
                dve.wait_ge(sem("b3_psum"), k + 1)
                xt = x[:, 2 * k:2 * k + 2, :].rearrange("p t d -> p (t d)")
                nc.vector.tensor_tensor(xt, xt, bank[k][:], ALU.add).then_inc(sem("b3_added"), 1)
            dve.wait_ge(sem("b3_added"), 4)
            dve.wait_ge(sem("comb_ready"), 1)
            dve.sem_inc(sem("h2_lo"), CREDIT)
            dve.sem_inc(sem("expert_added"), XCREDIT)
            with dve.Fori(0, NE // 2) as i:
                for u in range(2):
                    for half in range(2):
                        n4 = i * 16 + (8 * u + 4 * half)
                        for layer, h in ((1, h1), (2, h2)):
                            for f in range(FC):
                                dve.wait_ge(sem(f"h{layer}_f32"), n4 + (f + 1 + (CREDIT if layer == 2 else 0)))
                                nc.vector.tensor_tensor(h[:, half, 1, f, :], hf[:, f, :], h[:, half, 0, f, :],
                                                        ALU.subtract).then_inc(sem(f"h{layer}_lo"), 1)
                        for k in range(4):
                            t = 4 * half + k
                            dve.wait_ge(sem("l3_psum"), n4 + (k + 1))
                            dve.wait_ge(sem("expert_added"), n4 + (k + 1))
                            nc.vector.scalar_tensor_tensor(x[:, t, :], bank[4 + k][:, 0:D], comb[:, t, bass.ds(i * 2 + u, 1)], x[:, t, :],
                                                           ALU.mult, ALU.add).then_inc(sem("expert_added"), 1)
            def add_tile(i, u):
                dve.wait_ge(sem("out4_psum"), i * 2 + (u + 1))
                xt = x[:, bass.ds(i * 2 + u, 1), :].rearrange("p t d -> p (t d)")
                nc.vector.tensor_tensor(xt, xt, bank[7][:, 0:D], ALU.add).then_inc(sem("x4_added"), 1)

            def copy_p5T(i, j):
                u, g = j // 4, j % 4
                dve.wait_ge(sem("pt5_psum"), i * 8 + (j + 1))
                nc.vector.tensor_copy(p5T[:, u, 4 * g:4 * g + 4, :].rearrange("p h n -> p (h n)"), bank[3 + g % 2][:]).then_inc(sem("p5T_ready"), 1)

            def project(i, u):
                def step(n, ins):
                    ins.then_inc(sem("o5_step"), 1)
                    dve.wait_ge(sem("o5_step"), i * 14 + (7 * u + n))
                dve.wait_ge(sem("pv5_psum"), i * 2 + (u + 1))
                step(1, nc.vector.reciprocal(i5[:, u, :], r5[:, u, :]))
                step(2, nc.vector.tensor_tensor(o5[:, u, :].rearrange("p (h d) -> p h d", h=H4), bank[(7, 0)[u]][:, 0:D].rearrange("p (h d) -> p h d", h=H4),
                                                i5[:, u, :].unsqueeze(2).to_broadcast([P, H4, 16]), ALU.mult))
                step(3, nc.vector.tensor_reduce(osc[:, u, 0:1], o5[:, u, :], AX.X, ALU.max, apply_absolute_value=True))
                step(4, nc.vector.tensor_scalar(osc[:, u, 1:2], osc[:, u, 0:1], 1.0 / 127.0, 1e-8, ALU.mult, ALU.max))
                step(5, nc.vector.reciprocal(osc[:, u, 2:3], osc[:, u, 1:2]))
                step(6, nc.vector.tensor_scalar(oq[:, u, :], o5[:, u, :], osc[:, u, 2:3], ROUND, ALU.mult, ALU.add))
                step(7, nc.vector.tensor_scalar(oq[:, u, :], oq[:, u, :], -ROUND, 127.0, ALU.add, ALU.min))
                nc.vector.tensor_scalar(oi[:, u, :], oq[:, u, :], -127.0, None, ALU.max).then_inc(sem("oi_ready"), 1)

            for k, (dst, src) in enumerate(prep4_moves()):
                if k % 2:
                    dve.wait_ge(sem("prep4_psum"), k + 1)
                    nc.vector.tensor_copy(dst, src).then_inc(sem("prep4_dve"), 1)
            layernorm(4)
            xnT_copies(4)
            dve.sem_inc(sem("s4_masked"), 2)
            dve.sem_inc(sem("pT_ready"), 2)
            dve.sem_inc(sem("x4_added"), 1)

            def rope_k(i, u):
                kv = bank[0][:, 3 * P:4 * P]
                pe_ = kv[:, 64:128].rearrange("p (f two) -> p f two", two=2)
                sn_ = cst["sin"].rearrange("p (f two) -> p f two", two=2)
                turned = rk[:, 1].rearrange("p (f two) -> p f two", two=2)
                dve.wait_ge(sem("kvn_psum"), i * 2 + (u + 1))
                nc.vector.tensor_copy(kvr[:, u, 0:64], kv[:, 0:64]).then_inc(sem("rk_step"), 1)
                nc.vector.tensor_tensor(rk[:, 0], kv[:, 64:128], cst["cos"], ALU.mult).then_inc(sem("rk_step"), 1)
                for two in range(2):
                    nc.vector.tensor_tensor(turned[:, :, two], pe_[:, :, 1 - two], sn_[:, :, two], ALU.mult).then_inc(sem("rk_step"), 1)
                dve.wait_ge(sem("rk_step"), i * 8 + (4 * u + 4))
                nc.vector.tensor_tensor(kvr[:, u, 64:128], rk[:, 0], rk[:, 1], ALU.add).then_inc(sem("kvr_ready"), 1)

            causal = cst["causal"].unsqueeze(1).to_broadcast([P, 4, P])
            with dve.Fori(0, NT // 2) as i:
                for u in range(2):
                    rope_k(i, u)
                steps = [(u, g) for u in range(2) for g in range(4)]

                def invert(j):
                    u, g = steps[j]
                    dve.wait_ge(sem("exp_ready"), i * 8 + (j + 1))
                    nc.vector.reciprocal(rinv[:, u, 4 * g:4 * g + 4], rsum[:, u, 4 * g:4 * g + 4]).then_inc(sem("r4_ready"), 1)

                for j, (u, g) in enumerate(steps):
                    hs = slice(4 * g, 4 * g + 4)
                    dve.wait_ge(sem("s4_psum"), i * 8 + (j + 1))
                    nc.vector.scalar_tensor_tensor(sm[:, u, hs, :], bank[5 + g % 2][:].rearrange("p (h n) -> p h n", h=4), S4, causal,
                                                   ALU.mult, ALU.add).then_inc(sem("s4_masked"), 1)
                    dve.wait_ge(sem("s4_masked"), i * 8 + (j + 3))
                    nc.vector.tensor_reduce(nm[:, u, hs], sm[:, u, hs, :], AX.X, ALU.max, negate=True).then_inc(sem("nm_ready"), 1)
                    if j >= 2:
                        invert(j - 2)
                invert(6)
                invert(7)
                for u in range(2):
                    for g in range(4):
                        dve.wait_ge(sem("pt4_psum"), i * 8 + (4 * u + g + 1))
                        nc.vector.tensor_copy(pT[:, u, 4 * g:4 * g + 4, :].rearrange("p h n -> p (h n)"), bank[3 + g % 2][:]).then_inc(sem("pT_ready"), 1)
                    if u == 1:
                        add_tile(i, 0)
                add_tile(i, 1)
            def scales(dst_scale, dst_inverse, largest, floor):
                then(nc.vector.tensor_scalar(dst_scale, largest, 1.0 / 127.0, 1e-8 if floor else EPS, ALU.mult, ALU.max if floor else ALU.add))
                then(nc.vector.reciprocal(dst_inverse, dst_scale))

            layernorm(5)

            def quantise_x(s, low):
                dve.wait_ge(sem("xn_ready"), NT * s)
                then(nc.vector.tensor_reduce(xsc[:, 0, :], xn[:], AX.X, ALU.max, apply_absolute_value=True))
                scales(xsc[:, 1, :], xsc[:, 2, :], xsc[:, 0, :], s == 5)
                for t in range(NT):
                    then(nc.vector.tensor_scalar(xn[:, t, :], xn[:, t, :], xsc[:, 2, t:t + 1], ROUND, ALU.mult, ALU.add))
                then(nc.vector.tensor_scalar(xn[:], xn[:], -ROUND, 127.0, ALU.add, ALU.min))
                nc.vector.tensor_scalar(xi[:], xn[:], low, None, ALU.max).then_inc(sem("xi_ready"), 1)

            quantise_x(5, -127.0)
            dve.wait_ge(sem("w5_loaded"), 112)
            ew4 = ew[:].rearrange("p w c n -> p (w c) n")
            then(nc.vector.tensor_reduce(esc[:, 0, :], ew4, AX.X, ALU.max, apply_absolute_value=True))
            scales(esc[:, 1, :], esc[:, 2, :], esc[:, 0, :], True)
            for k in range(4):
                then(nc.vector.tensor_scalar(ediag[:, k, :], cst["ident"], esc[:, 1, k:k + 1], None, ALU.mult))
                then(nc.vector.tensor_scalar(eqf[:, k, :], ew4[:, k, :], esc[:, 2, k:k + 1], ROUND, ALU.mult, ALU.add))
            then(nc.vector.tensor_scalar(eqf[:], eqf[:], -ROUND, 127.0, ALU.add, ALU.min))
            nc.vector.tensor_scalar(eqi[:], eqf[:], -127.0, None, ALU.max).then_inc(sem("eqi_ready"), 1)
            for k in range(4):
                dve.wait_ge(sem("v5_psum"), k + 1)
                nc.vector.tensor_tensor(v5[:, 2 * k:2 * k + 2, :], bank[k][:].rearrange("p (t n) -> p t n", t=2),
                                        bv5[:].unsqueeze(1).to_broadcast([P, 2, D]), ALU.add).then_inc(sem("v5_ready"), 1)
            dve.wait_ge(sem("prep5_ready"), 8)
            for t in range(NT):
                dve.wait_ge(sem("q5_psum"), t // 2 + 1)
                then(nc.vector.scalar_tensor_tensor(q5[:, t, :], bank[4 + t // 2][:, D * (t % 2):D * (t % 2) + D], xsc[:, 1, t:t + 1], ewb[:, 0, :],
                                                    ALU.mult, ALU.mult))
                nc.vector.tensor_tensor(q5[:, t, :], q5[:, t, :], bq5[:], ALU.add).then_inc(sem("q5_ready"), 1)
            dve.wait_ge(sem("w6_loaded"), 48)
            then(nc.vector.tensor_reduce(fws[:, 0, :], fw[:], AX.X, ALU.add, apply_absolute_value=True))
            dve.sem_inc(sem("w6_sums"), 1)
            dve.wait_ge(sem("w6_total"), 1)
            then(nc.vector.tensor_scalar(fws[:, 2, :], bank[7][:, 0:3], 1.0 / (1024 * D), EPS, ALU.mult, ALU.add))
            nc.vector.reciprocal(fws[:, 3, :], fws[:, 2, :]).then_inc(sem("w6_scale"), 1)
            dve.sem_inc(sem("p5T_ready"), 2)
            dve.sem_inc(sem("x5_added"), 1)
            dve.wait_ge(sem("q5T_ready"), 4)
            with dve.Fori(0, NT // 2) as i:
                for u in range(2):
                    dve.wait_ge(sem("x5_added"), i * 2 + 1)
                    nc.vector.tensor_copy(q5s[:, u], q5T[:, :, bass.ds(i * 2 + u, 1), :].rearrange("p c t s -> p c (t s)")).then_inc(sem("q5s_ready"), 1)
                for u in range(2):
                    for g in range(4):
                        dve.wait_ge(sem("s5_psum"), i * 8 + (4 * u + g + 9))
                        nc.vector.tensor_reduce(n5[:, u, 4 * g:4 * g + 4], bank[5 + g % 2][:].rearrange("p (h n) -> p h n", h=4), AX.X, ALU.max,
                                                negate=True).then_inc(sem("n5_ready"), 1)
                        if u or g:
                            copy_p5T(i, 4 * u + g - 1)
                copy_p5T(i, 7)
                for u in range(2):
                    project(i, u)
                for u in range(2):
                    dve.wait_ge(sem("out5_psum"), i * 2 + (u + 1))
                    nc.vector.scalar_tensor_tensor(ot[:, u, :], bank[2][:, D * u:D * u + D], osc[:, u, 1:2], ewb[:, 1, :], ALU.mult, ALU.mult).then_inc(sem("ot_step"), 1)
                    dve.wait_ge(sem("ot_step"), i * 4 + (2 * u + 1))
                    nc.vector.tensor_tensor(ot[:, u, :], ot[:, u, :], bp5[:], ALU.add).then_inc(sem("ot_step"), 1)
                    dve.wait_ge(sem("ot_step"), i * 4 + (2 * u + 2))
                    xt = x[:, bass.ds(i * 2 + u, 1), :].rearrange("p t d -> p (t d)")
                    nc.vector.tensor_tensor(xt, xt, ot[:, u, :], ALU.add).then_inc(sem("x5_added"), 1)
            layernorm(6)
            quantise_x(6, -128.0)
            for w in range(2):
                nc.vector.tensor_scalar(fsg[:, :, w], xsc[:, 1, :], fws[:, 2, w:w + 1], None, ALU.mult).then_inc(sem("fsg_ready"), 1)
            dve.sem_inc(sem("x6_added"), 1)
            with dve.Fori(0, NT // 2) as i:
                for u in range(2):
                    dve.wait_ge(sem("fsg_ready"), 2)
                    dve.wait_ge(sem("silu_ready"), i * 4 + 2)
                    nc.vector.tensor_copy(fsn[:, u, :], fsg[:, bass.ds(i * 2 + u, 1), :].rearrange("p t w -> p (t w)")).then_inc(sem("fsn_ready"), 1)
                for u in range(2):
                    def step(n, ins):
                        ins.then_inc(sem("f_step"), 1)
                        dve.wait_ge(sem("f_step"), i * 20 + (10 * u + n))
                    for k in range(2):
                        dve.wait_ge(sem("silu_ready"), i * 4 + (2 * u + k + 3))
                        step(k + 1, nc.vector.scalar_tensor_tensor(fh[:, u, 512 * k:512 * k + 512], bank[4 * u + 2 + k][:], fsn[:, u, 1:2], fg[:, u, 512 * k:512 * k + 512],
                                                                   ALU.mult, ALU.mult))
                    step(3, nc.vector.tensor_reduce(fsd[:, u, 0:1], fh[:, u, :], AX.X, ALU.max, apply_absolute_value=True))
                    step(4, nc.vector.tensor_scalar(fsd[:, u, 1:2], fsd[:, u, 0:1], 1.0 / 127.0, EPS, ALU.mult, ALU.add))
                    step(5, nc.vector.reciprocal(fsd[:, u, 2:3], fsd[:, u, 1:2]))
                    step(6, nc.vector.tensor_scalar(fsd[:, u, 3:4], fsd[:, u, 1:2], fws[:, 2, 2:3], None, ALU.mult))
                    step(7, nc.vector.tensor_scalar(fq[:, u, :], fh[:, u, :], fsd[:, u, 2:3], ROUND, ALU.mult, ALU.add))
                    step(8, nc.vector.tensor_scalar(fq[:, u, :], fq[:, u, :], -ROUND, 127.0, ALU.add, ALU.min))
                    step(9, nc.vector.tensor_scalar(fhi[:, u, :], fq[:, u, :], -128.0, None, ALU.max))
                    nc.vector.tensor_copy(fsd[:, u, 0:1], fsd[:, u, 3:4]).then_inc(sem("f_step"), 1)
                for u in range(2):
                    dve.wait_ge(sem("down_psum"), i * 2 + (u + 1))
                    xt = x[:, bass.ds(i * 2 + u, 1), :].rearrange("p t d -> p (t d)")
                    nc.vector.scalar_tensor_tensor(xt, bank[4 * u + 1][:, 0:D], fsd[:, u, 3:4], xt, ALU.mult, ALU.add).then_inc(sem("x6_added"), 1)

        @block.tensor
        def _(pe):
            ident = cst["ident"]

            def transposes(s):
                for half in range(2):
                    for c in range(DC):
                        pe.wait_ge(sem("xn_ready"), NT * (s - 1) + 4 * half + 4)
                        for k in range(4):
                            last = nc.tensor.transpose(bank[2 * half + c][:, P * k:P * k + P], xn[:, 4 * half + k, P * c:P * c + P], ident)
                        last.then_inc(sem("xnT_psum"), 1)

            def all_xnT(s):
                pe.wait_ge(sem("xnT_act"), 2 * s)
                pe.wait_ge(sem("xnT_dve"), 2 * s)

            pe.wait_ge(sem("const_loaded"), 16)
            pe.wait_ge(sem("w1_loaded"), 48)
            for oc in range(DC):
                for dc in range(DC):
                    last = nc.tensor.transpose(bank[4][:, D * oc + P * dc:D * oc + P * dc + P], wo[:, dc, P * oc:P * oc + P], ident)
            last.then_inc(sem("prep1_psum"), 1)
            for ic in range(DC):
                for w, src in enumerate((wq, wkv)):
                    for oc in range(DC):
                        last = nc.tensor.matmul(bank[5 + ic][:, D * w:D * w + D], src[:, oc, P * ic:P * ic + P],
                                                cst["fourier"][:, D * oc:D * oc + D], start=(oc == 0), stop=(oc == DC - 1))
                last.then_inc(sem("prep1_psum"), 1)
            pe.wait_ge(sem("prep1_ready"), 1)
            for part in range(3):
                dst = (bank[7][:, 0:D], bank[7][:, D:2 * D], bank[4][:, 0:D])[part]
                for oc in range(DC):
                    last = nc.tensor.matmul(dst, cst["inverse"][:, 384 * oc + P * part:384 * oc + P * part + P], woT[:, oc, :],
                                            start=(oc == 0), stop=(oc == DC - 1))
                if part:
                    last.then_inc(sem("prep1_psum"), 1)
            transposes(1)
            all_xnT(1)
            pe.wait_ge(sem("prep1_ready"), 3)
            for t in range(NT):
                if t >= 4:
                    pe.wait_ge(sem("qk_ready"), t - 3)
                for c in range(DC):
                    last = nc.tensor.matmul(bank[t % 4][:], xnT[:, c, t, :], toF[:, c, :], start=(c == 0), stop=(c == DC - 1))
                last.then_inc(sem("qk_psum"), 1)
            pe.wait_ge(sem("prep1_ready"), 5)

            def attention_out(t):
                pe.wait_ge(sem("products_ready"), t + 1)
                if t >= 4:
                    pe.wait_ge(sem("x1_added"), t - 3)
                for j in range(4):
                    last = nc.tensor.matmul(bank[t % 4][:, 0:D], pr[:, t, j, :], toO[:, min(j, 2), :], start=(j == 0), stop=(j == 3))
                last.then_inc(sem("attn_psum"), 1)

            for t in range(NT):
                b = bank[4 + t % 4]
                pe.wait_ge(sem("qkn_ready"), 2 * t + 2)
                if t >= 4:
                    pe.wait_ge(sem("kqT_ready"), t - 3)
                for part in range(2):
                    nc.tensor.matmul(b[:, P * part:P * part + P], qk[:, t, D + P * part:D + P * part + P], cst["upper"], start=True, stop=True)
                for part in range(2):
                    last = nc.tensor.transpose(b[:, D + P * part:D + P * part + P], qk[:, t, P * part:P * part + P], ident)
                last.then_inc(sem("kq_psum"), 1)
                if t >= 1:
                    attention_out(t - 1)
            attention_out(NT - 1)
            pe.wait_ge(sem("kqT_ready"), NT)
            pe.wait_ge(sem("s2_loaded"), 16 * (HG + 2))
            for k in range(8):
                if k >= 2:
                    pe.wait_ge(sem("tap_ready"), k - 1)
                nc.tensor.matmul(bank[4 + k % 2][:], cst["reverse"], tapR[:, 2 * k:2 * k + 2, :].rearrange("p h n -> p (h n)"),
                                 start=True, stop=True).then_inc(sem("tap_psum"), 1)
            for half in range(2):
                for c in range(DC):
                    if half:
                        pe.wait_ge(sem("cxT_act" if c == 0 else "cxT_dve"), 1)
                    for k in range(4):
                        last = nc.tensor.transpose(bank[6 + c][:, P * k:P * k + P], cx[:, 4 * half + k, P * c:P * c + P], ident)
                    last.then_inc(sem("cxT_psum"), 1)
            transposes(2)
            pe.wait_ge(sem("tap_ready"), 8)
            pe.wait_ge(sem("cxT_act"), 2)
            pe.wait_ge(sem("cxT_dve"), 2)
            for k in range(4):
                pe.wait_ge(sem("wsk_ready"), k + 1)
                nc.tensor.matmul(bank[4 + k][:], cst["group8"], wsk[:, 2 * k:2 * k + 2, :].rearrange("p t d -> p (t d)"),
                                 start=True, stop=True).then_inc(sem("skip_psum"), 1)
            all_xnT(2)
            for h in range(HG):
                pe.wait_ge(sem("kvp_ready"), 2 * h + 2)
                if h >= 2:
                    pe.wait_ge(sem("yx_ready"), 2 * (h - 1))
                nc.tensor.matmul(bank[2 * (h % 2)][:], tap[:, h, 0:P], kvp[:, h % 2, 0, :], start=True, stop=True).then_inc(sem("conv_psum"), 1)
                nc.tensor.matmul(bank[2 * (h % 2) + 1][:], tap[:, h, P:2 * P], kvp[:, h % 2, 0, :], start=True, stop=False)
                nc.tensor.matmul(bank[2 * (h % 2) + 1][:], tap[:, h, 0:P], kvp[:, h % 2, 1, :], start=False, stop=True).then_inc(sem("conv_psum"), 1)
            pe.wait_ge(sem("yT_ready"), 2 * HG)
            pe.wait_ge(sem("skip_added"), 4)
            for k in range(4):
                for tt in range(2):
                    for c in range(DC):
                        last = nc.tensor.transpose(bank[4 + k][:, D * tt + P * c:D * tt + P * c + P], yT[:, c, 2 * k + tt, :], ident)
                last.then_inc(sem("conv_out_psum"), 1)
            pe.wait_ge(sem("gate_loaded"), 80)
            pe.wait_ge(sem("x2_added"), 4)
            nc.tensor.transpose(bank[4][:, 0:64], b12[:, :], ident[0:64, 0:64]).then_inc(sem("bT_psum"), 1)
            transposes(3)
            all_xnT(3)
            for t in range(NT):
                for c in range(DC):
                    last = nc.tensor.matmul(bank[7][:, NE * t:NE * t + NE], xnT[:, c, t, :], wg[:, c, :], start=(c == 0), stop=(c == DC - 1))
            last.then_inc(sem("logits_psum"), 1)
            pe.wait_ge(sem("comb_ready"), 1)
            for t in range(NT):
                last = nc.tensor.transpose(bank[5 + t // 4][0:NE, P * (t % 4):P * (t % 4) + P], comb[:, t, :], ident)
                if t % 4 == 3:
                    last.then_inc(sem("combT_psum"), 1)
            pe.wait_ge(sem("combT_ready"), 2)
            for t in range(NT):
                last = nc.tensor.matmul(bank[t // 2][:, D * (t % 2):D * (t % 2) + D], combT[:, t, :], b3[:, :], start=True, stop=True)
                if t % 2:
                    last.then_inc(sem("b3_psum"), 1)
            pe.wait_ge(sem("b3_added"), 4)
            pe.wait_ge(sem("bT_ready"), 1)
            pe.wait_ge(sem("xl_ready"), 1)
            pe.sem_inc(sem("expert_done"), 2)

            with pe.Fori(0, NE // 2) as i:
                for u in range(2):
                    pe.wait_ge(sem("w_split"), i * 2 + (u + 2))
                    w1 = [w[:, u, W1].rearrange("p (c n) -> p c n", c=DC) for w in (whi, wlo)]
                    w2 = [w[:, u, W2].rearrange("p (c n) -> p c n", c=FC) for w in (whi, wlo)]
                    w3 = [w[:, u, W3].rearrange("p (c n) -> p c n", c=FC) for w in (whi, wlo)]
                    for half in range(2):
                        n4 = i * 16 + (8 * u + 4 * half)
                        tok = slice(512 * half, 512 * half + 512)
                        passes = ((0, 0), (0, 1), (1, 0))
                        for f in range(FC):
                            col = slice(P * f, P * f + P)
                            pe.wait_ge(sem("h2_f32"), n4 + (f + 1))
                            for c in range(DC):
                                for a_, b_ in passes:
                                    last = nc.tensor.matmul(bank[f][:], w1[a_][:, c, col], (xh, xl)[b_][:, c, tok],
                                                            start=(c == 0 and a_ + b_ == 0), stop=(c == DC - 1 and a_ == 1))
                            last.then_inc(sem("l1_psum"), 1)
                        for f in range(FC):
                            col = slice(P * f, P * f + P)
                            pe.wait_ge(sem("h1_f32"), n4 + (f + 1))
                            for c in range(FC):
                                if f == 0:
                                    pe.wait_ge(sem("h1_lo"), n4 + (c + 1))
                                for a_, b_ in passes:
                                    last = nc.tensor.matmul(bank[f][:], w2[a_][:, c, col], h1[:, half, b_, c, :],
                                                            start=(c == 0 and a_ + b_ == 0), stop=(c == FC - 1 and a_ == 1))
                            last.then_inc(sem("l2_psum"), 1)
                        for k in range(4):
                            pe.wait_ge(sem("expert_added"), n4 + (k + 5))
                            for c in range(FC):
                                if k == 0:
                                    pe.wait_ge(sem("h2_lo"), n4 + (c + 5))
                                for a_, b_ in passes:
                                    last = nc.tensor.matmul(bank[4 + k][:, 0:D], h2[:, half, b_, c, P * k:P * k + P], w3[a_][:, c, :],
                                                            start=(c == 0 and a_ + b_ == 0), stop=(c == FC - 1 and a_ == 1))
                            last.then_inc(sem("l3_psum"), 1)
                    pe.wait_ge(sem("l3_psum"), i * 16 + (8 * u + 8))
                    pe.sem_inc(sem("expert_done"), 1)
            pe.wait_ge(sem("w4_loaded"), 96)
            x_done(pe, 3, NT - 1)

            def prep_copied(n):
                pe.wait_ge(sem("prep4_act"), (n + 1) // 2)
                pe.wait_ge(sem("prep4_dve"), n // 2)

            i64 = ident[0:64, 0:64]
            for k in range(2):
                for j in range(8):
                    last = nc.tensor.transpose(bank[k][0:64, 64 * j:64 * j + 64], wkvb[:, 8 * k + j, 0:64], i64)
                last.then_inc(sem("prep4_psum"), 1)
            for k in range(2):
                for j in range(8):
                    last = nc.tensor.transpose(bank[2 + k][:, 64 * j:64 * j + 64], wkvb[:, 8 * k + j, 64:192], i64)
                last.then_inc(sem("prep4_psum"), 1)
            for k in range(4):
                for j in range(4):
                    last = nc.tensor.transpose(bank[4 + k][0:64, P * j:P * j + P], wqb[:, 0, 4 * k + j, 0:64], ident)
                last.then_inc(sem("prep4_psum"), 1)
            prep_copied(2)
            for k in range(2):
                for j in range(8):
                    last = nc.tensor.transpose(bank[k][0:64, 64 * j:64 * j + 64], wqb[0:64, 1, 8 * k + j, 0:64], i64)
                last.then_inc(sem("prep4_psum"), 1)
            prep_copied(10)
            for lo, hi, at in ((0, P, 2), (P, QL, 4)):
                for k in range(2):
                    for j in range(8):
                        h = 8 * k + j
                        last = nc.tensor.matmul(bank[at + k][0:hi - lo, 64 * j:64 * j + 64], wqbT[:, h, lo:hi], wkT[:, h, :], start=True, stop=True)
                    last.then_inc(sem("prep4_psum"), 1)
            for k in range(4):
                for j in range(2):
                    for odd in range(2):
                        h = 4 * k + 2 * j + odd
                        last = nc.tensor.matmul(bank[(6, 7, 0, 1)[k]][64 * odd:64 * odd + 64, D * j:D * j + D], wvT[:, h, :], wo4[:, h, :], start=True, stop=True)
                last.then_inc(sem("prep4_psum"), 1)
            prep_copied(18)
            transposes(4)
            all_xnT(4)

            def latents(i, u):
                t = bass.ds(i * 2 + u, 1)
                if u == 0:
                    pe.wait_ge(sem("oT_ready"), i * 4 + 1)
                else:
                    pe.wait_ge(sem("kT_ready"), i * 2 + 1)
                for dst, w in ((bank[0][:, 0:P], wqa[:, :, 0:P]), (bank[0][:, P:2 * P], wkva[:]), (bank[0][0:64, 2 * P:3 * P], wqa[:, :, P:QL])):
                    for c in range(DC):
                        last = nc.tensor.matmul(dst, w[:, c, :], xnT[:, c, t, :].rearrange("p t s -> p (t s)"), start=(c == 0), stop=(c == DC - 1))
                last.then_inc(sem("lat_psum"), 1)
                pe.wait_ge(sem("lat_copied"), i * 2 + (u + 1))
                nc.tensor.transpose(bank[0][:, 3 * P:4 * P], kvT[:, u, :], ident).then_inc(sem("kvn_psum"), 1)

            def queries(i, u):
                for g in range(4):
                    hs = slice(4 * g, 4 * g + 4)
                    pe.wait_ge(sem("q4_copied"), i * 8 + (4 * u + g + 1))
                    nc.tensor.matmul(bank[1 + g % 2][:], ql0[:, u, :], wqb[:, 0, hs, :].rearrange("p h n -> p (h n)"), start=True, stop=False)
                    nc.tensor.matmul(bank[1 + g % 2][:], ql1[:, u, :], wqb[0:64, 1, hs, :].rearrange("p h n -> p (h n)"), start=False, stop=True).then_inc(sem("q4_psum"), 1)
                pe.wait_ge(sem("kvr_ready"), i * 2 + (u + 1))
                nc.tensor.transpose(bank[0][:, 3 * P:4 * P], kvr[:, u, :], ident).then_inc(sem("kT_psum"), 1)

            def turn_q(i, u, g):
                pe.wait_ge(sem("roped"), i * 8 + (4 * u + g + 1))
                if g < 2 and u == 0:
                    pe.wait_ge(sem("pT_ready"), i * 8 + (g + 1))
                else:
                    pe.wait_ge(sem("qT_ready"), i * 8 + (4 * u + g - 1))
                for k in range(4):
                    last = nc.tensor.transpose(bank[3 + g % 2][:, P * k:P * k + P], qs[:, u, 4 * g + k, :], ident)
                last.then_inc(sem("t4_psum"), 1)

            def scores(i, u, g):
                pe.wait_ge(sem("qT_ready"), i * 8 + (4 * u + g + 1))
                pe.wait_ge(sem("kT_ready"), i * 2 + (u + 1))
                pe.wait_ge(sem("s4_masked"), i * 8 + (4 * u + g + 1))
                for k in range(4):
                    last = nc.tensor.matmul(bank[5 + g % 2][:, P * k:P * k + P], qT[:, u, 4 * g + k, :], kT[:, u, :], start=True, stop=True)
                last.then_inc(sem("s4_psum"), 1)

            def turn_p(i, u, g):
                pe.wait_ge(sem("p4_ready"), i * 8 + (4 * u + g + 1))
                if g < 2 and u == 0:
                    pe.wait_ge(sem("qT_ready"), i * 8 + 8)
                else:
                    pe.wait_ge(sem("pT_ready"), i * 8 + (4 * u + g + 1))
                for k in range(4):
                    last = nc.tensor.transpose(bank[3 + g % 2][:, P * k:P * k + P], sm[:, u, 4 * g + k, :], ident)
                last.then_inc(sem("pt4_psum"), 1)

            def values(i, u):
                pe.wait_ge(sem("x4_added"), i * 2 + (u + 1))
                pe.wait_ge(sem("kT_ready"), i * 2 + 2)
                pe.wait_ge(sem("oT_ready"), i * 4 + (2 * u + 1))
                pe.wait_ge(sem("pT_ready"), i * 8 + (4 * u + 6))
                pairs = pT[:, u].rearrange("p (j odd) s -> p odd j s", odd=2)
                for k in range(2):
                    for odd in range(2):
                        last = nc.tensor.matmul(bank[7 if k == 0 else 0][64 * odd:64 * odd + 64, :], kvr[:, u, 0:64], pairs[:, odd, 4 * k:4 * k + 4, :], start=True, stop=True)
                    last.then_inc(sem("pv_psum"), 1)

            def output(i, u):
                pe.wait_ge(sem("oT_ready"), i * 4 + (2 * u + 3))
                for j in range(H4 // 2):
                    last = nc.tensor.matmul(bank[7][:, 0:D], oT[:, u, j, :], wvo[:, j, :], start=(j == 0), stop=(j == H4 // 2 - 1))
                last.then_inc(sem("out4_psum"), 1)

            with pe.Fori(0, NT // 2) as i:
                for u in range(2):
                    latents(i, u)
                    queries(i, u)
                steps = [(u, g) for u in range(2) for g in range(4)]
                for j, (u, g) in enumerate(steps):
                    turn_q(i, u, g)
                    if j >= 1:
                        scores(i, *steps[j - 1])
                scores(i, *steps[7])
                for g in range(4):
                    turn_p(i, 0, g)
                values(i, 0)
                for g in range(4):
                    turn_p(i, 1, g)
                output(i, 0)
                values(i, 1)
                output(i, 1)
            x_done(pe, 4, NT - 1)
            pe.wait_ge(sem("w5_loaded"), 112)
            for ic in range(DC):
                for oc in range(4):
                    last = nc.tensor.transpose(bank[ic][:, P * oc:P * oc + P], ewkv[:, oc, P * ic:P * ic + P], ident)
                last.then_inc(sem("prep5_psum"), 1)
            pe.wait_ge(sem("prep5_ready"), 2)
            for oc in range(DC):
                for half in range(2):
                    for ic in range(DC):
                        last = nc.tensor.matmul(bank[2 + 2 * oc + half][:], wkvT[:, ic, P * oc:P * oc + P],
                                                cxT[:, ic, 4 * half:4 * half + 4, :].rearrange("p t s -> p (t s)"), start=(ic == 0), stop=(ic == DC - 1))
                    last.then_inc(sem("prep5_psum"), 1)
            pe.wait_ge(sem("identb_ready"), 1)

            def turn_x(s):
                pe.wait_ge(sem("xi_ready"), s - 4)
                for c in range(DC):
                    b16 = bank[c][:].bitcast(BF16)
                    for t in range(NT):
                        last = nc.tensor.transpose(b16[:, P * t:P * t + P], xi[:, t, P * c:P * c + P], identb[:])
                    last.then_inc(sem("xiT_psum"), 1)

            turn_x(5)
            pe.wait_ge(sem("eqi_ready"), 1)
            b16 = bank[6][:].bitcast(BF16)
            for w in range(2):
                for ic in range(DC):
                    for oc in range(DC):
                        at = 512 * w + D * ic + P * oc
                        last = nc.tensor.transpose(b16[:, at:at + P], eqi[:, 2 * w + oc, P * ic:P * ic + P], identb[:])
            last.then_inc(sem("prep5_psum"), 1)
            nc.tensor.matmul(bank[7][:], cst["ones"], ediag[:].rearrange("p k n -> p (k n)"), start=True, stop=True).then_inc(sem("prep5_psum"), 1)
            pe.wait_ge(sem("xiT_ready"), 2)
            pe.wait_ge(sem("prep5_ready"), 6)
            for t in range(NT):
                for ic in range(DC):
                    last = nc.tensor.matmul(bank[t // 2][:, D * (t % 2):D * (t % 2) + D], cxT[:, ic, t, :], wkvT[:, ic, D:2 * D], start=(ic == 0), stop=(ic == DC - 1))
                if t % 2:
                    last.then_inc(sem("v5_psum"), 1)
            pe.wait_ge(sem("prep5_ready"), 7)
            pe.wait_ge(sem("prep5_ready"), 8)
            for t in range(NT):
                for ic in range(DC):
                    last = nc.tensor.matmul(bank[4 + t // 2][:, D * (t % 2):D * (t % 2) + D], xiT[:, ic, t, :], ewT[:, 0, ic, :], start=(ic == 0), stop=(ic == DC - 1))
                if t % 2:
                    last.then_inc(sem("q5_psum"), 1)
            pe.wait_ge(sem("v5_ready"), 4)
            for half in range(2):
                for c in range(DC):
                    pe.wait_ge(sem("q5_ready"), 4 * half + 4)
                    for k in range(4):
                        last = nc.tensor.transpose(bank[2 * half + c][:, P * k:P * k + P], q5[:, 4 * half + k, P * c:P * c + P], ident)
                    last.then_inc(sem("q5T_psum"), 1)
            pe.wait_ge(sem("w6_sums"), 1)
            pe.wait_ge(sem("q5_ready"), NT)
            nc.tensor.matmul(bank[7][:, 0:3], cst["ones"], fws[:, 0, :], start=True, stop=True).then_inc(sem("w6_total"), 1)
            pe.wait_ge(sem("w6_scale"), 1)
            pe.wait_ge(sem("q5T_ready"), 4)
            pe.sem_inc(sem("s5_psum"), 8)

            def scores5(i, u, g):
                pe.wait_ge(sem("kx_ready"), i * 4 + (2 * u + g // 2 + 1))
                pe.wait_ge(sem("q5s_ready"), i * 2 + (u + 1))
                pe.wait_ge(sem("exp5_ready"), i * 8 + (4 * u + g + 1))
                nc.tensor.matmul(bank[5 + g % 2][:], q5s[:, u, g // 2, :], kx[:, u, g // 2, 4 * (g % 2):4 * (g % 2) + 4, :].rearrange("p h s -> p (h s)"),
                                 start=True, stop=True).then_inc(sem("s5_psum"), 1)

            def turn_p5(i, u, g):
                pe.wait_ge(sem("exp5_ready"), i * 8 + (4 * u + g + 3))
                pe.wait_ge(sem("p5T_ready"), i * 8 + (4 * u + g + 1))
                for k in range(4):
                    last = nc.tensor.transpose(bank[3 + g % 2][:, P * k:P * k + P], s5m[:, u, 4 * g + k, :], ident)
                last.then_inc(sem("pt5_psum"), 1)

            def values5(i, u):
                pe.wait_ge(sem("p5T_ready"), i * 8 + (4 * u + 6))
                for h in range(H4):
                    last = nc.tensor.matmul(bank[(7, 0)[u]][:, 16 * h:16 * h + 16], p5T[:, u, h, :],
                                            v5[:, bass.ds(i * 2 + u, 1), 16 * h:16 * h + 16].rearrange("p t d -> p (t d)"), start=True, stop=True)
                last.then_inc(sem("pv5_psum"), 1)

            with pe.Fori(0, NT // 2) as i:
                steps = [(u, g) for u in range(2) for g in range(4)]
                for j, (u, g) in enumerate(steps):
                    scores5(i, u, g)
                    if j >= 1:
                        turn_p5(i, *steps[j - 1])
                turn_p5(i, *steps[7])
                for u in range(2):
                    values5(i, u)
                for u in range(2):
                    pe.wait_ge(sem("oi_ready"), i * 2 + (u + 1))
                    if u == 1:
                        pe.wait_ge(sem("oiT_ready"), i * 2 + 1)
                    for c in range(DC):
                        last = nc.tensor.transpose(bank[1][:, 0:P].bitcast(BF16)[:, P * c:P * c + P], oi[:, u, P * c:P * c + P], identb[:])
                    last.then_inc(sem("oiT_psum"), 1)
                for u in range(2):
                    pe.wait_ge(sem("oiT_ready"), i * 2 + (u + 1))
                    pe.wait_ge(sem("x5_added"), i * 2 + (u + 1))
                    for c in range(DC):
                        last = nc.tensor.matmul(bank[2][:, D * u:D * u + D], oiT[:, u, c, :], ewT[:, 1, c, :], start=(c == 0), stop=(c == DC - 1))
                    last.then_inc(sem("out5_psum"), 1)
            x_done(pe, 5, NT - 1)
            turn_x(6)
            pe.wait_ge(sem("w6_int"), 3)
            for w in range(2):
                for ic in range(DC):
                    b16 = bank[2 + 2 * w + ic][:].bitcast(BF16)
                    for oc in range(8):
                        last = nc.tensor.transpose(b16[:, P * oc:P * oc + P], fi[:, w, D * oc + P * ic:D * oc + P * ic + P], identb[:])
                    last.then_inc(sem("w6T_psum"), 1)
            for q in range(2):
                b16 = bank[6 + q][:].bitcast(BF16)
                for k in range(4):
                    for oc in range(DC):
                        last = nc.tensor.transpose(b16[:, D * k + P * oc:D * k + P * oc + P], fi[:, 2, 1024 * oc + P * (4 * q + k):1024 * oc + P * (4 * q + k) + P], identb[:])
                last.then_inc(sem("w6T_psum"), 1)
            pe.wait_ge(sem("w6T_ready"), 6)
            pe.wait_ge(sem("xiT_ready"), 4)
            with pe.Fori(0, NT // 2) as i:
                for u in range(2):
                    pe.wait_ge(sem("fsn_ready"), i * 2 + (u + 1))
                    pe.wait_ge(sem("x6_added"), i * 2 + 1)
                    for k in range(4):
                        for ic in range(DC):
                            last = nc.tensor.matmul(bank[4 * u + k][:], xiT[:, ic, bass.ds(i * 2 + u, 1), :].rearrange("p t s -> p (t s)"),
                                                    fguT[:, ic, k // 2, 512 * (k % 2):512 * (k % 2) + 512], start=(ic == 0), stop=(ic == DC - 1))
                    last.then_inc(sem("gu_psum"), 1)
                for u in range(2):
                    pe.wait_ge(sem("f_step"), i * 20 + (10 * u + 10))
                    b16 = bank[4 * u][:].bitcast(BF16)
                    for c in range(8):
                        last = nc.tensor.transpose(b16[:, P * c:P * c + P], fhi[:, u, P * c:P * c + P], identb[:])
                    last.then_inc(sem("fhT_psum"), 1)
                for u in range(2):
                    pe.wait_ge(sem("fhT_ready"), i * 2 + (u + 1))
                    for c in range(8):
                        last = nc.tensor.matmul(bank[4 * u + 1][:, 0:D], fhT[:, u, c, :], fdT[:, c, :], start=(c == 0), stop=(c == 7))
                    last.then_inc(sem("down_psum"), 1)
    return nc


_INS = ['x', 'fside_S2_0', 'ctx_2048', 'L0_attn_W_q', 'L0_attn_W_kv', 'L0_attn_W_o', 'L0_ffn_W1', 'L0_ffn_b1',
        'L0_ffn_W2', 'L0_ffn_b2', 'L0_ffn_W3', 'L0_ffn_b3', 'L0_ffn_Wg', 'L0_ffn_bg',
        'L1_attn_Wqa', 'L1_attn_Wqb', 'L1_attn_Wkva', 'L1_attn_Wkvb', 'L1_attn_Wo', 'L1_xattn_wq', 'L1_xattn_bq',
        'L1_xattn_wkv', 'L1_xattn_bkv', 'L1_xattn_wp', 'L1_xattn_bp', 'L1_ffn_w_gate', 'L1_ffn_w_up', 'L1_ffn_w_down']


def kernel(**inputs):
    import concourse.bacc as _bacc
    from concourse import mybir as _mybir
    from concourse.bass_utils import run_bass_kernel_spmd as _run

    nc = _bacc.Bacc("TRN2", target_bir_lowering=False, num_devices=1)
    host = {name: np.ascontiguousarray(inputs[name]) for name in _INS}
    taps = inputs["L0_xattn_k"]
    kpad = np.zeros((taps.shape[0], P + D), np.float32)
    kpad[:, P:] = taps
    host["kpad"] = kpad
    host["consts"] = shape_constants()[0]
    arrays, args = {}, {}
    for name, v in host.items():
        arrays[f"in_{name}"] = v
        args[name] = nc.dram_tensor(f"in_{name}", v.shape, _mybir.dt.from_np(v.dtype), kind="ExternalInput").ap()
    out = nc.dram_tensor("out_0", (NT, P, D), F32, kind="ExternalOutput").ap()
    decoder_kernel(nc, args, out)
    r = _run(nc, [arrays], core_ids=[0])
    return r.results[0]["out_0"]
```

```python
from contextlib import ExitStack

import numpy as np

import concourse.bass as bass
from concourse import mybir

P = 128
NT = 8
D = 256
DC = D // P
NE = 8
FH = 512
FC = FH // P
CH = 8
HG = P // CH
H4 = 16
QL = 192
S4 = float(np.float32(P) ** np.float32(-0.5))
SLOTS = 2 * P
ET = 2 * NT * P // SLOTS + NE - 1
ROUND = 12582912.0
EPS = 1e-5

ALU = mybir.AluOpType
ACT = mybir.ActivationFunctionType
AX = mybir.AxisListType
F32 = mybir.dt.float32
F16 = mybir.dt.float16
BF16 = mybir.dt.bfloat16
I32 = mybir.dt.int32
U32 = mybir.dt.uint32


EARLY = ("fourier", "inverse", "reverse", "group8")


def shape_constants():
    n = np.arange(16)
    parts = {}
    parts["ident"] = np.eye(P)
    parts["upper"] = np.triu(np.ones((P, P)))
    parts["reverse"] = np.eye(P)[::-1]
    parts["group8"] = np.kron(np.eye(HG), np.ones((CH, CH)))
    parts["ones"] = np.ones((P, P))
    f = np.zeros((D, 2, 16, 8))
    c = np.zeros((3, 16, 8, D))
    for h in range(16):
        for k in range(8):
            s = slice(16 * h, 16 * h + 16)
            co, si = np.cos(2 * np.pi * k * n / 16), np.sin(2 * np.pi * k * n / 16)
            f[s, 0, h, k] = 0.25 if k == 0 else co * np.sqrt(2) / 4
            f[s, 1, h, k] = 0.25 * (-1.0) ** n if k == 0 else si * np.sqrt(2) / 4
            c[0, h, k, s] = co / 16
            c[1, h, k, s] = (-1.0) ** n / 16 if k == 0 else -co / 16
            c[2, h, k, s] = si / 16
    f = f.reshape(D, D)
    parts["fourier"] = np.concatenate([f[:P], f[P:]], 1)
    ct = c.reshape(3 * P, D).T
    parts["inverse"] = np.concatenate([ct[:P], ct[P:]], 1)
    inv = 1.0 / 10000.0 ** (np.arange(32, dtype=np.float32) * np.float32(2.0) / np.float32(64))
    ang = (np.arange(P, dtype=np.float32)[:, None] * inv.astype(np.float32)[None, :]).astype(np.float32)
    parts["cos"] = np.repeat(np.cos(ang), 2, axis=1)
    parts["sin"] = np.stack([-np.sin(ang), np.sin(ang)], axis=2).reshape(P, 64)
    parts["causal"] = np.where(np.tril(np.ones((P, P))) > 0, 0.0, -1e30)
    parts["head16"] = np.kron(np.eye(8), np.ones((16, 1))) * 0.25
    parts["iota"] = np.tile(np.arange(16.0), (P, 1))
    parts["before"] = np.tile(np.tril(np.ones((NE, NE))).reshape(1, -1), (P, 1))
    at, cols = {}, 0
    parts = {name: parts[name] for name in sorted(parts, key=lambda name: name in EARLY)}
    for name, a in parts.items():
        at[name] = (cols, cols + a.shape[1])
        cols += a.shape[1]
    return np.concatenate(list(parts.values()), 1).astype(np.float32), at


CONST_AT = shape_constants()[1]


def decoder_kernel(nc, a, out):
    with ExitStack() as ctx:
        named = {}

        def sem(name):
            if name not in named:
                named[name] = ctx.enter_context(nc.semaphore(name))
            return named[name]

        def sb(name, shape, dt=F32, scope=ctx):
            return scope.enter_context(nc.sbuf_tensor(name, shape, dt))

        bank = [ctx.enter_context(nc.psum_tensor(f"bank{k}", [P, 512], F32)) for k in range(8)]

        ncol = max(hi for _, hi in CONST_AT.values())
        nlate = min(CONST_AT[name][0] for name in EARLY)
        const = sb("const", [P, nlate])
        cst = {name: const[:, lo:hi] for name, (lo, hi) in CONST_AT.items() if name not in EARLY}
        x = sb("x", [P, NT, D])
        s2c = ExitStack()
        cx = sb("cx", [P, NT, D], F32, s2c)
        s2c.close()
        wo4a = sb("wo4a", [P, H4 // 2, D])
        cxT = sb("cxT", [P, DC, NT, P])
        st = sb("st", [P, NT, 6])
        mv = sb("mv", [P, NT, 2])
        ve = sb("ve", [P, NT])
        sd = sb("sd", [P, NT])
        rs = sb("rs", [P, NT, 2])
        nw = sb("nw", [P, 2, NT])

        b12 = sb("b12", [2 * NE * FC, P], F32)
        identb = sb("identb", [P, P], BF16)
        xsc = sb("xsc", [P, 3, NT])
        fws = sb("fws", [P, 4, 3])
        fsg = sb("fsg", [P, NT, 2])
        fsn = sb("fsn", [P, 2, 2])
        fsd = sb("fsd", [P, 2, 4])
        be = sb("be", [P, 2, 2, FC])
        bT = sb("bT", [P, 2 * NE * FC], F32)
        b3 = sb("b3", [NE, D], F32)
        wg = sb("wg", [P, DC, NE], F32)
        bg = sb("bg", [P, NE], F32)
        lg = sb("lg", [P, NT, NE], F32)
        gm = sb("gm", [P, NT], F32)
        gs = sb("gs", [P, 2, NT], F32)
        gw = sb("gw", [P, NT, NE], F32)
        top = sb("top", [P, NT, 8], F32)
        topi = sb("topi", [P, NT, 8], U32)
        topf = sb("topf", [P, NT, 8], F32)
        pick = sb("pick", [P, 2, NT, NE], F32)
        pickw = sb("pickw", [P, 2, NT, NE], F32)
        sel = sb("sel", [P, NT, NE], F32)
        pre = sb("pre", [P, NT + 1, NE], F32)
        tl = sb("tl", [P, 3, NE], F32)
        tri = sb("tri", [P, NE, NE], F32)
        posf = sb("posf", [P, 2, NT], F32)
        pos = sb("pos", [P, 2, NT], U32)
        eidg = sb("eidg", [P, 16, NE - 1], F32)
        eidf = sb("eidf", [P, 16], F32)
        eid = sb("eid", [P, 16], I32)
        comb = sb("comb", [P, NT, NE], F32)
        sx = ExitStack()
        xn = sb("xn", [P, NT, D], F32, sx)
        xnT = sb("xnT", [P, DC, NT, P], F32, sx)
        sx.close()
        sx = ExitStack()
        sb("xn_place", [P, NT, D], F32, sx)
        combT = sb("combT", [NE, NT, P], F32, sx)
        sx.close()
        sx = ExitStack()
        xg = sb("xg", [P, 2, 2, D], F32, sx)
        xgT = sb("xgT", [P, 2, 2, DC, SLOTS], F16, sx)
        yb = sb("yb", [P, 2, 2, D], F32, sx)
        hf = sb("hf", [P, 2, 2 * SLOTS], F32, sx)
        sx.close()
        yg = sb("yg", [P, NT, 2, D])

        s3 = ExitStack()
        WE = 2 * 2 * FH + FC * D + 2 * FH
        wraw = sb("wraw", [P, 2, WE // 2], F32, s3)
        s3e = ExitStack()
        early = sb("early", [P, NE // 2, 2, WE], F16, s3e)
        const12 = sb("const12", [P, ncol - nlate], F32, s3e)
        cst.update({name: const12[:, lo - nlate:hi - nlate] for name, (lo, hi) in CONST_AT.items() if name in EARLY})
        s1, s2 = ExitStack(), ExitStack()
        tapR = sb("tapR", [P, HG, D], F32, s3e)
        skip = sb("skip", [P, 1], F32, s3e)
        wq = sb("wq", [P, DC, D], F32, s1)
        wkv = sb("wkv", [P, DC, D], F32, s1)
        wo = sb("wo", [P, DC, D], F32, s1)
        woT = sb("woT", [P, DC, D], F32, s1)
        toF = sb("toF", [P, DC, 2 * D], F32, s1)
        toO = sb("toO", [P, 3, D], F32, s1)
        sq = sb("sq", [P, 2, 512], F32, s1)
        ss = sb("ss", [P, NT * 32], F32, s1)
        sn = sb("sn", [P, NT * 32], F32, s1)
        rn = sb("rn", [P, 2, NT * 32], F32, s1)
        nn = sb("nn", [P, 2, NT * 32], F32, s1)
        qk = sb("qk", [P, NT, 512], F32, s1)
        kqT = sb("kqT", [P, 4, 512], F32, s1)
        pr = sb("pr", [P, 2, 4, P], F32, s1)
        s1.close()
        tap = sb("tap", [P, HG, D], F32, s2)
        wsk = sb("wsk", [P, NT, D], F32, s2)
        sk2 = sb("sk2", [P, 2, 512], F32, s2)
        kvp = sb("kvp", [P, 2, DC, 512], F32, s2)
        yx = sb("yx", [P, 2, 512], F32, s2)
        yT = sb("yT", [P, DC, NT, P], F32, s2)

        s2.close()
        s3e.close()
        wsp = sb("wsp", [P, NE, 2, WE], F16, s3)
        h1 = sb("h1", [P, 2, FC, SLOTS], F16, s3)
        h2 = sb("h2", [P, 2, FC, SLOTS], F16, s3)

        s4w = ExitStack()
        wqa = sb("wqa", [P, DC, QL], F32, s4w)
        wkva = sb("wkva", [P, DC, P], F32, s4w)
        s4w.close()
        s3.close()
        s4 = ExitStack()
        wqb = sb("wqb", [P, 2, H4, P], F32, s4)
        wvo = sb("wvo", [P, H4 // 2, D], F32, s4)
        s4p = ExitStack()
        wqbT = sb("wqbT", [64, H4, QL], F32, s4p)
        wkT = sb("wkT", [64, H4, 64], F32, s4p)
        wvT = sb("wvT", [P, H4, 64], F32, s4p)
        wo4b = sb("wo4b", [P, H4 // 2, D], F32, s4p)
        wkvb = sb("wkvb", [64, H4, 192], F32, s4p)
        s4p.close()
        ql0 = sb("ql0", [P, 2, P], F32, s4)
        ql1 = sb("ql1", [64, 2, P], F32, s4)
        kvT = sb("kvT", [P, 2, P], F32, s4)
        kvr = sb("kvr", [P, 2, P], F32, s4)
        kT = sb("kT", [P, 2, P], F32, s4)
        rk = sb("rk", [P, 2, 64], F32, s4)
        rq = sb("rq", [P, 2, 2, 4, 64], F32, s4)
        qs = sb("qs", [P, 2, H4, P], F32, s4)
        qT = sb("qT", [P, 2, H4, P], F32, s4)
        sm = sb("sm", [P, 2, H4, P], F32, s4)
        nm = sb("nm", [P, 2, H4], F32, s4)
        rsum = sb("rsum", [P, 2, H4], F32, s4)
        rinv = sb("rinv", [P, 2, H4], F32, s4)
        pT = sb("pT", [P, 2, H4, P], F32, s4)
        oT = sb("oT", [P, 2, H4 // 2, P], F32, s4)
        s4.close()

        s56, s5 = ExitStack(), ExitStack()
        xi = sb("xi", [P, NT, D], BF16, s56)
        xiT = sb("xiT", [P, DC, NT, P], BF16, s56)
        fw = sb("fw", [P, 3, 2048], F32, s56)
        fi = sb("fi", [P, 3, 2048], BF16, s56)
        ew = sb("ew", [P, 2, DC, D], F32, s5)
        ewkv = sb("ewkv", [P, 4, D], F32, s5)
        bq5 = sb("bq5", [P, D], F32, s5)
        bp5 = sb("bp5", [P, D], F32, s5)
        bv5 = sb("bv5", [P, D], F32, s5)
        bk5 = sb("bk5", [P, DC], F32, s5)
        eqf = sb("eqf", [P, 4, D], F32, s5)
        eqi = sb("eqi", [P, 4, D], BF16, s5)
        esc = sb("esc", [P, 3, 4], F32, s5)
        ediag = sb("ediag", [P, 4, P], F32, s5)
        ewb = sb("ewb", [P, 2, D], F32, s5)
        ewT = sb("ewT", [P, 2, DC, D], BF16, s5)
        wkvT = sb("wkvT", [P, DC, 512], F32, s5)
        k5T = sb("k5T", [P, DC, NT, P], F32, s5)
        v5 = sb("v5", [P, NT, D], F32, s5)
        q5, q5T = xn, xnT
        q5s = sb("q5s", [P, 2, DC, P], F32, s5)
        kx = sb("kx", [P, 2, DC, 8, P], F32, s5)
        s5m = sb("s5m", [P, 2, H4, P], F32, s5)
        n5 = sb("n5", [P, 2, H4], F32, s5)
        r5 = sb("r5", [P, 2, H4], F32, s5)
        i5 = sb("i5", [P, 2, H4], F32, s5)
        p5T = sb("p5T", [P, 2, H4, P], F32, s5)
        o5 = sb("o5", [P, 2, D], F32, s5)
        oq = sb("oq", [P, 2, D], F32, s5)
        oi = sb("oi", [P, 2, D], BF16, s5)
        osc = sb("osc", [P, 2, 3], F32, s5)
        oiT = sb("oiT", [P, 2, DC, P], BF16, s5)
        ot = sb("ot", [P, 2, D], F32, s5)
        s5.close()
        s6 = ExitStack()
        fguT = sb("fguT", [P, DC, 2, 1024], BF16, s6)
        fdT = sb("fdT", [P, 8, D], BF16, s6)
        fg = sb("fg", [P, 2, 1024], F32, s6)
        fh = sb("fh", [P, 2, 1024], F32, s6)
        fq = sb("fq", [P, 2, 1024], F32, s6)
        fhi = sb("fhi", [P, 2, 1024], BF16, s6)
        fhT = sb("fhT", [P, 2, 8, P], BF16, s6)
        s6.close()
        s56.close()

        CREDIT = 2
        W1 = slice(0, 1024)
        W3 = slice(1024, 2048)
        W2 = slice(2048, 4096)
        xs = nc.dram_tensor("sorted_rows", (ET * SLOTS, D), F32, kind="Internal").ap()
        ys = nc.dram_tensor("expert_rows", (ET * SLOTS, D), F32, kind="Internal").ap()

        def x_done(eng, s, t):
            if s == 0:
                eng.wait_ge(sem("x_loaded"), 16)
            elif s == 1:
                eng.wait_ge(sem("x1_added"), t + 1)
            elif s == 2:
                eng.wait_ge(sem("x2_added"), t // 2 + 1)
            elif s == 3:
                eng.wait_ge(sem("x3_added"), t + 1)
            else:
                eng.wait_ge(sem(f"x{s}_added"), t + 2)

        def prep4_moves():
            for k in range(2):
                yield wkT[:, 8 * k:8 * k + 8, :].rearrange("p h n -> p (h n)"), bank[k][0:64, :]
            for k in range(2):
                yield wvT[:, 8 * k:8 * k + 8, :].rearrange("p h n -> p (h n)"), bank[2 + k][:]
            for k in range(4):
                yield wqbT[:, 4 * k:4 * k + 4, 0:P], bank[4 + k][0:64, :].rearrange("p (h n) -> p h n", h=4)
            for k in range(2):
                yield wqbT[:, 8 * k:8 * k + 8, P:QL], bank[k][0:64, :].rearrange("p (h n) -> p h n", h=8)
            for k in range(2):
                yield wqb[:, 0, 8 * k:8 * k + 8, 0:64], bank[2 + k][:].rearrange("p (h n) -> p h n", h=8)
            for k in range(2):
                yield wqb[0:64, 1, 8 * k:8 * k + 8, 0:64], bank[4 + k][0:64, :].rearrange("p (h n) -> p h n", h=8)
            for k in range(4):
                yield wvo[:, 2 * k:2 * k + 2, :].rearrange("p j n -> p (j n)"), bank[(6, 7, 0, 1)[k]][:]

        block = ctx.enter_context(nc.Block())

        @block.sync
        def _(sp):
            sp.dma_start(x[:], a["x"].rearrange("b s d -> s b d")).then_inc(sem("x_loaded"), 16)
            sp.dma_start(const[:], a["consts"][:, 0:nlate]).then_inc(sem("const_loaded"), 16)
            sp.dma_start(const12[:], a["consts"][:, nlate:ncol]).then_inc(sem("const_loaded"), 16)
            for dst, name in ((wq, "L0_attn_W_q"), (wkv, "L0_attn_W_kv"), (wo, "L0_attn_W_o")):
                sp.dma_start(dst[:], a[name].rearrange("(c p) n -> p c n", p=P)).then_inc(sem("w1_loaded"), 16)
            sp.dma_start(cx[:], a["ctx_2048"].rearrange("b s d -> s b d")).then_inc(sem("s2_loaded"), 16)
            for h in range(HG):
                pad = a["kpad"]
                src = bass.AP(tensor=pad.tensor, offset=pad.offset + h * (P + D) + 1, ap=[[1, P], [1, D]])
                sp.dma_start(tapR[:, h, :], src).then_inc(sem("s2_loaded"), 16)
            with nc.allow_non_contiguous_dma(reason="one value per partition"):
                sp.dma_start(skip[:], a["fside_S2_0"].rearrange("(p o) -> p o", o=1)).then_inc(sem("s2_loaded"), 16)
            sp.dma_start(wg[:], a["L0_ffn_Wg"].rearrange("(c p) e -> p c e", p=P)).then_inc(sem("gate_loaded"), 16)
            sp.dma_start(bg[:], a["L0_ffn_bg"].partition_broadcast(P)).then_inc(sem("gate_loaded"), 16)
            sp.dma_start(b3[:], a["L0_ffn_b3"]).then_inc(sem("gate_loaded"), 16)
            for i, name in enumerate(("L0_ffn_b1", "L0_ffn_b2")):
                sp.dma_start(b12[32 * i:32 * i + 32, :], a[name].rearrange("e (c p) -> (e c) p", p=P)).then_inc(sem("gate_loaded"), 16)
            def expert_half(e, half):
                if e:
                    sp.wait_ge(sem("w_split"), 2 * e + half - 1)
                if half == 0:
                    sp.dma_start(wraw[:, 0, 0:1024].rearrange("p (c n) -> p c n", c=DC),
                                 a["L0_ffn_W1"][e].rearrange("(c p) n -> p c n", p=P)).then_inc(sem("w_loaded_even"), 16)
                    sp.dma_start(wraw[:, 0, 1024:2048].rearrange("p (c n) -> p c n", c=FC),
                                 a["L0_ffn_W3"][e].rearrange("(c p) n -> p c n", p=P)).then_inc(sem("w_loaded_even"), 16)
                else:
                    sp.dma_start(wraw[:, 1, :].rearrange("p (c n) -> p c n", c=FC),
                                 a["L0_ffn_W2"][e].rearrange("(c p) n -> p c n", p=P)).then_inc(sem("w_loaded_odd"), 16)

            sp.wait_ge(sem("zero_filled"), 32)
            for e in range(NE):
                if e == NE // 2:
                    x_done(sp, 2, NT - 1)
                for half in range(2):
                    expert_half(e, half)
            sp.dma_start(wo4a[:], a["L1_attn_Wo"][0:P * H4 // 2].rearrange("(h v) n -> v h n", v=P)).then_inc(sem("w4_loaded"), 16)
            sp.dma_start(wqa[:], a["L1_attn_Wqa"].rearrange("(c p) n -> p c n", p=P)).then_inc(sem("w4_loaded"), 16)
            sp.dma_start(wkva[:], a["L1_attn_Wkva"].rearrange("(c p) n -> p c n", p=P)).then_inc(sem("w4_loaded"), 16)
            sp.wait_ge(sem("w_split"), 2 * NE)
            sp.dma_start(wqb[:, 0].rearrange("p h n -> p (h n)"), a["L1_attn_Wqb"][0:P, :]).then_inc(sem("w4_loaded"), 16)
            sp.dma_start(wqb[0:64, 1].rearrange("p h n -> p (h n)"), a["L1_attn_Wqb"][P:QL, :]).then_inc(sem("w4_loaded"), 16)
            def rows_in(i, u):
                sp.dma_start(xg[:, u], xs[bass.ds(i * (2 * SLOTS) + SLOTS * u, SLOTS), :].rearrange("(b p) d -> p b d", p=P)).then_inc(sem(f"xg{u}_loaded"), 16)

            def rows_out(i, u):
                sp.wait_ge(sem("y_ready"), i * 2 + (u + 3))
                sp.dma_start(ys[bass.ds(i * (2 * SLOTS) + SLOTS * u, SLOTS), :].rearrange("(b p) d -> p b d", p=P), yb[:, u]).then_inc(sem(f"y{u}_stored"), 16)

            sp.wait_ge(sem("scattered"), 16 * 2 * NT)
            for j in range(2):
                rows_in(0, j)
            with sp.Fori(0, ET // 2 - 1) as i:
                for u in range(2):
                    sp.wait_ge(sem("xgT_psum"), i * 2 + (u + 1))
                    rows_in(i + 1, u)
                    rows_out(i, u)
            last = ET // 2 - 1
            sp.wait_ge(sem("xgT_psum"), ET - 2)
            rows_in(last + 1, 0)
            rows_out(last, 0)
            rows_out(last, 1)
            rows_out(last + 1, 0)
            sp.wait_ge(sem("l3_psum"), ET)
            sp.dma_start(wkvb[:].rearrange("p h n -> p (h n)"), a["L1_attn_Wkvb"]).then_inc(sem("w4_loaded"), 16)
            sp.dma_start(wo4b[:], a["L1_attn_Wo"][P * H4 // 2:].rearrange("(h v) n -> v h n", v=P)).then_inc(sem("wo4b_loaded"), 16)
            x_done(sp, 4, NT - 1)
            for i, name in enumerate(("L1_xattn_wq", "L1_xattn_wp")):
                sp.dma_start(ew[:, i], a[name].rearrange("(c p) n -> p c n", p=P)).then_inc(sem("w5_loaded"), 16)
            sp.dma_start(ewkv[:], a["L1_xattn_wkv"].rearrange("(c p) n -> p c n", p=P)).then_inc(sem("w5_loaded"), 16)
            sp.dma_start(bq5[:], a["L1_xattn_bq"].partition_broadcast(P)).then_inc(sem("w5_loaded"), 16)
            sp.dma_start(bp5[:], a["L1_xattn_bp"].partition_broadcast(P)).then_inc(sem("w5_loaded"), 16)
            sp.dma_start(bv5[:], a["L1_xattn_bkv"][D:2 * D].partition_broadcast(P)).then_inc(sem("w5_loaded"), 16)
            with nc.allow_non_contiguous_dma(reason="one value per partition"):
                sp.dma_start(bk5[:], a["L1_xattn_bkv"][0:D].rearrange("(c p) -> p c", p=P)).then_inc(sem("w5_loaded"), 16)
            for i, (name, c) in enumerate((("L1_ffn_w_gate", 8), ("L1_ffn_w_up", 8), ("L1_ffn_w_down", 2))):
                sp.dma_start(fw[:, i, :].rearrange("p (c n) -> p c n", c=c), a[name].rearrange("(c p) n -> p c n", p=P)).then_inc(sem("w6_loaded"), 16)
            with sp.Fori(0, NT) as t:
                sp.wait_ge(sem("x6_added"), t + 2)
                sp.dma_start(out[bass.ds(t, 1)].rearrange("b s d -> s (b d)"), x[:, bass.ds(t, 1), :].rearrange("p t d -> p (t d)")).then_inc(sem("stored"), 16)
            sp.wait_ge(sem("stored"), 16 * NT)

        @block.gpsimd
        def _(pool):
            zeros = wraw[:].rearrange("p h n -> p (h n)")[:, 0:ET * D].rearrange("p (b d) -> p b d", d=D)
            nc.gpsimd.memset(wraw[:], 0.0).then_inc(sem("zeroed"), 1)
            pool.wait_ge(sem("zeroed"), 1)
            pool.wait_ge(sem("w1_loaded"), 48)
            for k in range(2):
                rows = ET * P
                pool.dma_start(xs[rows * k:rows * k + rows, :].rearrange("(b p) d -> p b d", p=P), zeros).then_inc(sem("zero_filled"), 16)

            def split_low(k):
                e, half = k // 2, k % 2
                cols = slice(2048 * half, 2048 * half + 2048)
                pool.wait_ge(sem("w_hi"), k + 1)
                nc.gpsimd.tensor_tensor(wsp[:, e, 1, cols], wraw[:, half, :], wsp[:, e, 0, cols], ALU.subtract).then_inc(sem("w_split"), 1)

            for k in range(NE):
                split_low(k)
            pool.wait_ge(sem("xnT_act"), 4)
            pool.wait_ge(sem("xnT_dve"), 4)
            pool.wait_ge(sem("cxT_act"), 2)
            pool.wait_ge(sem("cxT_dve"), 2)
            for h in range(HG):
                if h >= 2:
                    pool.wait_ge(sem("conv_psum"), 2 * (h - 1))
                for c in range(DC):
                    g = slice(CH * h, CH * h + CH)
                    nc.gpsimd.tensor_tensor(
                        kvp[:, h % 2, c, :].rearrange("p (b i j) -> p b i j", b=NT, i=CH),
                        xnT[:, c, :, g].unsqueeze(3).to_broadcast([P, NT, CH, CH]),
                        cxT[:, c, :, g].unsqueeze(2).to_broadcast([P, NT, CH, CH]),
                        ALU.mult).then_inc(sem("kvp_ready"), 1)
            for k in range(NE, 2 * NE):
                split_low(k)
            pool.wait_ge(sem("zero_filled"), 32)
            pool.wait_ge(sem("route_ready"), 4)
            for t in range(NT):
                for r in range(2):
                    pool.indirect_dma_start(xs[:, :], bass.IndirectOffsetOnAxis(ap=pos[:, r, t:t + 1], axis=0), xn[:, t, :], None).then_inc(sem("scattered"), 16)
            pool.wait_ge(sem("y0_stored"), 16 * (ET // 2 + 2))
            pool.wait_ge(sem("y1_stored"), 16 * (ET // 2 + 1))
            for t in range(NT):
                for r in range(2):
                    pool.indirect_dma_start(yg[:, t, r, :], None, ys[:, :], bass.IndirectOffsetOnAxis(ap=pos[:, r, t:t + 1], axis=0)).then_inc(sem(f"gathered{t // 4}"), 16)
            own = [0]
            chain = sem("pool_own")

            def rope_q(i, u, g):
                v = qs[:, u, 4 * g:4 * g + 4, 64:128]
                pairs = v.rearrange("p h (f two) -> p h f two", two=2)
                cosb = cst["cos"].unsqueeze(1).to_broadcast([P, 4, 64])
                sinb = cst["sin"].rearrange("p (f two) -> p f two", two=2).unsqueeze(1).to_broadcast([P, 4, 32, 2])
                turned = rq[:, g % 2, 1].rearrange("p h (f two) -> p h f two", two=2)
                pool.wait_ge(sem("q4_copied"), i * 8 + (4 * u + g + 3))
                pool.sem_inc(sem("slot_claimed"), 1)
                nc.gpsimd.tensor_tensor(rq[:, g % 2, 0], v, cosb, ALU.mult).then_inc(chain, 1)
                for two in range(2):
                    nc.gpsimd.tensor_tensor(turned[:, :, :, two], pairs[:, :, :, 1 - two], sinb[:, :, :, two], ALU.mult).then_inc(chain, 1)
                pool.wait_ge(chain, i * 24 + (3 * (4 * u + g) + 3))
                nc.gpsimd.tensor_tensor(v, rq[:, g % 2, 0], rq[:, g % 2, 1], ALU.add).then_inc(sem("roped"), 1)

            with pool.Fori(0, NT // 2) as i:
                for u in range(2):
                    for g in range(4):
                        rope_q(i, u, g)
                for u in range(2):
                    for g in range(4):
                        hs = slice(4 * g, 4 * g + 4)
                        pool.wait_ge(sem("r4_ready"), i * 8 + (4 * u + g + 1))
                        nc.gpsimd.tensor_tensor(sm[:, u, hs, :], sm[:, u, hs, :],
                                                rinv[:, u, hs].unsqueeze(2).to_broadcast([P, 4, P]), ALU.mult).then_inc(sem("p4_ready"), 1)
            pool.wait_ge(sem("prep5_ready"), 6)

            def spread_keys(i, u):
                for c in range(DC):
                    pool.wait_ge(sem("s5_psum"), i * 8 + (4 * u + 4))
                    nc.gpsimd.tensor_tensor(kx[:, u, c], k5T[:, c, bass.ds(i * 2 + u, 1), :].to_broadcast([P, 8, P]),
                                            cst["head16"].unsqueeze(2).to_broadcast([P, 8, P]), ALU.mult).then_inc(sem("kx_ready"), 1)

            with pool.Fori(0, NT // 2) as i:
                for u in range(2):
                    spread_keys(i, u)
            pool.wait_ge(sem("w6_scale"), 1)
            for k in range(3):
                nc.gpsimd.tensor_scalar(fw[:, k, :], fw[:, k, :], fws[:, 3, k:k + 1], ROUND, ALU.mult, ALU.add).then_inc(sem("w6_step"), 1)
            for k in range(3):
                pool.wait_ge(sem("w6_step"), k + 1)
                nc.gpsimd.tensor_scalar(fw[:, k, :], fw[:, k, :], -ROUND, 1.0, ALU.add, ALU.min).then_inc(sem("w6_step"), 1)
            for k in range(3):
                pool.wait_ge(sem("w6_step"), k + 4)
                nc.gpsimd.tensor_scalar(fi[:, k, :], fw[:, k, :], -1.0, None, ALU.max).then_inc(sem("w6_int"), 1)


        @block.scalar
        def _(act):
            def deviation(s):
                act.wait_ge(sem("ln_var"), s)
                nc.scalar.activation(sd[:], ve[:], ACT.Sqrt).then_inc(sem("ln_sd"), 1)

            def xnT_copies(s):
                for half in range(2):
                    act.wait_ge(sem("xnT_psum"), 4 * (s - 1) + 2 * half + 1)
                    nc.scalar.copy(xnT[:, 0, 4 * half:4 * half + 4, :].rearrange("p t s -> p (t s)"), bank[2 * half][:]).then_inc(sem("xnT_act"), 1)

            def split_high(k):
                e, half = k // 2, k % 2
                act.wait_ge(sem("w_loaded_odd" if half else "w_loaded_even"), (16 if half else 32) * (e + 1))
                nc.scalar.copy(wsp[:, e, 0, 2048 * half:2048 * half + 2048], wraw[:, half, :]).then_inc(sem("w_hi"), 1)

            act.wait_ge(sem("prep1_psum"), 1)
            nc.scalar.copy(woT[:].rearrange("p c n -> p (c n)"), bank[4][:]).then_inc(sem("prep1_ready"), 1)
            for c in range(DC):
                act.wait_ge(sem("prep1_psum"), c + 2)
                nc.scalar.copy(toF[:, c, :], bank[5 + c][:]).then_inc(sem("prep1_ready"), 1)
            act.wait_ge(sem("prep1_psum"), 4)
            nc.scalar.copy(toO[:, 0:2, :].rearrange("p c n -> p (c n)"), bank[7][:]).then_inc(sem("prep1_ready"), 1)
            act.wait_ge(sem("prep1_psum"), 5)
            nc.scalar.copy(toO[:, 2, :], bank[4][:, 0:D]).then_inc(sem("prep1_ready"), 1)
            nc.scalar.copy(identb[:], cst["ident"]).then_inc(sem("prep1_ready"), 1)
            deviation(1)
            xnT_copies(1)
            for t in range(NT):
                act.wait_ge(sem("qk_psum"), t + 1)
                if t >= 2:
                    act.wait_ge(sem("ss_done"), t - 1)
                nc.scalar.activation(sq[:, t % 2, :], bank[t % 4][:], ACT.Square).then_inc(sem("sq_ready"), 1)
                nc.scalar.copy(qk[:, t, :], bank[t % 4][:]).then_inc(sem("qk_ready"), 1)
            act.wait_ge(sem("ss_done"), NT)
            nc.scalar.activation(sn[:], ss[:], ACT.Sqrt).then_inc(sem("norm_ready"), 1)
            for t in range(NT):
                act.wait_ge(sem("kq_psum"), t + 1)
                if t >= 4:
                    act.wait_ge(sem("products_ready"), t - 3)
                nc.scalar.copy(kqT[:, t % 4, :], bank[4 + t % 4][:]).then_inc(sem("kqT_ready"), 1)
            for k in range(4):
                split_high(k)
            for k in range(8):
                act.wait_ge(sem("tap_psum"), k + 1)
                nc.scalar.copy(tap[:, 2 * k:2 * k + 2, :].rearrange("p h n -> p (h n)"), bank[4 + k % 2][:]).then_inc(sem("tap_ready"), 1)
            for half in range(2):
                act.wait_ge(sem("cxT_psum"), 2 * half + 1)
                nc.scalar.copy(cxT[:, 0, 4 * half:4 * half + 4, :].rearrange("p t s -> p (t s)"), bank[6][:]).then_inc(sem("cxT_act"), 1)
            deviation(2)
            xnT_copies(2)
            for k in range(4, 8):
                split_high(k)
            act.wait_ge(sem("gate_psum"), 1)
            nc.scalar.copy(bT[:], bank[4][:, 0:64]).then_inc(sem("gate_act"), 1)
            deviation(3)
            split_high(8)
            xnT_copies(3)
            split_high(9)
            split_high(10)
            act.wait_ge(sem("route_ready"), 1)
            nc.scalar.activation(gw[:].rearrange("p t e -> p (t e)"), lg[:].rearrange("p t e -> p (t e)"), ACT.Exp).then_inc(sem("gate_act"), 1)
            split_high(11)
            split_high(12)
            for k in range(2):
                act.wait_ge(sem("gate_psum"), k + 4)
                nc.scalar.copy(combT[:, 4 * k:4 * k + 4, :].rearrange("p t s -> p (t s)"), bank[5 + k][0:NE, :]).then_inc(sem("gate_act"), 1)
            for k in range(13, 16):
                split_high(k)
            act.sem_inc(sem("h1_f32"), CREDIT)
            act.sem_inc(sem("h2_f32"), CREDIT)
            act.sem_inc(sem("y_ready"), CREDIT)
            act.sem_inc(sem("y0_stored"), 16)
            act.sem_inc(sem("y1_stored"), 16)
            act.wait_ge(sem("route_ready"), 5)
            act.wait_ge(sem("gate_act"), 1)

            def hidden(layer, i, u):
                e = act.value_load(eid[0:1, bass.ds(i * 2 + u, 1)], min_val=0, max_val=NE - 1)
                nc.scalar.copy(be[:, layer - 1, u, :], bT[:, bass.ds(e * FC + 32 * (layer - 1), FC)]).then_inc(sem("bias_ready"), 1)
                act.wait_ge(sem("bias_ready"), i * 4 + (2 * u + layer))
                for p in range(2):
                    n = i * 4 + (2 * u + p)
                    act.wait_ge(sem(f"l{layer}_psum"), n + 1)
                    act.wait_ge(sem("h2_lo" if layer == 1 else "h1_lo"), n + 1)
                    for k in range(2):
                        last = nc.scalar.activation(hf[:, p, SLOTS * k:SLOTS * k + SLOTS], bank[2 * (layer - 1) + p][:, SLOTS * k:SLOTS * k + SLOTS],
                                                    ACT.Gelu, bias=be[:, layer - 1, u, 2 * p + k:2 * p + k + 1])
                    last.then_inc(sem(f"h{layer}_f32"), 1)

            def expert_out(i, u):
                act.wait_ge(sem("l3_psum"), i * 2 + (u + 1))
                act.wait_ge(sem(f"y{u}_stored"), i * 16 + 16)
                nc.scalar.copy(yb[:, u].rearrange("p b d -> p (b d)"), bank[4 + u][:]).then_inc(sem("y_ready"), 1)

            hidden(1, 0, 0)
            with act.Fori(0, ET // 2) as i:
                for u in range(2):
                    hidden(2, i, u)
                    hidden(1, i + u, 1 - u)
                    expert_out(i, u)
            hidden(2, ET // 2, 0)
            expert_out(ET // 2, 0)
            def prep(k, dst, src):
                act.wait_ge(sem("prep4_psum"), k + 1)
                nc.scalar.copy(dst, src).then_inc(sem("prep4_act"), 1)

            for k, (dst, src) in enumerate(prep4_moves()):
                if k % 2 == 0:
                    prep(k, dst, src)
            deviation(4)
            xnT_copies(4)
            act.sem_inc(sem("q4_copied"), 2)
            act.sem_inc(sem("oT_ready"), 1)

            def latents(i, u):
                act.wait_ge(sem("lat_psum"), i * 2 + (u + 1))
                nc.scalar.copy(ql0[:, u, :], bank[0][:, 0:P])
                nc.scalar.copy(kvT[:, u, :], bank[0][:, P:2 * P])
                nc.scalar.copy(ql1[:, u, :], bank[0][0:64, 2 * P:3 * P]).then_inc(sem("lat_copied"), 1)

            def exps(i, u, g):
                act.wait_ge(sem("nm_ready"), i * 8 + (4 * u + g + 1))
                for h in range(4 * g, 4 * g + 4):
                    last = nc.scalar.activation(sm[:, u, h, :], sm[:, u, h, :], ACT.Exp, bias=nm[:, u, h:h + 1], accum_out=rsum[:, u, h:h + 1])
                last.then_inc(sem("exp_ready"), 1)

            with act.Fori(0, NT // 2) as i:
                for u in range(2):
                    latents(i, u)
                    for g in range(4):
                        act.wait_ge(sem("q4_psum"), i * 8 + (4 * u + g + 1))
                        nc.scalar.copy(qs[:, u, 4 * g:4 * g + 4, :].rearrange("p h n -> p (h n)"), bank[1 + g % 2][:]).then_inc(sem("q4_copied"), 1)
                    act.wait_ge(sem("kT_psum"), i * 2 + (u + 1))
                    nc.scalar.copy(kT[:, u, :], bank[0][:, 3 * P:4 * P]).then_inc(sem("kT_ready"), 1)
                steps = [(u, g) for u in range(2) for g in range(4)]
                for j, (u, g) in enumerate(steps):
                    act.wait_ge(sem("t4_psum"), i * 8 + (j + 1))
                    nc.scalar.copy(qT[:, u, 4 * g:4 * g + 4, :].rearrange("p h n -> p (h n)"), bank[3 + g % 2][:]).then_inc(sem("qT_ready"), 1)
                    if j >= 2:
                        exps(i, *steps[j - 2])
                exps(i, *steps[6])
                exps(i, *steps[7])
                for u in range(2):
                    for k in range(2):
                        act.wait_ge(sem("pv_psum"), i * 4 + (2 * u + k + 1))
                        nc.scalar.copy(oT[:, u, 4 * k:4 * k + 4, :].rearrange("p h n -> p (h n)"), bank[7 if k == 0 else 0][:]).then_inc(sem("oT_ready"), 1)
            deviation(5)
            for k in range(2):
                act.wait_ge(sem("prep5_psum"), k + 1)
                nc.scalar.copy(wkvT[:, k, :], bank[k][:]).then_inc(sem("prep5_ready"), 1)
            act.wait_ge(sem("w5_loaded"), 112)
            for k in range(4):
                act.wait_ge(sem("prep5_psum"), k + 3)
                nc.scalar.activation(k5T[:, k // 2, 4 * (k % 2):4 * (k % 2) + 4, :].rearrange("p t s -> p (t s)"), bank[2 + k][:], ACT.Identity,
                                     bias=bk5[:, k // 2:k // 2 + 1]).then_inc(sem("prep5_ready"), 1)
            act.wait_ge(sem("prep5_psum"), 7)
            nc.scalar.copy(ewT[:].rearrange("p w c n -> p (w c n)"), bank[6][:].bitcast(BF16)).then_inc(sem("prep5_ready"), 1)
            act.wait_ge(sem("prep5_psum"), 8)
            nc.scalar.copy(ewb[:].rearrange("p w n -> p (w n)"), bank[7][:]).then_inc(sem("prep5_ready"), 1)

            def xiT_copies(s):
                for c in range(DC):
                    act.wait_ge(sem("xiT_psum"), 2 * (s - 5) + c + 1)
                    nc.scalar.copy(xiT[:, c].rearrange("p t s -> p (t s)"), bank[c][:].bitcast(BF16)).then_inc(sem("xiT_ready"), 1)

            xiT_copies(5)
            for k in range(4):
                act.wait_ge(sem("q5T_psum"), k + 1)
                nc.scalar.copy(q5T[:, k % 2, 4 * (k // 2):4 * (k // 2) + 4, :].rearrange("p t s -> p (t s)"), bank[k][:]).then_inc(sem("q5T_ready"), 1)
            act.sem_inc(sem("exp5_ready"), 2)
            with act.Fori(0, NT // 2) as i:
                for u in range(2):
                    for g in range(4):
                        act.wait_ge(sem("n5_ready"), i * 8 + (4 * u + g + 1))
                        for k in range(4):
                            h = 4 * g + k
                            last = nc.scalar.activation(s5m[:, u, h, :], bank[5 + g % 2][:, P * k:P * k + P], ACT.Exp,
                                                        bias=n5[:, u, h:h + 1], accum_out=r5[:, u, h:h + 1])
                        last.then_inc(sem("exp5_ready"), 1)
                for u in range(2):
                    act.wait_ge(sem("oiT_psum"), i * 2 + (u + 1))
                    nc.scalar.copy(oiT[:, u].rearrange("p c s -> p (c s)"), bank[1][:, 0:P].bitcast(BF16)).then_inc(sem("oiT_ready"), 1)
            deviation(6)
            xiT_copies(6)
            for k in range(6):
                act.wait_ge(sem("w6T_psum"), k + 1)
                b16 = bank[2 + k][:].bitcast(BF16)
                if k < 4:
                    nc.scalar.copy(fguT[:, k % 2, k // 2, :], b16).then_inc(sem("w6T_ready"), 1)
                else:
                    nc.scalar.copy(fdT[:, 4 * (k - 4):4 * (k - 4) + 4, :].rearrange("p c n -> p (c n)"), b16).then_inc(sem("w6T_ready"), 1)
            act.sem_inc(sem("silu_ready"), 2)
            with act.Fori(0, NT // 2) as i:
                for u in range(2):
                    for k in range(2):
                        act.wait_ge(sem("gu_psum"), i * 2 + (u + 1))
                        nc.scalar.activation(fg[:, u, 512 * k:512 * k + 512], bank[4 * u + k][:], ACT.Silu, scale=fsn[:, u, 0:1]).then_inc(sem("silu_ready"), 1)
                for u in range(2):
                    act.wait_ge(sem("fhT_psum"), i * 2 + (u + 1))
                    nc.scalar.copy(fhT[:, u].rearrange("p c s -> p (c s)"), bank[4 * u][:].bitcast(BF16)).then_inc(sem("fhT_ready"), 1)

        @block.vector
        def _(dve):
            own = [0]

            def then(ins):
                own[0] += 1
                ins.then_inc(sem("dve_own"), 1)
                dve.wait_ge(sem("dve_own"), own[0])

            def rsqrt_refined(v, root, r, tmp):
                then(nc.vector.reciprocal(r[:, 0], root))
                then(nc.vector.tensor_tensor(tmp[:, 0], r[:, 0], r[:, 0], ALU.mult))
                then(nc.vector.tensor_tensor(tmp[:, 1], tmp[:, 0], v, ALU.mult))
                then(nc.vector.tensor_scalar(tmp[:, 0], tmp[:, 1], -0.5, 1.5, ALU.mult, ALU.add))
                then(nc.vector.tensor_tensor(r[:, 1], r[:, 0], tmp[:, 0], ALU.mult))

            def layernorm(s):
                for t in range(NT):
                    x_done(dve, s - 1, t)
                    nc.vector.bn_stats(st[:, t, :], x[:, t, :]).then_inc(sem("ln_stats"), 1)
                for t in range(NT):
                    dve.wait_ge(sem("ln_stats"), NT * (s - 1) + t + 1)
                    nc.vector.bn_aggr(mv[:, t, :], st[:, t, :]).then_inc(sem("ln_mean"), 1)
                dve.wait_ge(sem("ln_mean"), NT * s)
                nc.vector.tensor_scalar(ve[:], mv[:, :, 1], EPS, None, ALU.add).then_inc(sem("ln_var"), 1)
                dve.wait_ge(sem("ln_sd"), s)
                r2 = rs[:].rearrange("p t k -> p k t")
                rsqrt_refined(ve[:], sd[:], r2, nw)
                for t in range(NT):
                    nc.vector.tensor_scalar(xn[:, t, :], x[:, t, :], mv[:, t, 0:1], rs[:, t, 1:2], ALU.subtract, ALU.mult).then_inc(sem("xn_ready"), 1)

            def xnT_copies(s):
                for half in range(2):
                    dve.wait_ge(sem("xnT_psum"), 4 * (s - 1) + 2 * half + 2)
                    nc.vector.tensor_copy(xnT[:, 1, 4 * half:4 * half + 4, :].rearrange("p t s -> p (t s)"), bank[2 * half + 1][:]).then_inc(sem("xnT_dve"), 1)

            layernorm(1)
            xnT_copies(1)
            for t in range(NT):
                dve.wait_ge(sem("sq_ready"), t + 1)
                nc.vector.tensor_reduce(ss[:, 32 * t:32 * t + 32],
                                        sq[:, t % 2, :].rearrange("p (w a h k) -> p w h a k", w=2, a=2, k=8),
                                        AX.XY, ALU.add).then_inc(sem("ss_done"), 1)
            dve.wait_ge(sem("norm_ready"), 1)
            rsqrt_refined(ss[:], sn[:], rn, nn)
            for t in range(NT):
                dve.wait_ge(sem("qk_ready"), t + 1)
                for w in range(2):
                    v = qk[:, t, D * w:D * w + D].rearrange("p (a h k) -> p a h k", a=2, k=8)
                    r = rn[:, 1, 32 * t + 16 * w:32 * t + 16 * w + 16].unsqueeze(1).unsqueeze(3).to_broadcast([P, 2, 16, 8])
                    nc.vector.tensor_tensor(v, v, r, ALU.mult).then_inc(sem("qkn_ready"), 1)

            def add_attention(t):
                dve.wait_ge(sem("attn_psum"), t + 1)
                nc.vector.tensor_tensor(x[:, t, :], x[:, t, :], bank[t % 4][:, 0:D], ALU.add).then_inc(sem("x1_added"), 1)

            for t in range(NT):
                dve.wait_ge(sem("kqT_ready"), t + 1)
                k, w = t % 4, t % 2
                nc.vector.tensor_tensor(pr[:, w, 0:2, :].rearrange("p a s -> p (a s)"), kqT[:, k, 0:256], kqT[:, k, 256:512], ALU.mult)
                nc.vector.tensor_tensor(pr[:, w, 2, :], kqT[:, k, 0:128], kqT[:, k, 384:512], ALU.mult)
                nc.vector.tensor_tensor(pr[:, w, 3, :], kqT[:, k, 128:256], kqT[:, k, 256:384], ALU.mult).then_inc(sem("products_ready"), 1)
                if t >= 1:
                    add_attention(t - 1)
            add_attention(NT - 1)
            for half in range(2):
                dve.wait_ge(sem("cxT_psum"), 2 * half + 2)
                nc.vector.tensor_copy(cxT[:, 1, 4 * half:4 * half + 4, :].rearrange("p t s -> p (t s)"), bank[7][:]).then_inc(sem("cxT_dve"), 1)
            layernorm(2)
            dve.wait_ge(sem("s2_loaded"), 16 * (HG + 2))
            for k in range(4):
                two = slice(2 * k, 2 * k + 2)
                dve.wait_ge(sem("xn_ready"), NT + 2 * k + 2)
                nc.vector.scalar_tensor_tensor(wsk[:, two, :], xn[:, two, :], skip[:, 0:1], cx[:, two, :],
                                               ALU.mult, ALU.mult).then_inc(sem("wsk_ready"), 1)
            xnT_copies(2)
            for k in range(4):
                two = slice(2 * k, 2 * k + 2)
                dve.wait_ge(sem("skip_psum"), k + 1)
                then(nc.vector.tensor_tensor(sk2[:, k % 2, :], bank[4 + k][:], cx[:, two, :].rearrange("p t d -> p (t d)"), ALU.mult))
                xt = x[:, two, :].rearrange("p t d -> p (t d)")
                nc.vector.tensor_tensor(xt, xt, sk2[:, k % 2, :], ALU.add).then_inc(sem("skip_added"), 1)
            for h in range(HG):
                g = slice(CH * h, CH * h + CH)
                for lc in range(DC):
                    dve.wait_ge(sem("conv_psum"), 2 * h + lc + 1)
                    b = 2 * (h % 2) + lc
                    if h >= 1:
                        dve.wait_ge(sem("yT_ready"), 2 * (h - 1) + lc + 1)
                    nc.vector.tensor_tensor(yx[:, lc, :].rearrange("p (b j i) -> p b j i", b=NT, j=CH),
                                            bank[b][:].rearrange("p (b i j) -> p b j i", b=NT, i=CH),
                                            cxT[:, lc, :, g].unsqueeze(2).to_broadcast([P, NT, CH, CH]),
                                            ALU.mult).then_inc(sem("yx_ready"), 1)
                for lc in range(DC):
                    dve.wait_ge(sem("yx_ready"), 2 * h + lc + 1)
                    nc.vector.tensor_reduce(yT[:, lc, :, g], yx[:, lc, :].rearrange("p (b j i) -> p b j i", b=NT, j=CH),
                                            AX.X, ALU.add).then_inc(sem("yT_ready"), 1)
            dve.wait_ge(sem("skip_added"), 4)
            for k in range(4):
                dve.wait_ge(sem("conv_out_psum"), k + 1)
                xt = x[:, 2 * k:2 * k + 2, :].rearrange("p t d -> p (t d)")
                nc.vector.tensor_tensor(xt, xt, bank[4 + k][:], ALU.add).then_inc(sem("x2_added"), 1)
            layernorm(3)
            xnT_copies(3)
            dve.wait_ge(sem("gate_psum"), 2)
            dve.wait_ge(sem("gate_loaded"), 80)
            bg8 = bg[:].unsqueeze(1).to_broadcast([P, NT, NE])
            then(nc.vector.tensor_tensor(lg[:], bank[7][:, 0:64].rearrange("p (t e) -> p t e", e=NE), bg8, ALU.add))
            then(nc.vector.tensor_reduce(gm[:], lg[:], AX.X, ALU.max))
            nc.vector.tensor_tensor(lg[:], lg[:], gm[:].unsqueeze(2).to_broadcast([P, NT, NE]), ALU.subtract).then_inc(sem("route_ready"), 1)
            dve.wait_ge(sem("gate_act"), 2)
            then(nc.vector.tensor_reduce(gs[:, 0, :], gw[:], AX.X, ALU.add))
            then(nc.vector.reciprocal(gs[:, 1, :], gs[:, 0, :]))
            then(nc.vector.tensor_tensor(gw[:], gw[:], gs[:, 1, :].unsqueeze(2).to_broadcast([P, NT, NE]), ALU.mult))
            def burst(instructions):
                for ins in instructions:
                    own[0] += 1
                    ins.then_inc(sem("dve_own"), 1)
                dve.wait_ge(sem("dve_own"), own[0])

            burst(nc.vector.max(top[:, t, :], gw[:, t, :]) for t in range(NT))
            burst(nc.vector.max_index(topi[:, t, :], top[:, t, :], gw[:, t, :]) for t in range(NT))
            then(nc.vector.tensor_copy(topf[:], topi[:]))
            iota = cst["iota"][:, 0:NE].unsqueeze(1).to_broadcast([P, NT, NE])
            burst(nc.vector.tensor_tensor(pick[:, r], iota, topf[:, :, r:r + 1].to_broadcast([P, NT, NE]), ALU.is_equal) for r in range(2))
            nc.vector.tensor_tensor(sel[:], pick[:, 0], pick[:, 1], ALU.add).then_inc(sem("route_ready"), 1)
            burst(nc.vector.tensor_tensor(pickw[:, r], pick[:, r], top[:, :, r:r + 1].to_broadcast([P, NT, NE]), ALU.mult) for r in range(2))
            nc.vector.tensor_tensor(comb[:], pickw[:, 0], pickw[:, 1], ALU.add).then_inc(sem("route_ready"), 1)
            nc.vector.memset(pre[:, 0, :], 0.0)
            dve.wait_ge(sem("gate_psum"), 3)
            rank = bank[4][:, 0:64].rearrange("p (t e) -> p t e", e=NE)
            count = bank[4][:, 64:128].rearrange("p (t e) -> p t e", e=NE)
            then(nc.vector.tensor_copy(pre[:, 1, :], count[:, 0, :]))
            for t in range(1, NT):
                then(nc.vector.tensor_tensor(pre[:, t + 1, :], pre[:, t, :], count[:, t, :], ALU.add))
            then(nc.vector.tensor_scalar(tl[:, 0, :], pre[:, NT, :], 1.0 / SLOTS, 0.5 - 0.5 / SLOTS, ALU.mult, ALU.add))
            then(nc.vector.tensor_scalar(tl[:, 0, :], tl[:, 0, :], ROUND, None, ALU.add))
            then(nc.vector.tensor_scalar(tl[:, 0, :], tl[:, 0, :], -ROUND, None, ALU.add))
            then(nc.vector.tensor_tensor(tri[:], cst["before"].rearrange("p (e f) -> p e f", e=NE), tl[:, 0, :].unsqueeze(1).to_broadcast([P, NE, NE]), ALU.mult))
            then(nc.vector.tensor_reduce(tl[:, 1, :], tri[:], AX.X, ALU.add))
            then(nc.vector.tensor_tensor(tl[:, 2, :], tl[:, 1, :], tl[:, 0, :], ALU.subtract))
            then(nc.vector.tensor_scalar(tl[:, 2, :], tl[:, 2, :], float(SLOTS), -1.0, ALU.mult, ALU.add))
            then(nc.vector.tensor_tensor(sel[:], rank, pre[:, 0:NT, :], ALU.add))
            then(nc.vector.tensor_tensor(sel[:], sel[:], tl[:, 2, :].unsqueeze(1).to_broadcast([P, NT, NE]), ALU.add))
            burst(nc.vector.tensor_tensor(pick[:, r], pick[:, r], sel[:], ALU.mult) for r in range(2))
            burst(nc.vector.tensor_reduce(posf[:, r], pick[:, r], AX.X, ALU.add) for r in range(2))
            nc.vector.tensor_copy(pos[:], posf[:]).then_inc(sem("route_ready"), 1)
            then(nc.vector.tensor_tensor(eidg[:], cst["iota"].unsqueeze(2).to_broadcast([P, 16, NE - 1]),
                                         tl[:, 1, 0:NE - 1].unsqueeze(1).to_broadcast([P, 16, NE - 1]), ALU.is_ge))
            then(nc.vector.tensor_reduce(eidf[:], eidg[:], AX.X, ALU.add))
            nc.vector.tensor_copy(eid[:], eidf[:]).then_inc(sem("route_ready"), 1)
            for k in range(4):
                dve.wait_ge(sem("b3_psum"), k + 1)
                xt = x[:, 2 * k:2 * k + 2, :].rearrange("p t d -> p (t d)")
                nc.vector.tensor_tensor(xt, xt, bank[k][:], ALU.add).then_inc(sem("b3_added"), 1)
            dve.wait_ge(sem("b3_added"), 4)
            dve.sem_inc(sem("h2_lo"), CREDIT)
            dve.sem_inc(sem("xgT_split"), 1)

            def split_rows(i, u):
                dve.wait_ge(sem("xgT_psum"), i * 2 + (u + 1))
                nc.vector.tensor_copy(xgT[:, u, 0].rearrange("p c n -> p (c n)"), bank[6][:]).then_inc(sem("xgT_hi"), 1)
                dve.wait_ge(sem("xgT_hi"), i * 2 + (u + 1))
                nc.vector.tensor_tensor(xgT[:, u, 1].rearrange("p c n -> p (c n)"), bank[6][:], xgT[:, u, 0].rearrange("p c n -> p (c n)"),
                                        ALU.subtract).then_inc(sem("xgT_split"), 1)

            def split_hidden(layer, i, u):
                h = h1 if layer == 1 else h2
                for p in range(2):
                    n = i * 4 + (2 * u + p)
                    hi = h[:, 0, 2 * p:2 * p + 2, :].rearrange("p f n -> p (f n)")
                    dve.wait_ge(sem(f"h{layer}_f32"), n + (1 + CREDIT))
                    nc.vector.tensor_copy(hi, hf[:, p, :]).then_inc(sem("h_hi"), 1)
                    dve.wait_ge(sem("h_hi"), i * 8 + (4 * u + 2 * layer + p - 1))
                    nc.vector.tensor_tensor(h[:, 1, 2 * p:2 * p + 2, :].rearrange("p f n -> p (f n)"), hf[:, p, :], hi, ALU.subtract).then_inc(sem(f"h{layer}_lo"), 1)

            split_rows(0, 0)
            split_rows(0, 1)
            split_hidden(1, 0, 0)
            with dve.Fori(0, ET // 2 - 1) as i:
                for u in range(2):
                    split_hidden(2, i, u)
                    split_hidden(1, i + u, 1 - u)
                    split_rows(i + 1, u)
            last = ET // 2 - 1
            split_hidden(2, last, 0)
            split_hidden(1, last, 1)
            split_rows(last + 1, 0)
            split_hidden(2, last, 1)
            split_hidden(1, last + 1, 0)
            split_hidden(2, last + 1, 0)

            def add_experts():
                for t in range(NT):
                    for r in range(2):
                        dve.wait_ge(sem(f"gathered{t // 4}"), 16 * 8)
                        add = nc.vector.scalar_tensor_tensor(x[:, t, :], yg[:, t, r, :], top[:, t, r:r + 1], x[:, t, :], ALU.mult, ALU.add)
                        if r:
                            add.then_inc(sem("x3_added"), 1)
                        else:
                            then(add)

            def add_tile(i, u):
                dve.wait_ge(sem("out4_psum"), i * 2 + (u + 1))
                xt = x[:, bass.ds(i * 2 + u, 1), :].rearrange("p t d -> p (t d)")
                nc.vector.tensor_tensor(xt, xt, bank[7][:, 0:D], ALU.add).then_inc(sem("x4_added"), 1)

            def copy_p5T(i, j):
                u, g = j // 4, j % 4
                dve.wait_ge(sem("pt5_psum"), i * 8 + (j + 1))
                nc.vector.tensor_copy(p5T[:, u, 4 * g:4 * g + 4, :].rearrange("p h n -> p (h n)"), bank[3 + g % 2][:]).then_inc(sem("p5T_ready"), 1)

            def project(i, u):
                def step(n, ins):
                    ins.then_inc(sem("o5_step"), 1)
                    dve.wait_ge(sem("o5_step"), i * 18 + (7 * u + n))
                dve.wait_ge(sem("pv5_psum"), i * 2 + (u + 1))
                step(1, nc.vector.reciprocal(i5[:, u, :], r5[:, u, :]))
                step(2, nc.vector.tensor_tensor(o5[:, u, :].rearrange("p (h d) -> p h d", h=H4), bank[(7, 0)[u]][:, 0:D].rearrange("p (h d) -> p h d", h=H4),
                                                i5[:, u, :].unsqueeze(2).to_broadcast([P, H4, 16]), ALU.mult))
                step(3, nc.vector.tensor_reduce(osc[:, u, 0:1], o5[:, u, :], AX.X, ALU.max, apply_absolute_value=True))
                step(4, nc.vector.tensor_scalar(osc[:, u, 1:2], osc[:, u, 0:1], 1.0 / 127.0, 1e-8, ALU.mult, ALU.max))
                step(5, nc.vector.reciprocal(osc[:, u, 2:3], osc[:, u, 1:2]))
                step(6, nc.vector.tensor_scalar(oq[:, u, :], o5[:, u, :], osc[:, u, 2:3], ROUND, ALU.mult, ALU.add))
                step(7, nc.vector.tensor_scalar(oq[:, u, :], oq[:, u, :], -ROUND, 127.0, ALU.add, ALU.min))
                nc.vector.tensor_scalar(oi[:, u, :], oq[:, u, :], -127.0, None, ALU.max).then_inc(sem("oi_ready"), 1)

            for k, (dst, src) in enumerate(prep4_moves()):
                if k % 2:
                    dve.wait_ge(sem("prep4_psum"), k + 1)
                    nc.vector.tensor_copy(dst, src).then_inc(sem("prep4_dve"), 1)
            add_experts()
            layernorm(4)
            xnT_copies(4)
            dve.sem_inc(sem("s4_masked"), 2)
            dve.sem_inc(sem("pT_ready"), 2)
            dve.sem_inc(sem("x4_added"), 1)

            def rope_k(i, u):
                kv = bank[0][:, 3 * P:4 * P]
                pe_ = kv[:, 64:128].rearrange("p (f two) -> p f two", two=2)
                sn_ = cst["sin"].rearrange("p (f two) -> p f two", two=2)
                turned = rk[:, 1].rearrange("p (f two) -> p f two", two=2)
                dve.wait_ge(sem("kvn_psum"), i * 2 + (u + 1))
                nc.vector.tensor_copy(kvr[:, u, 0:64], kv[:, 0:64]).then_inc(sem("rk_step"), 1)
                nc.vector.tensor_tensor(rk[:, 0], kv[:, 64:128], cst["cos"], ALU.mult).then_inc(sem("rk_step"), 1)
                for two in range(2):
                    nc.vector.tensor_tensor(turned[:, :, two], pe_[:, :, 1 - two], sn_[:, :, two], ALU.mult).then_inc(sem("rk_step"), 1)
                dve.wait_ge(sem("rk_step"), i * 8 + (4 * u + 4))
                nc.vector.tensor_tensor(kvr[:, u, 64:128], rk[:, 0], rk[:, 1], ALU.add).then_inc(sem("kvr_ready"), 1)

            causal = cst["causal"].unsqueeze(1).to_broadcast([P, 4, P])
            with dve.Fori(0, NT // 2) as i:
                for u in range(2):
                    rope_k(i, u)
                steps = [(u, g) for u in range(2) for g in range(4)]

                def invert(j):
                    u, g = steps[j]
                    dve.wait_ge(sem("exp_ready"), i * 8 + (j + 1))
                    nc.vector.reciprocal(rinv[:, u, 4 * g:4 * g + 4], rsum[:, u, 4 * g:4 * g + 4]).then_inc(sem("r4_ready"), 1)

                for j, (u, g) in enumerate(steps):
                    hs = slice(4 * g, 4 * g + 4)
                    dve.wait_ge(sem("s4_psum"), i * 8 + (j + 1))
                    nc.vector.scalar_tensor_tensor(sm[:, u, hs, :], bank[5 + g % 2][:].rearrange("p (h n) -> p h n", h=4), S4, causal,
                                                   ALU.mult, ALU.add).then_inc(sem("s4_masked"), 1)
                    dve.wait_ge(sem("s4_masked"), i * 8 + (j + 3))
                    nc.vector.tensor_reduce(nm[:, u, hs], sm[:, u, hs, :], AX.X, ALU.max, negate=True).then_inc(sem("nm_ready"), 1)
                    if j >= 2:
                        invert(j - 2)
                invert(6)
                invert(7)
                for u in range(2):
                    for g in range(4):
                        dve.wait_ge(sem("pt4_psum"), i * 8 + (4 * u + g + 1))
                        nc.vector.tensor_copy(pT[:, u, 4 * g:4 * g + 4, :].rearrange("p h n -> p (h n)"), bank[3 + g % 2][:]).then_inc(sem("pT_ready"), 1)
                    if u == 1:
                        add_tile(i, 0)
                add_tile(i, 1)
            def scales(dst_scale, dst_inverse, largest, floor):
                then(nc.vector.tensor_scalar(dst_scale, largest, 1.0 / 127.0, 1e-8 if floor else EPS, ALU.mult, ALU.max if floor else ALU.add))
                then(nc.vector.reciprocal(dst_inverse, dst_scale))

            layernorm(5)

            def quantise_x(s, low):
                dve.wait_ge(sem("xn_ready"), NT * s)
                then(nc.vector.tensor_reduce(xsc[:, 0, :], xn[:], AX.X, ALU.max, apply_absolute_value=True))
                scales(xsc[:, 1, :], xsc[:, 2, :], xsc[:, 0, :], s == 5)
                for t in range(NT):
                    then(nc.vector.tensor_scalar(xn[:, t, :], xn[:, t, :], xsc[:, 2, t:t + 1], ROUND, ALU.mult, ALU.add))
                then(nc.vector.tensor_scalar(xn[:], xn[:], -ROUND, 127.0, ALU.add, ALU.min))
                nc.vector.tensor_scalar(xi[:], xn[:], low, None, ALU.max).then_inc(sem("xi_ready"), 1)

            quantise_x(5, -127.0)
            dve.wait_ge(sem("w5_loaded"), 112)
            ew4 = ew[:].rearrange("p w c n -> p (w c) n")
            then(nc.vector.tensor_reduce(esc[:, 0, :], ew4, AX.X, ALU.max, apply_absolute_value=True))
            scales(esc[:, 1, :], esc[:, 2, :], esc[:, 0, :], True)
            for k in range(4):
                then(nc.vector.tensor_scalar(ediag[:, k, :], cst["ident"], esc[:, 1, k:k + 1], None, ALU.mult))
                then(nc.vector.tensor_scalar(eqf[:, k, :], ew4[:, k, :], esc[:, 2, k:k + 1], ROUND, ALU.mult, ALU.add))
            then(nc.vector.tensor_scalar(eqf[:], eqf[:], -ROUND, 127.0, ALU.add, ALU.min))
            nc.vector.tensor_scalar(eqi[:], eqf[:], -127.0, None, ALU.max).then_inc(sem("eqi_ready"), 1)
            for k in range(4):
                dve.wait_ge(sem("v5_psum"), k + 1)
                nc.vector.tensor_tensor(v5[:, 2 * k:2 * k + 2, :], bank[k][:].rearrange("p (t n) -> p t n", t=2),
                                        bv5[:].unsqueeze(1).to_broadcast([P, 2, D]), ALU.add).then_inc(sem("v5_ready"), 1)
            dve.wait_ge(sem("prep5_ready"), 8)
            for t in range(NT):
                dve.wait_ge(sem("q5_psum"), t // 2 + 1)
                then(nc.vector.scalar_tensor_tensor(q5[:, t, :], bank[4 + t // 2][:, D * (t % 2):D * (t % 2) + D], xsc[:, 1, t:t + 1], ewb[:, 0, :],
                                                    ALU.mult, ALU.mult))
                nc.vector.tensor_tensor(q5[:, t, :], q5[:, t, :], bq5[:], ALU.add).then_inc(sem("q5_ready"), 1)
            dve.wait_ge(sem("w6_loaded"), 48)
            then(nc.vector.tensor_reduce(fws[:, 0, :], fw[:], AX.X, ALU.add, apply_absolute_value=True))
            dve.sem_inc(sem("w6_sums"), 1)
            dve.wait_ge(sem("w6_total"), 1)
            then(nc.vector.tensor_scalar(fws[:, 2, :], bank[7][:, 0:3], 1.0 / (1024 * D), EPS, ALU.mult, ALU.add))
            nc.vector.reciprocal(fws[:, 3, :], fws[:, 2, :]).then_inc(sem("w6_scale"), 1)
            dve.sem_inc(sem("p5T_ready"), 2)
            dve.sem_inc(sem("x5_added"), 1)
            dve.wait_ge(sem("q5T_ready"), 4)
            with dve.Fori(0, NT // 2) as i:
                for u in range(2):
                    dve.wait_ge(sem("x5_added"), i * 2 + 1)
                    nc.vector.tensor_copy(q5s[:, u], q5T[:, :, bass.ds(i * 2 + u, 1), :].rearrange("p c t s -> p c (t s)")).then_inc(sem("q5s_ready"), 1)
                for u in range(2):
                    for g in range(4):
                        dve.wait_ge(sem("s5_psum"), i * 8 + (4 * u + g + 9))
                        nc.vector.tensor_reduce(n5[:, u, 4 * g:4 * g + 4], bank[5 + g % 2][:].rearrange("p (h n) -> p h n", h=4), AX.X, ALU.max,
                                                negate=True).then_inc(sem("n5_ready"), 1)
                        if u or g:
                            copy_p5T(i, 4 * u + g - 1)
                copy_p5T(i, 7)
                for u in range(2):
                    project(i, u)
                for u in range(2):
                    dve.wait_ge(sem("out5_psum"), i * 2 + (u + 1))
                    nc.vector.scalar_tensor_tensor(ot[:, u, :], bank[2][:, D * u:D * u + D], osc[:, u, 1:2], ewb[:, 1, :], ALU.mult, ALU.mult).then_inc(sem("o5_step"), 1)
                    dve.wait_ge(sem("o5_step"), i * 18 + (2 * u + 15))
                    nc.vector.tensor_tensor(ot[:, u, :], ot[:, u, :], bp5[:], ALU.add).then_inc(sem("o5_step"), 1)
                    dve.wait_ge(sem("o5_step"), i * 18 + (2 * u + 16))
                    xt = x[:, bass.ds(i * 2 + u, 1), :].rearrange("p t d -> p (t d)")
                    nc.vector.tensor_tensor(xt, xt, ot[:, u, :], ALU.add).then_inc(sem("x5_added"), 1)
            layernorm(6)
            quantise_x(6, -128.0)
            for w in range(2):
                nc.vector.tensor_scalar(fsg[:, :, w], xsc[:, 1, :], fws[:, 2, w:w + 1], None, ALU.mult).then_inc(sem("fsg_ready"), 1)
            dve.sem_inc(sem("x6_added"), 1)
            with dve.Fori(0, NT // 2) as i:
                for u in range(2):
                    dve.wait_ge(sem("fsg_ready"), 2)
                    dve.wait_ge(sem("silu_ready"), i * 4 + 2)
                    nc.vector.tensor_copy(fsn[:, u, :], fsg[:, bass.ds(i * 2 + u, 1), :].rearrange("p t w -> p (t w)")).then_inc(sem("fsn_ready"), 1)
                for u in range(2):
                    def step(n, ins):
                        ins.then_inc(sem("f_step"), 1)
                        dve.wait_ge(sem("f_step"), i * 20 + (10 * u + n))
                    for k in range(2):
                        dve.wait_ge(sem("silu_ready"), i * 4 + (2 * u + k + 3))
                        step(k + 1, nc.vector.scalar_tensor_tensor(fh[:, u, 512 * k:512 * k + 512], bank[4 * u + 2 + k][:], fsn[:, u, 1:2], fg[:, u, 512 * k:512 * k + 512],
                                                                   ALU.mult, ALU.mult))
                    step(3, nc.vector.tensor_reduce(fsd[:, u, 0:1], fh[:, u, :], AX.X, ALU.max, apply_absolute_value=True))
                    step(4, nc.vector.tensor_scalar(fsd[:, u, 1:2], fsd[:, u, 0:1], 1.0 / 127.0, EPS, ALU.mult, ALU.add))
                    step(5, nc.vector.reciprocal(fsd[:, u, 2:3], fsd[:, u, 1:2]))
                    step(6, nc.vector.tensor_scalar(fsd[:, u, 3:4], fsd[:, u, 1:2], fws[:, 2, 2:3], None, ALU.mult))
                    step(7, nc.vector.tensor_scalar(fq[:, u, :], fh[:, u, :], fsd[:, u, 2:3], ROUND, ALU.mult, ALU.add))
                    step(8, nc.vector.tensor_scalar(fq[:, u, :], fq[:, u, :], -ROUND, 127.0, ALU.add, ALU.min))
                    step(9, nc.vector.tensor_scalar(fhi[:, u, :], fq[:, u, :], -128.0, None, ALU.max))
                    nc.vector.tensor_copy(fsd[:, u, 0:1], fsd[:, u, 3:4]).then_inc(sem("f_step"), 1)
                for u in range(2):
                    dve.wait_ge(sem("down_psum"), i * 2 + (u + 1))
                    xt = x[:, bass.ds(i * 2 + u, 1), :].rearrange("p t d -> p (t d)")
                    nc.vector.scalar_tensor_tensor(xt, bank[4 * u + 1][:, 0:D], fsd[:, u, 3:4], xt, ALU.mult, ALU.add).then_inc(sem("x6_added"), 1)

        @block.tensor
        def _(pe):
            ident = cst["ident"]

            def transposes(s):
                for half in range(2):
                    for c in range(DC):
                        pe.wait_ge(sem("xn_ready"), NT * (s - 1) + 4 * half + 4)
                        for k in range(4):
                            last = nc.tensor.transpose(bank[2 * half + c][:, P * k:P * k + P], xn[:, 4 * half + k, P * c:P * c + P], ident)
                        last.then_inc(sem("xnT_psum"), 1)

            def all_xnT(s):
                pe.wait_ge(sem("xnT_act"), 2 * s)
                pe.wait_ge(sem("xnT_dve"), 2 * s)

            pe.wait_ge(sem("const_loaded"), 32)
            pe.wait_ge(sem("w1_loaded"), 48)
            for oc in range(DC):
                for dc in range(DC):
                    last = nc.tensor.transpose(bank[4][:, D * oc + P * dc:D * oc + P * dc + P], wo[:, dc, P * oc:P * oc + P], ident)
            last.then_inc(sem("prep1_psum"), 1)
            for ic in range(DC):
                for w, src in enumerate((wq, wkv)):
                    for oc in range(DC):
                        last = nc.tensor.matmul(bank[5 + ic][:, D * w:D * w + D], src[:, oc, P * ic:P * ic + P],
                                                cst["fourier"][:, D * oc:D * oc + D], start=(oc == 0), stop=(oc == DC - 1))
                last.then_inc(sem("prep1_psum"), 1)
            pe.wait_ge(sem("prep1_ready"), 1)
            for part in range(3):
                dst = (bank[7][:, 0:D], bank[7][:, D:2 * D], bank[4][:, 0:D])[part]
                for oc in range(DC):
                    last = nc.tensor.matmul(dst, cst["inverse"][:, 384 * oc + P * part:384 * oc + P * part + P], woT[:, oc, :],
                                            start=(oc == 0), stop=(oc == DC - 1))
                if part:
                    last.then_inc(sem("prep1_psum"), 1)
            transposes(1)
            all_xnT(1)
            pe.wait_ge(sem("prep1_ready"), 3)
            for t in range(NT):
                if t >= 4:
                    pe.wait_ge(sem("qk_ready"), t - 3)
                for c in range(DC):
                    last = nc.tensor.matmul(bank[t % 4][:], xnT[:, c, t, :], toF[:, c, :], start=(c == 0), stop=(c == DC - 1))
                last.then_inc(sem("qk_psum"), 1)
            pe.wait_ge(sem("prep1_ready"), 5)

            def attention_out(t):
                pe.wait_ge(sem("products_ready"), t + 1)
                if t >= 4:
                    pe.wait_ge(sem("x1_added"), t - 3)
                for j in range(4):
                    last = nc.tensor.matmul(bank[t % 4][:, 0:D], pr[:, t % 2, j, :], toO[:, min(j, 2), :], start=(j == 0), stop=(j == 3))
                last.then_inc(sem("attn_psum"), 1)

            for t in range(NT):
                b = bank[4 + t % 4]
                pe.wait_ge(sem("qkn_ready"), 2 * t + 2)
                if t >= 4:
                    pe.wait_ge(sem("kqT_ready"), t - 3)
                for part in range(2):
                    nc.tensor.matmul(b[:, P * part:P * part + P], qk[:, t, D + P * part:D + P * part + P], cst["upper"], start=True, stop=True)
                for part in range(2):
                    last = nc.tensor.transpose(b[:, D + P * part:D + P * part + P], qk[:, t, P * part:P * part + P], ident)
                last.then_inc(sem("kq_psum"), 1)
                if t >= 1:
                    attention_out(t - 1)
            attention_out(NT - 1)
            pe.wait_ge(sem("kqT_ready"), NT)
            pe.wait_ge(sem("s2_loaded"), 16 * (HG + 2))
            for k in range(8):
                if k >= 2:
                    pe.wait_ge(sem("tap_ready"), k - 1)
                nc.tensor.matmul(bank[4 + k % 2][:], cst["reverse"], tapR[:, 2 * k:2 * k + 2, :].rearrange("p h n -> p (h n)"),
                                 start=True, stop=True).then_inc(sem("tap_psum"), 1)
            for half in range(2):
                for c in range(DC):
                    if half:
                        pe.wait_ge(sem("cxT_act" if c == 0 else "cxT_dve"), 1)
                    for k in range(4):
                        last = nc.tensor.transpose(bank[6 + c][:, P * k:P * k + P], cx[:, 4 * half + k, P * c:P * c + P], ident)
                    last.then_inc(sem("cxT_psum"), 1)
            transposes(2)
            pe.wait_ge(sem("tap_ready"), 8)
            pe.wait_ge(sem("cxT_act"), 2)
            pe.wait_ge(sem("cxT_dve"), 2)
            for k in range(4):
                pe.wait_ge(sem("wsk_ready"), k + 1)
                nc.tensor.matmul(bank[4 + k][:], cst["group8"], wsk[:, 2 * k:2 * k + 2, :].rearrange("p t d -> p (t d)"),
                                 start=True, stop=True).then_inc(sem("skip_psum"), 1)
            all_xnT(2)
            for h in range(HG):
                pe.wait_ge(sem("kvp_ready"), 2 * h + 2)
                if h >= 2:
                    pe.wait_ge(sem("yx_ready"), 2 * (h - 1))
                nc.tensor.matmul(bank[2 * (h % 2)][:], tap[:, h, 0:P], kvp[:, h % 2, 0, :], start=True, stop=True).then_inc(sem("conv_psum"), 1)
                nc.tensor.matmul(bank[2 * (h % 2) + 1][:], tap[:, h, P:2 * P], kvp[:, h % 2, 0, :], start=True, stop=False)
                nc.tensor.matmul(bank[2 * (h % 2) + 1][:], tap[:, h, 0:P], kvp[:, h % 2, 1, :], start=False, stop=True).then_inc(sem("conv_psum"), 1)
            pe.wait_ge(sem("yT_ready"), 2 * HG)
            pe.wait_ge(sem("skip_added"), 4)
            for k in range(4):
                for tt in range(2):
                    for c in range(DC):
                        last = nc.tensor.transpose(bank[4 + k][:, D * tt + P * c:D * tt + P * c + P], yT[:, c, 2 * k + tt, :], ident)
                last.then_inc(sem("conv_out_psum"), 1)
            pe.wait_ge(sem("gate_loaded"), 80)
            pe.wait_ge(sem("x2_added"), 4)
            nc.tensor.transpose(bank[4][:, 0:64], b12[:, :], ident[0:64, 0:64]).then_inc(sem("gate_psum"), 1)
            transposes(3)
            all_xnT(3)
            for t in range(NT):
                for c in range(DC):
                    last = nc.tensor.matmul(bank[7][:, NE * t:NE * t + NE], xnT[:, c, t, :], wg[:, c, :], start=(c == 0), stop=(c == DC - 1))
            last.then_inc(sem("gate_psum"), 1)
            pe.wait_ge(sem("route_ready"), 2)
            pe.wait_ge(sem("gate_act"), 1)
            for k, m in enumerate(("upper", "ones")):
                last = nc.tensor.matmul(bank[4][:, 64 * k:64 * k + 64], cst[m], sel[:].rearrange("p t e -> p (t e)"), start=True, stop=True)
            last.then_inc(sem("gate_psum"), 1)
            pe.wait_ge(sem("route_ready"), 3)
            for t in range(NT):
                last = nc.tensor.transpose(bank[5 + t // 4][0:NE, P * (t % 4):P * (t % 4) + P], comb[:, t, :], ident)
                if t % 4 == 3:
                    last.then_inc(sem("gate_psum"), 1)
            pe.wait_ge(sem("gate_act"), 4)
            for t in range(NT):
                last = nc.tensor.matmul(bank[t // 2][:, D * (t % 2):D * (t % 2) + D], combT[:, t, :], b3[:, :], start=True, stop=True)
                if t % 2:
                    last.then_inc(sem("b3_psum"), 1)
            pe.wait_ge(sem("b3_added"), 4)
            pe.wait_ge(sem("route_ready"), 5)

            def turn_rows(i, u):
                pe.wait_ge(sem(f"xg{u}_loaded"), i * 16 + 16)
                pe.wait_ge(sem("xgT_split"), i * 2 + (u + 1))
                for c in range(DC):
                    for b in range(2):
                        last = nc.tensor.transpose(bank[6][:, SLOTS * c + P * b:SLOTS * c + P * b + P], xg[:, u, b, P * c:P * c + P], ident)
                last.then_inc(sem("xgT_psum"), 1)

            def expert_weights(e, cols, chunks):
                return [wsp[:, bass.ds(e, 1), part, cols].rearrange("p e (c n) -> p (e c) n", c=chunks) for part in range(2)]

            passes = ((0, 0), (0, 1), (1, 0))

            def layer(n_layer, i, u, e):
                chunks, cols, inp = ((DC, W1, xgT[:, u]), (FC, W2, h1))[n_layer - 1]
                w = expert_weights(e, cols, chunks)
                for p in range(2):
                    n = i * 4 + (2 * u + p)
                    b = bank[2 * (n_layer - 1) + p]
                    pe.wait_ge(sem(f"h{n_layer}_f32"), n + 1)
                    for f in range(2 * p, 2 * p + 2):
                        for c in range(chunks):
                            if n_layer == 1:
                                pe.wait_ge(sem("xgT_split"), i * 2 + (u + 2))
                            elif f == 0:
                                pe.wait_ge(sem("h1_lo"), i * 4 + (2 * u + c // 2 + 1))
                            for a_, b_ in passes:
                                last = nc.tensor.matmul(b[:, SLOTS * (f % 2):SLOTS * (f % 2) + SLOTS], w[a_][:, c, P * f:P * f + P], inp[:, b_, c, :],
                                                        start=(c == 0 and a_ + b_ == 0), stop=(c == chunks - 1 and a_ == 1))
                    last.then_inc(sem(f"l{n_layer}_psum"), 1)

            def layer3(i, u, e):
                w = expert_weights(e, W3, FC)
                pe.wait_ge(sem("y_ready"), i * 2 + (u + 1))
                for b in range(2):
                    for c in range(FC):
                        if b == 0:
                            pe.wait_ge(sem("h2_lo"), i * 4 + (2 * u + c // 2 + 1 + CREDIT))
                        for a_, b_ in passes:
                            last = nc.tensor.matmul(bank[4 + u][:, D * b:D * b + D], h2[:, b_, c, P * b:P * b + P], w[a_][:, c, :],
                                                    start=(c == 0 and a_ + b_ == 0), stop=(c == FC - 1 and a_ == 1))
                last.then_inc(sem("l3_psum"), 1)

            def expert_of(i, u):
                return pe.value_load(eid[0:1, bass.ds(i * 2 + u, 1)], min_val=0, max_val=NE - 1)

            turn_rows(0, 0)
            turn_rows(0, 1)
            pe.wait_ge(sem("w_split"), 2 * NE)
            layer(1, 0, 0, expert_of(0, 0))
            with pe.Fori(0, ET // 2 - 1) as i:
                for u in range(2):
                    e, e_next = expert_of(i, u), expert_of(i + u, 1 - u)
                    layer(2, i, u, e)
                    layer(1, i + u, 1 - u, e_next)
                    layer3(i, u, e)
                    turn_rows(i + 1, u)
            for j in range(ET - 3, ET):
                i, u = j // 2, j % 2
                e = expert_of(i, u)
                layer(2, i, u, e)
                if j + 1 < ET:
                    layer(1, i + u, 1 - u, expert_of(i + u, 1 - u))
                layer3(i, u, e)
                if j + 2 < ET:
                    turn_rows(i + 1, u)
            pe.wait_ge(sem("y_ready"), ET + CREDIT)
            pe.wait_ge(sem("w4_loaded"), 96)

            def prep_copied(n):
                pe.wait_ge(sem("prep4_act"), (n + 1) // 2)
                pe.wait_ge(sem("prep4_dve"), n // 2)

            i64 = ident[0:64, 0:64]
            for k in range(2):
                for j in range(8):
                    last = nc.tensor.transpose(bank[k][0:64, 64 * j:64 * j + 64], wkvb[:, 8 * k + j, 0:64], i64)
                last.then_inc(sem("prep4_psum"), 1)
            for k in range(2):
                for j in range(8):
                    last = nc.tensor.transpose(bank[2 + k][:, 64 * j:64 * j + 64], wkvb[:, 8 * k + j, 64:192], i64)
                last.then_inc(sem("prep4_psum"), 1)
            for k in range(4):
                for j in range(4):
                    last = nc.tensor.transpose(bank[4 + k][0:64, P * j:P * j + P], wqb[:, 0, 4 * k + j, 0:64], ident)
                last.then_inc(sem("prep4_psum"), 1)
            prep_copied(2)
            for k in range(2):
                for j in range(8):
                    last = nc.tensor.transpose(bank[k][0:64, 64 * j:64 * j + 64], wqb[0:64, 1, 8 * k + j, 0:64], i64)
                last.then_inc(sem("prep4_psum"), 1)
            prep_copied(10)
            for lo, hi, at in ((0, P, 2), (P, QL, 4)):
                for k in range(2):
                    for j in range(8):
                        h = 8 * k + j
                        last = nc.tensor.matmul(bank[at + k][0:hi - lo, 64 * j:64 * j + 64], wqbT[:, h, lo:hi], wkT[:, h, :], start=True, stop=True)
                    last.then_inc(sem("prep4_psum"), 1)
            pe.wait_ge(sem("wo4b_loaded"), 16)
            for k in range(4):
                for j in range(2):
                    for odd in range(2):
                        h = 4 * k + 2 * j + odd
                        last = nc.tensor.matmul(bank[(6, 7, 0, 1)[k]][64 * odd:64 * odd + 64, D * j:D * j + D], wvT[:, h, :], (wo4a, wo4b)[h // 8][:, h % 8, :], start=True, stop=True)
                last.then_inc(sem("prep4_psum"), 1)
            prep_copied(18)
            transposes(4)
            all_xnT(4)

            def latents(i, u):
                t = bass.ds(i * 2 + u, 1)
                if u == 0:
                    pe.wait_ge(sem("oT_ready"), i * 4 + 1)
                else:
                    pe.wait_ge(sem("kT_ready"), i * 2 + 1)
                for dst, w in ((bank[0][:, 0:P], wqa[:, :, 0:P]), (bank[0][:, P:2 * P], wkva[:]), (bank[0][0:64, 2 * P:3 * P], wqa[:, :, P:QL])):
                    for c in range(DC):
                        last = nc.tensor.matmul(dst, w[:, c, :], xnT[:, c, t, :].rearrange("p t s -> p (t s)"), start=(c == 0), stop=(c == DC - 1))
                last.then_inc(sem("lat_psum"), 1)
                pe.wait_ge(sem("lat_copied"), i * 2 + (u + 1))
                nc.tensor.transpose(bank[0][:, 3 * P:4 * P], kvT[:, u, :], ident).then_inc(sem("kvn_psum"), 1)

            def queries(i, u):
                for g in range(4):
                    hs = slice(4 * g, 4 * g + 4)
                    pe.wait_ge(sem("q4_copied"), i * 8 + (4 * u + g + 1))
                    nc.tensor.matmul(bank[1 + g % 2][:], ql0[:, u, :], wqb[:, 0, hs, :].rearrange("p h n -> p (h n)"), start=True, stop=False)
                    nc.tensor.matmul(bank[1 + g % 2][:], ql1[:, u, :], wqb[0:64, 1, hs, :].rearrange("p h n -> p (h n)"), start=False, stop=True).then_inc(sem("q4_psum"), 1)
                pe.wait_ge(sem("kvr_ready"), i * 2 + (u + 1))
                nc.tensor.transpose(bank[0][:, 3 * P:4 * P], kvr[:, u, :], ident).then_inc(sem("kT_psum"), 1)

            def turn_q(i, u, g):
                pe.wait_ge(sem("roped"), i * 8 + (4 * u + g + 1))
                if g < 2 and u == 0:
                    pe.wait_ge(sem("pT_ready"), i * 8 + (g + 1))
                else:
                    pe.wait_ge(sem("qT_ready"), i * 8 + (4 * u + g - 1))
                for k in range(4):
                    last = nc.tensor.transpose(bank[3 + g % 2][:, P * k:P * k + P], qs[:, u, 4 * g + k, :], ident)
                last.then_inc(sem("t4_psum"), 1)

            def scores(i, u, g):
                pe.wait_ge(sem("qT_ready"), i * 8 + (4 * u + g + 1))
                pe.wait_ge(sem("kT_ready"), i * 2 + (u + 1))
                pe.wait_ge(sem("s4_masked"), i * 8 + (4 * u + g + 1))
                for k in range(4):
                    last = nc.tensor.matmul(bank[5 + g % 2][:, P * k:P * k + P], qT[:, u, 4 * g + k, :], kT[:, u, :], start=True, stop=True)
                last.then_inc(sem("s4_psum"), 1)

            def turn_p(i, u, g):
                pe.wait_ge(sem("p4_ready"), i * 8 + (4 * u + g + 1))
                if g < 2 and u == 0:
                    pe.wait_ge(sem("qT_ready"), i * 8 + 8)
                else:
                    pe.wait_ge(sem("pT_ready"), i * 8 + (4 * u + g + 1))
                for k in range(4):
                    last = nc.tensor.transpose(bank[3 + g % 2][:, P * k:P * k + P], sm[:, u, 4 * g + k, :], ident)
                last.then_inc(sem("pt4_psum"), 1)

            def values(i, u):
                pe.wait_ge(sem("x4_added"), i * 2 + (u + 1))
                pe.wait_ge(sem("kT_ready"), i * 2 + 2)
                pe.wait_ge(sem("oT_ready"), i * 4 + (2 * u + 1))
                pe.wait_ge(sem("pT_ready"), i * 8 + (4 * u + 6))
                pairs = pT[:, u].rearrange("p (j odd) s -> p odd j s", odd=2)
                for k in range(2):
                    for odd in range(2):
                        last = nc.tensor.matmul(bank[7 if k == 0 else 0][64 * odd:64 * odd + 64, :], kvr[:, u, 0:64], pairs[:, odd, 4 * k:4 * k + 4, :], start=True, stop=True)
                    last.then_inc(sem("pv_psum"), 1)

            def output(i, u):
                pe.wait_ge(sem("oT_ready"), i * 4 + (2 * u + 3))
                for j in range(H4 // 2):
                    last = nc.tensor.matmul(bank[7][:, 0:D], oT[:, u, j, :], wvo[:, j, :], start=(j == 0), stop=(j == H4 // 2 - 1))
                last.then_inc(sem("out4_psum"), 1)

            with pe.Fori(0, NT // 2) as i:
                for u in range(2):
                    latents(i, u)
                    queries(i, u)
                steps = [(u, g) for u in range(2) for g in range(4)]
                for j, (u, g) in enumerate(steps):
                    turn_q(i, u, g)
                    if j >= 1:
                        scores(i, *steps[j - 1])
                scores(i, *steps[7])
                for g in range(4):
                    turn_p(i, 0, g)
                values(i, 0)
                for g in range(4):
                    turn_p(i, 1, g)
                output(i, 0)
                values(i, 1)
                output(i, 1)
            x_done(pe, 4, NT - 1)
            pe.wait_ge(sem("w5_loaded"), 112)
            for ic in range(DC):
                for oc in range(4):
                    last = nc.tensor.transpose(bank[ic][:, P * oc:P * oc + P], ewkv[:, oc, P * ic:P * ic + P], ident)
                last.then_inc(sem("prep5_psum"), 1)
            pe.wait_ge(sem("prep5_ready"), 2)
            for oc in range(DC):
                for half in range(2):
                    for ic in range(DC):
                        last = nc.tensor.matmul(bank[2 + 2 * oc + half][:], wkvT[:, ic, P * oc:P * oc + P],
                                                cxT[:, ic, 4 * half:4 * half + 4, :].rearrange("p t s -> p (t s)"), start=(ic == 0), stop=(ic == DC - 1))
                    last.then_inc(sem("prep5_psum"), 1)
            pe.wait_ge(sem("prep1_ready"), 6)

            def turn_x(s):
                pe.wait_ge(sem("xi_ready"), s - 4)
                for c in range(DC):
                    b16 = bank[c][:].bitcast(BF16)
                    for t in range(NT):
                        last = nc.tensor.transpose(b16[:, P * t:P * t + P], xi[:, t, P * c:P * c + P], identb[:])
                    last.then_inc(sem("xiT_psum"), 1)

            turn_x(5)
            pe.wait_ge(sem("eqi_ready"), 1)
            b16 = bank[6][:].bitcast(BF16)
            for w in range(2):
                for ic in range(DC):
                    for oc in range(DC):
                        at = 512 * w + D * ic + P * oc
                        last = nc.tensor.transpose(b16[:, at:at + P], eqi[:, 2 * w + oc, P * ic:P * ic + P], identb[:])
            last.then_inc(sem("prep5_psum"), 1)
            nc.tensor.matmul(bank[7][:], cst["ones"], ediag[:].rearrange("p k n -> p (k n)"), start=True, stop=True).then_inc(sem("prep5_psum"), 1)
            pe.wait_ge(sem("xiT_ready"), 2)
            pe.wait_ge(sem("prep5_ready"), 6)
            for t in range(NT):
                for ic in range(DC):
                    last = nc.tensor.matmul(bank[t // 2][:, D * (t % 2):D * (t % 2) + D], cxT[:, ic, t, :], wkvT[:, ic, D:2 * D], start=(ic == 0), stop=(ic == DC - 1))
                if t % 2:
                    last.then_inc(sem("v5_psum"), 1)
            pe.wait_ge(sem("prep5_ready"), 7)
            pe.wait_ge(sem("prep5_ready"), 8)
            for t in range(NT):
                for ic in range(DC):
                    last = nc.tensor.matmul(bank[4 + t // 2][:, D * (t % 2):D * (t % 2) + D], xiT[:, ic, t, :], ewT[:, 0, ic, :], start=(ic == 0), stop=(ic == DC - 1))
                if t % 2:
                    last.then_inc(sem("q5_psum"), 1)
            pe.wait_ge(sem("v5_ready"), 4)
            for half in range(2):
                for c in range(DC):
                    pe.wait_ge(sem("q5_ready"), 4 * half + 4)
                    for k in range(4):
                        last = nc.tensor.transpose(bank[2 * half + c][:, P * k:P * k + P], q5[:, 4 * half + k, P * c:P * c + P], ident)
                    last.then_inc(sem("q5T_psum"), 1)
            pe.wait_ge(sem("w6_sums"), 1)
            pe.wait_ge(sem("q5_ready"), NT)
            nc.tensor.matmul(bank[7][:, 0:3], cst["ones"], fws[:, 0, :], start=True, stop=True).then_inc(sem("w6_total"), 1)
            pe.wait_ge(sem("w6_scale"), 1)
            pe.wait_ge(sem("q5T_ready"), 4)
            pe.sem_inc(sem("s5_psum"), 8)

            def scores5(i, u, g):
                pe.wait_ge(sem("kx_ready"), i * 4 + (2 * u + g // 2 + 1))
                pe.wait_ge(sem("q5s_ready"), i * 2 + (u + 1))
                pe.wait_ge(sem("exp5_ready"), i * 8 + (4 * u + g + 1))
                nc.tensor.matmul(bank[5 + g % 2][:], q5s[:, u, g // 2, :], kx[:, u, g // 2, 4 * (g % 2):4 * (g % 2) + 4, :].rearrange("p h s -> p (h s)"),
                                 start=True, stop=True).then_inc(sem("s5_psum"), 1)

            def turn_p5(i, u, g):
                pe.wait_ge(sem("exp5_ready"), i * 8 + (4 * u + g + 3))
                pe.wait_ge(sem("p5T_ready"), i * 8 + (4 * u + g + 1))
                for k in range(4):
                    last = nc.tensor.transpose(bank[3 + g % 2][:, P * k:P * k + P], s5m[:, u, 4 * g + k, :], ident)
                last.then_inc(sem("pt5_psum"), 1)

            def values5(i, u):
                pe.wait_ge(sem("p5T_ready"), i * 8 + (4 * u + 6))
                for h in range(H4):
                    last = nc.tensor.matmul(bank[(7, 0)[u]][:, 16 * h:16 * h + 16], p5T[:, u, h, :],
                                            v5[:, bass.ds(i * 2 + u, 1), 16 * h:16 * h + 16].rearrange("p t d -> p (t d)"), start=True, stop=True)
                last.then_inc(sem("pv5_psum"), 1)

            with pe.Fori(0, NT // 2) as i:
                steps = [(u, g) for u in range(2) for g in range(4)]
                for j, (u, g) in enumerate(steps):
                    scores5(i, u, g)
                    if j >= 1:
                        turn_p5(i, *steps[j - 1])
                turn_p5(i, *steps[7])
                for u in range(2):
                    values5(i, u)
                for u in range(2):
                    pe.wait_ge(sem("oi_ready"), i * 2 + (u + 1))
                    if u == 1:
                        pe.wait_ge(sem("oiT_ready"), i * 2 + 1)
                    for c in range(DC):
                        last = nc.tensor.transpose(bank[1][:, 0:P].bitcast(BF16)[:, P * c:P * c + P], oi[:, u, P * c:P * c + P], identb[:])
                    last.then_inc(sem("oiT_psum"), 1)
                for u in range(2):
                    pe.wait_ge(sem("oiT_ready"), i * 2 + (u + 1))
                    pe.wait_ge(sem("x5_added"), i * 2 + (u + 1))
                    for c in range(DC):
                        last = nc.tensor.matmul(bank[2][:, D * u:D * u + D], oiT[:, u, c, :], ewT[:, 1, c, :], start=(c == 0), stop=(c == DC - 1))
                    last.then_inc(sem("out5_psum"), 1)
            x_done(pe, 5, NT - 1)
            turn_x(6)
            pe.wait_ge(sem("w6_int"), 3)
            for w in range(2):
                for ic in range(DC):
                    b16 = bank[2 + 2 * w + ic][:].bitcast(BF16)
                    for oc in range(8):
                        last = nc.tensor.transpose(b16[:, P * oc:P * oc + P], fi[:, w, D * oc + P * ic:D * oc + P * ic + P], identb[:])
                    last.then_inc(sem("w6T_psum"), 1)
            for q in range(2):
                b16 = bank[6 + q][:].bitcast(BF16)
                for k in range(4):
                    for oc in range(DC):
                        last = nc.tensor.transpose(b16[:, D * k + P * oc:D * k + P * oc + P], fi[:, 2, 1024 * oc + P * (4 * q + k):1024 * oc + P * (4 * q + k) + P], identb[:])
                last.then_inc(sem("w6T_psum"), 1)
            pe.wait_ge(sem("w6T_ready"), 6)
            pe.wait_ge(sem("xiT_ready"), 4)
            with pe.Fori(0, NT // 2) as i:
                for u in range(2):
                    pe.wait_ge(sem("fsn_ready"), i * 2 + (u + 1))
                    pe.wait_ge(sem("x6_added"), i * 2 + 1)
                    for k in range(4):
                        for ic in range(DC):
                            last = nc.tensor.matmul(bank[4 * u + k][:], xiT[:, ic, bass.ds(i * 2 + u, 1), :].rearrange("p t s -> p (t s)"),
                                                    fguT[:, ic, k // 2, 512 * (k % 2):512 * (k % 2) + 512], start=(ic == 0), stop=(ic == DC - 1))
                    last.then_inc(sem("gu_psum"), 1)
                for u in range(2):
                    pe.wait_ge(sem("f_step"), i * 20 + (10 * u + 10))
                    b16 = bank[4 * u][:].bitcast(BF16)
                    for c in range(8):
                        last = nc.tensor.transpose(b16[:, P * c:P * c + P], fhi[:, u, P * c:P * c + P], identb[:])
                    last.then_inc(sem("fhT_psum"), 1)
                for u in range(2):
                    pe.wait_ge(sem("fhT_ready"), i * 2 + (u + 1))
                    for c in range(8):
                        last = nc.tensor.matmul(bank[4 * u + 1][:, 0:D], fhT[:, u, c, :], fdT[:, c, :], start=(c == 0), stop=(c == 7))
                    last.then_inc(sem("down_psum"), 1)
    return nc


_INS = ['x', 'fside_S2_0', 'ctx_2048', 'L0_attn_W_q', 'L0_attn_W_kv', 'L0_attn_W_o', 'L0_ffn_W1', 'L0_ffn_b1',
        'L0_ffn_W2', 'L0_ffn_b2', 'L0_ffn_W3', 'L0_ffn_b3', 'L0_ffn_Wg', 'L0_ffn_bg',
        'L1_attn_Wqa', 'L1_attn_Wqb', 'L1_attn_Wkva', 'L1_attn_Wkvb', 'L1_attn_Wo', 'L1_xattn_wq', 'L1_xattn_bq',
        'L1_xattn_wkv', 'L1_xattn_bkv', 'L1_xattn_wp', 'L1_xattn_bp', 'L1_ffn_w_gate', 'L1_ffn_w_up', 'L1_ffn_w_down']


def kernel(**inputs):
    import concourse.bacc as _bacc
    from concourse import mybir as _mybir
    from concourse.bass_utils import run_bass_kernel_spmd as _run

    nc = _bacc.Bacc("TRN2", target_bir_lowering=False, num_devices=1)
    host = {name: np.ascontiguousarray(inputs[name]) for name in _INS}
    taps = inputs["L0_xattn_k"]
    kpad = np.zeros((taps.shape[0], P + D), np.float32)
    kpad[:, P:] = taps
    host["kpad"] = kpad
    host["consts"] = shape_constants()[0]
    arrays, args = {}, {}
    for name, v in host.items():
        arrays[f"in_{name}"] = v
        args[name] = nc.dram_tensor(f"in_{name}", v.shape, _mybir.dt.from_np(v.dtype), kind="ExternalInput").ap()
    out = nc.dram_tensor("out_0", (NT, P, D), F32, kind="ExternalOutput").ap()
    decoder_kernel(nc, args, out)
    r = _run(nc, [arrays], core_ids=[0])
    return r.results[0]["out_0"]
```

```python
from contextlib import ExitStack

import numpy as np

import concourse.bass as bass
from concourse import mybir

P = 128
NT = 8
D = 256
DC = D // P
NE = 8
FH = 512
FC = FH // P
CH = 8
HG = P // CH
SCALED_BY_VECTOR = 5
POOL_HALVES = 4
H4 = 16
QL = 192
S4 = float(np.float32(P) ** np.float32(-0.5))
SLOTS = 2 * P
ET = 2 * NT * P // SLOTS + NE - 1
ROUND = 12582912.0
EPS = 1e-5

ALU = mybir.AluOpType
ACT = mybir.ActivationFunctionType
AX = mybir.AxisListType
F32 = mybir.dt.float32
F16 = mybir.dt.float16
BF16 = mybir.dt.bfloat16
I32 = mybir.dt.int32
U32 = mybir.dt.uint32


EARLY = ("fourier", "inverse", "reverse", "group8")


def shape_constants():
    n = np.arange(16)
    parts = {}
    parts["ident"] = np.eye(P)
    parts["upper"] = np.triu(np.ones((P, P)))
    parts["reverse"] = np.eye(P)[::-1]
    parts["group8"] = np.kron(np.eye(HG), np.ones((CH, CH)))
    parts["ones"] = np.ones((P, P))
    f = np.zeros((D, 2, 16, 8))
    c = np.zeros((3, 16, 8, D))
    for h in range(16):
        for k in range(8):
            s = slice(16 * h, 16 * h + 16)
            co, si = np.cos(2 * np.pi * k * n / 16), np.sin(2 * np.pi * k * n / 16)
            f[s, 0, h, k] = 0.25 if k == 0 else co * np.sqrt(2) / 4
            f[s, 1, h, k] = 0.25 * (-1.0) ** n if k == 0 else si * np.sqrt(2) / 4
            c[0, h, k, s] = co / 16
            c[1, h, k, s] = (-1.0) ** n / 16 if k == 0 else -co / 16
            c[2, h, k, s] = si / 16
    f = f.reshape(D, D)
    parts["fourier"] = np.concatenate([f[:P], f[P:]], 1)
    ct = c.reshape(3 * P, D).T
    parts["inverse"] = np.concatenate([ct[:P], ct[P:]], 1)
    inv = 1.0 / 10000.0 ** (np.arange(32, dtype=np.float32) * np.float32(2.0) / np.float32(64))
    ang = (np.arange(P, dtype=np.float32)[:, None] * inv.astype(np.float32)[None, :]).astype(np.float32)
    parts["cos"] = np.repeat(np.cos(ang), 2, axis=1)
    parts["sin"] = np.stack([-np.sin(ang), np.sin(ang)], axis=2).reshape(P, 64)
    parts["causal"] = np.where(np.tril(np.ones((P, P))) > 0, 0.0, -1e30)
    parts["head16"] = np.kron(np.eye(8), np.ones((16, 1))) * 0.25
    parts["iota"] = np.tile(np.arange(16.0), (P, 1))
    parts["before"] = np.tile(np.tril(np.ones((NE, NE))).reshape(1, -1), (P, 1))
    at, cols = {}, 0
    parts = {name: parts[name] for name in sorted(parts, key=lambda name: name in EARLY)}
    for name, a in parts.items():
        at[name] = (cols, cols + a.shape[1])
        cols += a.shape[1]
    return np.concatenate(list(parts.values()), 1).astype(np.float32), at


CONST_AT = shape_constants()[1]


def decoder_kernel(nc, a, out):
    with ExitStack() as ctx:
        named = {}

        def sem(name):
            if name not in named:
                named[name] = ctx.enter_context(nc.semaphore(name))
            return named[name]

        def sb(name, shape, dt=F32, scope=ctx):
            return scope.enter_context(nc.sbuf_tensor(name, shape, dt))

        bank = [ctx.enter_context(nc.psum_tensor(f"bank{k}", [P, 512], F32)) for k in range(8)]

        ncol = max(hi for _, hi in CONST_AT.values())
        nlate = min(CONST_AT[name][0] for name in EARLY)
        const = sb("const", [P, nlate])
        cst = {name: const[:, lo:hi] for name, (lo, hi) in CONST_AT.items() if name not in EARLY}
        x = sb("x", [P, NT, D])
        s2c = ExitStack()
        cx = sb("cx", [P, NT, D], F32, s2c)
        s2c.close()
        wo4a = sb("wo4a", [P, H4 // 2, D])
        cxT = sb("cxT", [P, DC, NT, P])
        st = sb("st", [P, NT, 6])
        mv = sb("mv", [P, NT, 2])
        ve = sb("ve", [P, NT])
        sd = sb("sd", [P, NT])
        unread = sb("unread", [1, 1])
        rs = sb("rs", [P, NT, 2])
        nw = sb("nw", [P, 2, NT])

        b12 = sb("b12", [2 * NE * FC, P], F32)
        identb = sb("identb", [P, P], BF16)
        xsc = sb("xsc", [P, 3, NT])
        fws = sb("fws", [P, 4, 3])
        fsg = sb("fsg", [P, NT, 2])
        fsn = sb("fsn", [P, 2, 2])
        fsd = sb("fsd", [P, 2, 4])
        be = sb("be", [P, 2, 2, FC])
        bT = sb("bT", [P, 2 * NE * FC], F32)
        b3 = sb("b3", [NE, D], F32)
        wg = sb("wg", [P, DC, NE], F32)
        bg = sb("bg", [P, NE], F32)
        lg = sb("lg", [P, NT, NE], F32)
        gm = sb("gm", [P, NT], F32)
        gs = sb("gs", [P, 2, NT], F32)
        gw = sb("gw", [P, NT, NE], F32)
        top = sb("top", [P, NT, 8], F32)
        topi = sb("topi", [P, NT, 8], U32)
        topf = sb("topf", [P, NT, 8], F32)
        pick = sb("pick", [P, 2, NT, NE], F32)
        pickw = sb("pickw", [P, 2, NT, NE], F32)
        sel = sb("sel", [P, NT, NE], F32)
        pre = sb("pre", [P, NT + 1, NE], F32)
        tl = sb("tl", [P, 3, NE], F32)
        tri = sb("tri", [P, NE, NE], F32)
        posf = sb("posf", [P, 2, NT], F32)
        pos = sb("pos", [P, 2, NT], U32)
        eidg = sb("eidg", [P, 16, NE - 1], F32)
        eidf = sb("eidf", [P, 16], F32)
        eid = sb("eid", [P, 16], I32)
        comb = sb("comb", [P, NT, NE], F32)
        sx = ExitStack()
        xn = sb("xn", [P, NT, D], F32, sx)
        xnT = sb("xnT", [P, DC, NT, P], F32, sx)
        sx.close()
        sx = ExitStack()
        sb("xn_place", [P, NT, D], F32, sx)
        combT = sb("combT", [NE, NT, P], F32, sx)
        sx.close()
        sx = ExitStack()
        xg = sb("xg", [P, 2, 2, D], F32, sx)
        xgT = sb("xgT", [P, 2, 2, DC, SLOTS], F16, sx)
        yb = sb("yb", [P, 2, 2, D], F32, sx)
        hf = sb("hf", [P, 2, 2 * SLOTS], F32, sx)
        sx.close()
        yg = sb("yg", [P, NT, 2, D])

        s3 = ExitStack()
        WE = 2 * 2 * FH + FC * D + 2 * FH
        wraw = sb("wraw", [P, 2, WE // 2], F32, s3)
        s3e = ExitStack()
        early = sb("early", [P, NE // 2, 2, WE], F16, s3e)
        const12 = sb("const12", [P, ncol - nlate], F32, s3e)
        cst.update({name: const12[:, lo - nlate:hi - nlate] for name, (lo, hi) in CONST_AT.items() if name in EARLY})
        s1, s2 = ExitStack(), ExitStack()
        tapR = sb("tapR", [P, HG, D], F32, s3e)
        skip = sb("skip", [P, 1], F32, s3e)
        wq = sb("wq", [P, DC, D], F32, s1)
        wkv = sb("wkv", [P, DC, D], F32, s1)
        wo = sb("wo", [P, DC, D], F32, s1)
        woT = sb("woT", [P, DC, D], F32, s1)
        toF = sb("toF", [P, DC, 2 * D], F32, s1)
        toO = sb("toO", [P, 3, D], F32, s1)
        sq = sb("sq", [P, 2, 512], F32, s1)
        ss = sb("ss", [P, NT * 32], F32, s1)
        sn = sb("sn", [P, NT * 32], F32, s1)
        rn = sb("rn", [P, 2, NT * 32], F32, s1)
        nn = sb("nn", [P, 2, NT * 32], F32, s1)
        qk = sb("qk", [P, NT, 512], F32, s1)
        kqT = sb("kqT", [P, 4, 512], F32, s1)
        pr = sb("pr", [P, 2, 4, P], F32, s1)
        s1.close()
        tap = sb("tap", [P, HG, D], F32, s2)
        wsk = sb("wsk", [P, NT, D], F32, s2)
        sk2 = sb("sk2", [P, 2, 512], F32, s2)
        kvp = sb("kvp", [P, 2, DC, 512], F32, s2)
        yx = sb("yx", [P, 2, 512], F32, s2)
        yT = sb("yT", [P, DC, NT, P], F32, s2)

        s2.close()
        s3e.close()
        wsp = sb("wsp", [P, NE, 2, WE], F16, s3)
        h1 = sb("h1", [P, 2, FC, SLOTS], F16, s3)
        h2 = sb("h2", [P, 2, FC, SLOTS], F16, s3)

        s4w = ExitStack()
        wqa = sb("wqa", [P, DC, QL], F32, s4w)
        wkva = sb("wkva", [P, DC, P], F32, s4w)
        s4w.close()
        s3.close()
        s4 = ExitStack()
        sq4 = ExitStack()
        wqb = sb("wqb", [P, 2, H4, P], F32, sq4)
        sq4.close()
        kx = sb("kx", [P, 2, DC, 8, P])
        ew = sb("ew", [P, 2, DC, D], F32)
        ewkv = sb("ewkv", [P, 4, D], F32)
        bq5 = sb("bq5", [P, D], F32)
        bp5 = sb("bp5", [P, D], F32)
        bv5 = sb("bv5", [P, D], F32)
        bk5 = sb("bk5", [P, DC], F32)
        eqf = sb("eqf", [P, 4, D], F32)
        eqi = sb("eqi", [P, 4, D], BF16)
        esc = sb("esc", [P, 3, 4], F32)
        ediag = sb("ediag", [P, 4, P], F32)
        wvo = sb("wvo", [P, H4 // 2, D], F32, s4)
        s4p = ExitStack()
        wqbT = sb("wqbT", [64, H4, QL], F32, s4p)
        wkT = sb("wkT", [64, H4, 64], F32, s4p)
        wvT = sb("wvT", [P, H4, 64], F32, s4p)
        wo4b = sb("wo4b", [P, H4 // 2, D], F32, s4p)
        wkvb = sb("wkvb", [64, H4, 192], F32, s4p)
        s4p.close()
        ql0 = sb("ql0", [P, 2, P], F32, s4)
        ql1 = sb("ql1", [64, 2, P], F32, s4)
        kvT = sb("kvT", [P, 2, P], F32, s4)
        kvr = sb("kvr", [P, 2, P], F32, s4)
        kT = sb("kT", [P, 2, P], F32, s4)
        rk = sb("rk", [P, 2, 64], F32, s4)
        rq = sb("rq", [P, 2, 2, 4, 64], F32, s4)
        qs = sb("qs", [P, 2, H4, P], F32, s4)
        qT = sb("qT", [P, 2, H4, P], F32, s4)
        sm = sb("sm", [P, 2, H4, P], F32, s4)
        nm = sb("nm", [P, 2, H4], F32, s4)
        rsum = sb("rsum", [P, 2, H4], F32, s4)
        rinv = sb("rinv", [P, 2, H4], F32, s4)
        pT = sb("pT", [P, 2, H4, P], F32, s4)
        oT = sb("oT", [P, 2, H4 // 2, P], F32, s4)
        s4.close()

        s56, s5 = ExitStack(), ExitStack()
        xi = sb("xi", [P, NT, D], BF16, s56)
        xiT = sb("xiT", [P, DC, NT, P], BF16, s56)
        fw = sb("fw", [P, 3, 2048], F32, s56)
        fi = sb("fi", [P, 3, 2048], BF16, s56)
        ewb = sb("ewb", [P, 2, D], F32, s5)
        ewT = sb("ewT", [P, 2, DC, D], BF16, s5)
        wkvT = sb("wkvT", [P, DC, 512], F32, s5)
        k5T = sb("k5T", [P, DC, NT, P], F32, s5)
        v5 = sb("v5", [P, NT, D], F32, s5)
        q5, q5T = xn, xnT
        q5s = sb("q5s", [P, 2, DC, P], F32, s5)
        v5s = sb("v5s", [P, 2, D], F32, s5)
        s5m = sb("s5m", [P, 2, H4, P], F32, s5)
        n5 = sb("n5", [P, 2, H4], F32, s5)
        r5 = sb("r5", [P, 2, H4], F32, s5)
        i5 = sb("i5", [P, 2, H4], F32, s5)
        p5T = sb("p5T", [P, 2, H4, P], F32, s5)
        o5 = sb("o5", [P, 2, D], F32, s5)
        oq = sb("oq", [P, 2, D], F32, s5)
        oi = sb("oi", [P, 2, D], BF16, s5)
        osc = sb("osc", [P, 2, 3], F32, s5)
        oiT = sb("oiT", [P, 2, DC, P], BF16, s5)
        ot = sb("ot", [P, 2, D], F32, s5)
        s5.close()
        s6 = ExitStack()
        fguT = sb("fguT", [P, DC, 2, 1024], BF16, s6)
        fdT = sb("fdT", [P, 8, D], BF16, s6)
        fg = sb("fg", [P, 2, 1024], F32, s6)
        fh = sb("fh", [P, 2, 1024], F32, s6)
        fq = sb("fq", [P, 2, 1024], F32, s6)
        fhi = sb("fhi", [P, 2, 1024], BF16, s6)
        fhT = sb("fhT", [P, 2, 8, P], BF16, s6)
        s6.close()
        s56.close()

        CREDIT = 2
        W1 = slice(0, 1024)
        W3 = slice(1024, 2048)
        W2 = slice(2048, 4096)
        xs = nc.dram_tensor("sorted_rows", (ET * SLOTS, D), F32, kind="Internal").ap()
        ys = nc.dram_tensor("expert_rows", (ET * SLOTS, D), F32, kind="Internal").ap()

        def x_done(eng, s, t):
            if s == 0:
                eng.wait_ge(sem("x_loaded"), 16)
            elif s == 1:
                eng.wait_ge(sem("x1_added"), t + 1)
            elif s == 2:
                eng.wait_ge(sem("x2_added"), t // 2 + 1)
            elif s == 3:
                eng.wait_ge(sem("x3_added"), t + 1)
            else:
                eng.wait_ge(sem(f"x{s}_added"), t + 2)

        def prep4_moves():
            for k in range(2):
                yield wkT[:, 8 * k:8 * k + 8, :].rearrange("p h n -> p (h n)"), bank[k][0:64, :]
            for k in range(2):
                yield wvT[:, 8 * k:8 * k + 8, :].rearrange("p h n -> p (h n)"), bank[2 + k][:]
            for k in range(4):
                yield wqbT[:, 4 * k:4 * k + 4, 0:P], bank[4 + k][0:64, :].rearrange("p (h n) -> p h n", h=4)
            for k in range(2):
                yield wqbT[:, 8 * k:8 * k + 8, P:QL], bank[k][0:64, :].rearrange("p (h n) -> p h n", h=8)
            for k in range(2):
                yield wqb[:, 0, 8 * k:8 * k + 8, 0:64], bank[2 + k][:].rearrange("p (h n) -> p h n", h=8)
            for k in range(2):
                yield wqb[0:64, 1, 8 * k:8 * k + 8, 0:64], bank[4 + k][0:64, :].rearrange("p (h n) -> p h n", h=8)
            for k in range(4):
                yield wvo[:, 2 * k:2 * k + 2, :].rearrange("p j n -> p (j n)"), bank[(6, 7, 0, 1)[k]][:]

        block = ctx.enter_context(nc.Block())

        @block.sync
        def _(sp):
            sp.dma_start(x[:], a["x"].rearrange("b s d -> s b d")).then_inc(sem("x_loaded"), 16)
            sp.dma_start(const[:], a["consts"][:, 0:nlate]).then_inc(sem("const_loaded"), 16)
            sp.dma_start(const12[:], a["consts"][:, nlate:ncol]).then_inc(sem("const_loaded"), 16)
            for dst, name in ((wq, "L0_attn_W_q"), (wkv, "L0_attn_W_kv"), (wo, "L0_attn_W_o")):
                sp.dma_start(dst[:], a[name].rearrange("(c p) n -> p c n", p=P)).then_inc(sem("w1_loaded"), 16)
            sp.dma_start(cx[:], a["ctx_2048"].rearrange("b s d -> s b d")).then_inc(sem("s2_loaded"), 16)
            for h in range(HG):
                pad = a["kpad"]
                src = bass.AP(tensor=pad.tensor, offset=pad.offset + h * (P + D) + 1, ap=[[1, P], [1, D]])
                sp.dma_start(tapR[:, h, :], src).then_inc(sem("s2_loaded"), 16)
            with nc.allow_non_contiguous_dma(reason="one value per partition"):
                sp.dma_start(skip[:], a["fside_S2_0"].rearrange("(p o) -> p o", o=1)).then_inc(sem("s2_loaded"), 16)
            sp.dma_start(wg[:], a["L0_ffn_Wg"].rearrange("(c p) e -> p c e", p=P)).then_inc(sem("gate_loaded"), 16)
            sp.dma_start(bg[:], a["L0_ffn_bg"].partition_broadcast(P)).then_inc(sem("gate_loaded"), 16)
            sp.dma_start(b3[:], a["L0_ffn_b3"]).then_inc(sem("gate_loaded"), 16)
            for i, name in enumerate(("L0_ffn_b1", "L0_ffn_b2")):
                sp.dma_start(b12[32 * i:32 * i + 32, :], a[name].rearrange("e (c p) -> (e c) p", p=P)).then_inc(sem("gate_loaded"), 16)
            def expert_half(e, half):
                k = 2 * e + half
                if 2 <= k < 12:
                    sp.wait_ge(sem("w_split"), k - 1)
                elif k >= 12:
                    sp.wait_ge(sem("w_split_dve"), k - 11)
                if half == 0:
                    sp.dma_start(wraw[:, 0, 0:1024].rearrange("p (c n) -> p c n", c=DC),
                                 a["L0_ffn_W1"][e].rearrange("(c p) n -> p c n", p=P)).then_inc(sem("w_loaded_even"), 16)
                    sp.dma_start(wraw[:, 0, 1024:2048].rearrange("p (c n) -> p c n", c=FC),
                                 a["L0_ffn_W3"][e].rearrange("(c p) n -> p c n", p=P)).then_inc(sem("w_loaded_even"), 16)
                else:
                    sp.dma_start(wraw[:, 1, :].rearrange("p (c n) -> p c n", c=FC),
                                 a["L0_ffn_W2"][e].rearrange("(c p) n -> p c n", p=P)).then_inc(sem("w_loaded_odd"), 16)

            for e in range(NE):
                if e == NE // 2:
                    x_done(sp, 2, NT - 1)
                for half in range(2):
                    expert_half(e, half)
            def rows_in(i, u):
                sp.dma_start(xg[:, u], xs[bass.ds(i * (2 * SLOTS) + SLOTS * u, SLOTS), :].rearrange("(b p) d -> p b d", p=P)).then_inc(sem(f"xg{u}_loaded"), 16)

            def rows_out(i, u):
                sp.wait_ge(sem("y_ready"), i * 2 + (u + 3))
                sp.dma_start(ys[bass.ds(i * (2 * SLOTS) + SLOTS * u, SLOTS), :].rearrange("(b p) d -> p b d", p=P), yb[:, u]).then_inc(sem(f"y{u}_stored"), 16)

            sp.wait_ge(sem("scattered"), 16 * 2 * NT)
            for j in range(2):
                rows_in(0, j)
            sp.dma_start(wo4a[:], a["L1_attn_Wo"][0:P * H4 // 2].rearrange("(h v) n -> v h n", v=P)).then_inc(sem("w4_loaded"), 16)
            sp.dma_start(wqa[:], a["L1_attn_Wqa"].rearrange("(c p) n -> p c n", p=P)).then_inc(sem("w4_loaded"), 16)
            sp.dma_start(wkva[:], a["L1_attn_Wkva"].rearrange("(c p) n -> p c n", p=P)).then_inc(sem("w4_loaded"), 16)
            sp.wait_ge(sem("w_split_dve"), 6)
            sp.dma_start(wqb[:, 0].rearrange("p h n -> p (h n)"), a["L1_attn_Wqb"][0:P, :]).then_inc(sem("w4_loaded"), 16)
            sp.dma_start(wqb[0:64, 1].rearrange("p h n -> p (h n)"), a["L1_attn_Wqb"][P:QL, :]).then_inc(sem("w4_loaded"), 16)
            with sp.Fori(0, ET // 2 - 1) as i:
                for u in range(2):
                    sp.wait_ge(sem("xgT_psum"), i * 2 + (u + 1))
                    rows_in(i + 1, u)
                    rows_out(i, u)
            last = ET // 2 - 1
            sp.wait_ge(sem("xgT_psum"), ET - 2)
            rows_in(last + 1, 0)
            rows_out(last, 0)
            rows_out(last, 1)
            rows_out(last + 1, 0)
            sp.wait_ge(sem("l3_psum"), ET)
            sp.dma_start(wkvb[:].rearrange("p h n -> p (h n)"), a["L1_attn_Wkvb"]).then_inc(sem("w4_loaded"), 16)
            sp.dma_start(wo4b[:], a["L1_attn_Wo"][P * H4 // 2:].rearrange("(h v) n -> v h n", v=P)).then_inc(sem("wo4b_loaded"), 16)
            for i, name in enumerate(("L1_xattn_wq", "L1_xattn_wp")):
                sp.dma_start(ew[:, i], a[name].rearrange("(c p) n -> p c n", p=P)).then_inc(sem("w5_loaded"), 16)
            sp.dma_start(ewkv[:], a["L1_xattn_wkv"].rearrange("(c p) n -> p c n", p=P)).then_inc(sem("w5_loaded"), 16)
            sp.dma_start(bq5[:], a["L1_xattn_bq"].partition_broadcast(P)).then_inc(sem("w5_loaded"), 16)
            sp.dma_start(bp5[:], a["L1_xattn_bp"].partition_broadcast(P)).then_inc(sem("w5_loaded"), 16)
            sp.dma_start(bv5[:], a["L1_xattn_bkv"][D:2 * D].partition_broadcast(P)).then_inc(sem("w5_loaded"), 16)
            with nc.allow_non_contiguous_dma(reason="one value per partition"):
                sp.dma_start(bk5[:], a["L1_xattn_bkv"][0:D].rearrange("(c p) -> p c", p=P)).then_inc(sem("w5_loaded"), 16)
            x_done(sp, 4, NT - 1)
            for i, (name, c) in enumerate((("L1_ffn_w_gate", 8), ("L1_ffn_w_up", 8), ("L1_ffn_w_down", 2))):
                sp.dma_start(fw[:, i, :].rearrange("p (c n) -> p c n", c=c), a[name].rearrange("(c p) n -> p c n", p=P)).then_inc(sem("w6_loaded"), 16)
            with sp.Fori(0, NT) as t:
                sp.wait_ge(sem("x6_added"), t + 3)
                sp.dma_start(out[bass.ds(t, 1)].rearrange("b s d -> s (b d)"), x[:, bass.ds(t, 1), :].rearrange("p t d -> p (t d)")).then_inc(sem("stored"), 16)
            sp.wait_ge(sem("stored"), 16 * NT)

        @block.gpsimd
        def _(pool):
            unused = early[:, NE // 2 - 1].rearrange("p a n -> p (a n)").bitcast(F32)
            zeros = unused[:, 0:ET * D].rearrange("p (b d) -> p b d", d=D)
            nc.gpsimd.memset(unused, 0.0).then_inc(sem("zeroed"), 1)
            pool.wait_ge(sem("zeroed"), 1)
            pool.wait_ge(sem("w1_loaded"), 48)
            for k in range(2):
                rows = ET * P
                pool.dma_start(xs[rows * k:rows * k + rows, :].rearrange("(b p) d -> p b d", p=P), zeros).then_inc(sem("zero_filled"), 16)

            def split_low(k):
                e, half = k // 2, k % 2
                cols = slice(2048 * half, 2048 * half + 2048)
                if k < POOL_HALVES:
                    pool.wait_ge(sem("w_hi_pool"), k + 1)
                else:
                    pool.wait_ge(sem("w_hi"), k - POOL_HALVES + 1)
                nc.gpsimd.tensor_tensor(wsp[:, e, 1, cols], wraw[:, half, :], wsp[:, e, 0, cols], ALU.subtract).then_inc(sem("w_split"), 1)

            for k in range(POOL_HALVES):
                pool.wait_ge(sem("w_loaded_odd" if k % 2 else "w_loaded_even"), (16 if k % 2 else 32) * (k // 2 + 1))
                cols = slice(2048 * (k % 2), 2048 * (k % 2) + 2048)
                nc.gpsimd.tensor_copy(wsp[:, k // 2, 0, cols], wraw[:, k % 2, :]).then_inc(sem("w_hi_pool"), 1)
                split_low(k)
            pool.wait_ge(sem("xnT_act"), 4)
            pool.wait_ge(sem("xnT_dve"), 4)
            pool.wait_ge(sem("cxT_ready"), 4)
            for h in range(HG):
                if h >= 2:
                    pool.wait_ge(sem("conv_psum"), 2 * (h - 1))
                for c in range(DC):
                    g = slice(CH * h, CH * h + CH)
                    nc.gpsimd.tensor_tensor(
                        kvp[:, h % 2, c, :].rearrange("p (b i j) -> p b i j", b=NT, i=CH),
                        xnT[:, c, :, g].unsqueeze(3).to_broadcast([P, NT, CH, CH]),
                        cxT[:, c, :, g].unsqueeze(2).to_broadcast([P, NT, CH, CH]),
                        ALU.mult).then_inc(sem("kvp_ready"), 1)
            for k in range(POOL_HALVES, 10):
                split_low(k)
            pool.wait_ge(sem("zero_filled"), 32)
            pool.wait_ge(sem("route_ready"), 4)
            for t in range(NT):
                for r in range(2):
                    pool.indirect_dma_start(xs[:, :], bass.IndirectOffsetOnAxis(ap=pos[:, r, t:t + 1], axis=0), xn[:, t, :], None).then_inc(sem("scattered"), 16)
            pool.wait_ge(sem("y0_stored"), 16 * (ET // 2 + 2))
            pool.wait_ge(sem("y1_stored"), 16 * (ET // 2 + 1))
            for t in range(NT):
                for r in range(2):
                    pool.indirect_dma_start(yg[:, t, r, :], None, ys[:, :], bass.IndirectOffsetOnAxis(ap=pos[:, r, t:t + 1], axis=0)).then_inc(sem(f"gathered{t // 4}"), 16)
            def rope_q(i, u, g):
                v = qs[:, u, 4 * g:4 * g + 4, 64:128]
                pairs = v.rearrange("p h (f two) -> p h f two", two=2)
                cosb = cst["cos"].unsqueeze(1).to_broadcast([P, 4, 64])
                sinb = cst["sin"].rearrange("p (f two) -> p f two", two=2).unsqueeze(1).to_broadcast([P, 4, 32, 2])
                turned = rq[:, g % 2, 1].rearrange("p h (f two) -> p h f two", two=2)
                pool.wait_ge(sem("q4_copied"), i * 8 + (4 * u + g + 3))
                nc.gpsimd.tensor_tensor(rq[:, g % 2, 0], v, cosb, ALU.mult).then_inc(sem("rope_step"), 1)
                for two in range(2):
                    nc.gpsimd.tensor_tensor(turned[:, :, :, two], pairs[:, :, :, 1 - two], sinb[:, :, :, two], ALU.mult).then_inc(sem("rope_step"), 1)
                pool.wait_ge(sem("rope_step"), i * 24 + (3 * (4 * u + g) + 3))
                nc.gpsimd.tensor_tensor(v, rq[:, g % 2, 0], rq[:, g % 2, 1], ALU.add).then_inc(sem("roped"), 1)

            def divide(i, j):
                u, hs = j // 4, slice(4 * (j % 4), 4 * (j % 4) + 4)
                pool.wait_ge(sem("r4_ready"), i * 8 + (j + 1))
                nc.gpsimd.tensor_tensor(sm[:, u, hs, :], sm[:, u, hs, :],
                                        rinv[:, u, hs].unsqueeze(2).to_broadcast([P, 4, P]), ALU.mult).then_inc(sem("p4_ready"), 1)

            def pair4(i, after):
                for j in range(8):
                    if after is not None:
                        rope_q(after, j // 4, j % 4)
                    if j >= 2:
                        divide(i, j - 2)
                divide(i, 6)
                divide(i, 7)

            for j in range(8):
                rope_q(0, j // 4, j % 4)
            with pool.Fori(0, NT // 2 - 1) as i:
                pair4(i, i + 1)
            pair4(NT // 2 - 1, None)
            pool.wait_ge(sem("w5_loaded"), 112)
            pool.wait_ge(sem("xn_ready"), 5 * NT)
            nc.gpsimd.tensor_tensor(x[:], x[:], bp5[:].unsqueeze(1).to_broadcast([P, NT, D]), ALU.add).then_inc(sem("x_biased"), 1)
            pool.sem_inc(sem("s5_psum"), 8)
            pool.wait_ge(sem("prep5_ready"), 6)

            def spread_keys(i, u):
                for c in range(DC):
                    pool.wait_ge(sem("s5_psum"), i * 8 + (4 * u + 4))
                    nc.gpsimd.tensor_tensor(kx[:, u, c], k5T[:, c, bass.ds(i * 2 + u, 1), :].to_broadcast([P, 8, P]),
                                            cst["head16"].unsqueeze(2).to_broadcast([P, 8, P]), ALU.mult).then_inc(sem("kx_ready"), 1)

            def ternary(w, step):
                nc.gpsimd.tensor_scalar(fw[:, w, :], fw[:, w, :], fws[:, 3, w:w + 1], ROUND, ALU.mult, ALU.add).then_inc(sem("w6_step"), 1)
                pool.wait_ge(sem("w6_step"), step + 1)
                nc.gpsimd.tensor_scalar(fw[:, w, :], fw[:, w, :], -ROUND, 1.0, ALU.add, ALU.min).then_inc(sem("w6_step"), 1)
                pool.wait_ge(sem("w6_step"), step + 2)
                nc.gpsimd.tensor_scalar(fi[:, w, :], fw[:, w, :], -1.0, None, ALU.max).then_inc(sem("w6_ternary"), 1)

            for i in range(NT // 2):
                for u in range(2):
                    spread_keys(i, u)
                if i == 0:
                    pool.wait_ge(sem("w6_scale"), 1)
                if i < 3:
                    ternary(i, 2 * i)

        @block.scalar
        def _(act):
            def preload(function):
                nc.scalar.activation(unread[:], cst["ident"][0:1, 0:1], function)

            def deviation(s):
                act.wait_ge(sem("ln_var"), s)
                nc.scalar.activation(sd[:], ve[:], ACT.Sqrt).then_inc(sem("ln_sd"), 1)

            def xnT_copies(s):
                for half in range(2):
                    act.wait_ge(sem("xnT_psum"), 4 * (s - 1) + 2 * half + 1)
                    nc.scalar.copy(xnT[:, 0, 4 * half:4 * half + 4, :].rearrange("p t s -> p (t s)"), bank[2 * half][:]).then_inc(sem("xnT_act"), 1)

            def split_high(k):
                e, half = k // 2, k % 2
                act.wait_ge(sem("w_loaded_odd" if half else "w_loaded_even"), (16 if half else 32) * (e + 1))
                nc.scalar.copy(wsp[:, e, 0, 2048 * half:2048 * half + 2048], wraw[:, half, :]).then_inc(sem("w_hi"), 1)

            deviation(1)
            act.wait_ge(sem("prep1_psum"), 1)
            nc.scalar.copy(woT[:].rearrange("p c n -> p (c n)"), bank[4][:]).then_inc(sem("prep1_ready"), 1)
            for c in range(DC):
                act.wait_ge(sem("prep1_psum"), c + 2)
                nc.scalar.copy(toF[:, c, :], bank[5 + c][:]).then_inc(sem("prep1_ready"), 1)
            xnT_copies(1)
            def norms(half):
                act.wait_ge(sem("ss_done"), 4 * half + 4)
                cols = slice(P * half, P * half + P)
                nc.scalar.activation(sn[:, cols], ss[:, cols], ACT.Sqrt).then_inc(sem("norm_ready"), 1)

            for t in range(NT):
                act.wait_ge(sem("qk_psum"), t + 1)
                if t >= 2:
                    act.wait_ge(sem("ss_done"), t - 1)
                nc.scalar.activation(sq[:, t % 2, :], bank[t % 4][:], ACT.Square).then_inc(sem("sq_ready"), 1)
                nc.scalar.copy(qk[:, t, :], bank[t % 4][:]).then_inc(sem("qk_ready"), 1)
                if t == 3:
                    norms(0)
            act.wait_ge(sem("prep1_psum"), 4)
            nc.scalar.copy(toO[:, 0:2, :].rearrange("p c n -> p (c n)"), bank[7][:]).then_inc(sem("prep1_ready"), 1)
            act.wait_ge(sem("prep1_psum"), 5)
            nc.scalar.copy(toO[:, 2, :], bank[4][:, 0:D]).then_inc(sem("prep1_ready"), 1)
            nc.scalar.copy(identb[:], cst["ident"]).then_inc(sem("prep1_ready"), 1)
            norms(1)
            for t in range(NT):
                act.wait_ge(sem("kq_psum"), t + 1)
                if t >= 4:
                    act.wait_ge(sem("products_ready"), t - 3)
                nc.scalar.copy(kqT[:, t % 4, :], bank[4 + t % 4][:]).then_inc(sem("kqT_ready"), 1)
            for k in range(8):
                act.wait_ge(sem("tap_psum"), k + 1)
                nc.scalar.copy(tap[:, 2 * k:2 * k + 2, :].rearrange("p h n -> p (h n)"), bank[4 + k % 2][:]).then_inc(sem("tap_ready"), 1)
            deviation(2)
            for half in range(2):
                for c in range(DC):
                    act.wait_ge(sem("cxT_psum"), 2 * half + c + 1)
                    nc.scalar.copy(cxT[:, c, 4 * half:4 * half + 4, :].rearrange("p t s -> p (t s)"), bank[6 + c][:]).then_inc(sem("cxT_ready"), 1)
            xnT_copies(2)
            for k in range(POOL_HALVES, 6):
                split_high(k)
            act.wait_ge(sem("zero_filled"), 32)
            split_high(6)
            act.wait_ge(sem("gate_psum"), 1)
            nc.scalar.copy(bT[:], bank[4][:, 0:64]).then_inc(sem("gate_act"), 1)
            deviation(3)
            split_high(7)
            xnT_copies(3)
            split_high(8)
            split_high(9)
            act.wait_ge(sem("route_ready"), 1)
            nc.scalar.activation(gw[:].rearrange("p t e -> p (t e)"), lg[:].rearrange("p t e -> p (t e)"), ACT.Exp).then_inc(sem("gate_act"), 1)
            split_high(10)
            split_high(11)
            for k in range(2):
                act.wait_ge(sem("gate_psum"), k + 4)
                nc.scalar.copy(combT[:, 4 * k:4 * k + 4, :].rearrange("p t s -> p (t s)"), bank[5 + k][0:NE, :]).then_inc(sem("gate_act"), 1)
            for k in range(12, 16):
                split_high(k)
            act.sem_inc(sem("h1_f32"), CREDIT)
            act.sem_inc(sem("h2_f32"), CREDIT)
            act.sem_inc(sem("y_ready"), CREDIT)
            act.sem_inc(sem("y0_stored"), 16)
            act.sem_inc(sem("y1_stored"), 16)
            act.wait_ge(sem("route_ready"), 5)
            act.wait_ge(sem("gate_act"), 1)

            def hidden(layer, i, u):
                e = act.value_load(eid[0:1, bass.ds(i * 2 + u, 1)], min_val=0, max_val=NE - 1)
                nc.scalar.copy(be[:, layer - 1, u, :], bT[:, bass.ds(e * FC + 32 * (layer - 1), FC)]).then_inc(sem("bias_ready"), 1)
                act.wait_ge(sem("bias_ready"), i * 4 + (2 * u + layer))
                for p in range(2):
                    n = i * 4 + (2 * u + p)
                    act.wait_ge(sem(f"l{layer}_psum"), n + 1)
                    act.wait_ge(sem("h2_lo" if layer == 1 else "h1_lo"), n + 1)
                    for k in range(2):
                        last = nc.scalar.activation(hf[:, p, SLOTS * k:SLOTS * k + SLOTS], bank[2 * (layer - 1) + p][:, SLOTS * k:SLOTS * k + SLOTS],
                                                    ACT.Gelu, bias=be[:, layer - 1, u, 2 * p + k:2 * p + k + 1])
                    last.then_inc(sem(f"h{layer}_f32"), 1)

            def expert_out(i, u):
                act.wait_ge(sem("l3_psum"), i * 2 + (u + 1))
                act.wait_ge(sem(f"y{u}_stored"), i * 16 + 16)
                nc.scalar.copy(yb[:, u].rearrange("p b d -> p (b d)"), bank[4 + u][:]).then_inc(sem("y_ready"), 1)

            preload(ACT.Gelu)
            hidden(1, 0, 0)
            with act.Fori(0, ET // 2) as i:
                for u in range(2):
                    hidden(2, i, u)
                    hidden(1, i + u, 1 - u)
                    expert_out(i, u)
            hidden(2, ET // 2, 0)
            expert_out(ET // 2, 0)
            def prep(k, dst, src):
                act.wait_ge(sem("prep4_psum"), k + 1)
                nc.scalar.copy(dst, src).then_inc(sem("prep4_act"), 1)

            moves4 = list(prep4_moves())
            for k, (dst, src) in enumerate(moves4[:-1]):
                prep(k, dst, src)
            preload(ACT.Sqrt)
            deviation(4)
            prep(len(moves4) - 1, *moves4[-1])
            xnT_copies(4)
            preload(ACT.Exp)
            act.sem_inc(sem("q4_copied"), 2)

            def query_latents(i):
                act.wait_ge(sem("lat_psum"), i + 1)
                nc.scalar.copy(ql0[:].rearrange("p u s -> p (u s)"), bank[0][:, 0:2 * P])
                nc.scalar.copy(ql1[:].rearrange("p u s -> p (u s)"), bank[0][0:64, 2 * P:4 * P]).then_inc(sem("lat_copied"), 1)

            def key_latents(i, u):
                act.wait_ge(sem("kv_psum"), i * 2 + (u + 1))
                nc.scalar.copy(kvT[:, u, :], bank[0][:, 0:P]).then_inc(sem("kvT_ready"), 1)

            def exps(i, u, g):
                act.wait_ge(sem("nm_ready"), i * 8 + (4 * u + g + 1))
                for h in range(4 * g, 4 * g + 4):
                    last = nc.scalar.activation(sm[:, u, h, :], sm[:, u, h, :], ACT.Exp, bias=nm[:, u, h:h + 1], accum_out=rsum[:, u, h:h + 1])
                last.then_inc(sem("exp_ready"), 1)

            def queries(i, j):
                u, g = j // 4, j % 4
                act.wait_ge(sem("q4_psum"), i * 8 + (j + 1))
                nc.scalar.copy(qs[:, u, 4 * g:4 * g + 4, :].rearrange("p h n -> p (h n)"), bank[1 + g % 2][:]).then_inc(sem("q4_copied"), 1)

            def pair4(i, after):
                for j in range(8):
                    u, g = j // 4, j % 4
                    act.wait_ge(sem("t4_psum"), i * 8 + (j + 1))
                    nc.scalar.copy(qT[:, u, 4 * g:4 * g + 4, :].rearrange("p h n -> p (h n)"), bank[3 + g % 2][:]).then_inc(sem("qT_ready"), 1)
                    if j == 0:
                        act.wait_ge(sem("kT_psum"), i + 1)
                        nc.scalar.copy(kT[:].rearrange("p u s -> p (u s)"), bank[0][:, 2 * P:4 * P]).then_inc(sem("kT_ready"), 1)
                    if after is not None:
                        if j == 0:
                            query_latents(after)
                        queries(after, j)
                    if j >= 2:
                        exps(i, (j - 2) // 4, (j - 2) % 4)
                exps(i, 1, 2)
                exps(i, 1, 3)
                for u in range(2):
                    for k in range(2):
                        act.wait_ge(sem("pv_psum"), i * 4 + (2 * u + k + 1))
                        nc.scalar.copy(oT[:, u, 4 * k:4 * k + 4, :].rearrange("p h n -> p (h n)"), bank[7 if k == 0 else 0][:]).then_inc(sem("oT_ready"), 1)
                    if after is not None:
                        key_latents(after, u)

            query_latents(0)
            for j in range(8):
                queries(0, j)
                if j in (0, 4):
                    key_latents(0, j // 4)
            with act.Fori(0, NT // 2 - 1) as i:
                pair4(i, i + 1)
            pair4(NT // 2 - 1, None)
            preload(ACT.Sqrt)
            for k in range(2):
                act.wait_ge(sem("prep5_psum"), k + 1)
                nc.scalar.copy(wkvT[:, k, :], bank[k][:]).then_inc(sem("prep5_ready"), 1)
            deviation(5)
            act.wait_ge(sem("w5_loaded"), 112)
            for k in range(4):
                act.wait_ge(sem("prep5_psum"), k + 3)
                nc.scalar.activation(k5T[:, k // 2, 4 * (k % 2):4 * (k % 2) + 4, :].rearrange("p t s -> p (t s)"), bank[2 + k][:], ACT.Identity,
                                     bias=bk5[:, k // 2:k // 2 + 1]).then_inc(sem("prep5_ready"), 1)
            act.wait_ge(sem("prep5_psum"), 7)
            nc.scalar.copy(ewT[:].rearrange("p w c n -> p (w c n)"), bank[2][:].bitcast(BF16)).then_inc(sem("prep5_ready"), 1)
            act.wait_ge(sem("prep5_psum"), 8)
            nc.scalar.copy(ewb[:].rearrange("p w n -> p (w n)"), bank[3][:]).then_inc(sem("prep5_ready"), 1)

            def xiT_copy(s):
                act.wait_ge(sem("xiT_psum"), 2 * (s - 5) + 1)
                nc.scalar.copy(xiT[:, 0].rearrange("p t s -> p (t s)"), bank[4 if s == 5 else 0][:].bitcast(BF16)).then_inc(sem("xiT_ready"), 1)

            def magnitudes(k, unused):
                act.wait_ge(sem("w6_loaded"), 48)
                nc.scalar.activation(unused.rearrange("p h n -> p (h n)"), fw[:, k, :], ACT.Abs, accum_out=fws[:, 0, k:k + 1]).then_inc(sem("prep5_ready"), 1)

            magnitudes(0, s5m[:, 0])
            magnitudes(1, s5m[:, 1])
            xiT_copy(5)
            magnitudes(2, p5T[:, 0])
            for k in range(4):
                act.wait_ge(sem("q5T_psum"), k + 1)
                nc.scalar.copy(q5T[:, k % 2, 4 * (k // 2):4 * (k // 2) + 4, :].rearrange("p t s -> p (t s)"), bank[4 + k][:]).then_inc(sem("q5T_ready"), 1)
            preload(ACT.Exp)
            act.sem_inc(sem("exp5_ready"), 2)
            act.sem_inc(sem("p5T_act"), 1)
            act.wait_ge(sem("prep5_ready"), 11)

            def pair5(i, before):
                for j in range(8):
                    u, g = j // 4, j % 4
                    act.wait_ge(sem("n5_ready"), i * 8 + (j + 1))
                    for k in range(4):
                        h = 4 * g + k
                        last = nc.scalar.activation(s5m[:, u, h, :], bank[5 + g % 2][:, P * k:P * k + P], ACT.Exp,
                                                    bias=n5[:, u, h:h + 1], accum_out=r5[:, u, h:h + 1])
                    last.then_inc(sem("exp5_ready"), 1)
                    if j == 5 and before is not None:
                        outputs5(before)
                    if j and j % 2 == 0:
                        copy_p5T_odd(i, j - 1)
                copy_p5T_odd(i, 7)

            def copy_p5T_odd(i, j):
                u, g = j // 4, j % 4
                act.wait_ge(sem("pt5_psum"), i * 8 + (j + 1))
                nc.scalar.copy(p5T[:, u, 4 * g:4 * g + 4, :].rearrange("p h n -> p (h n)"), bank[4][:]).then_inc(sem("p5T_act"), 1)

            def outputs5(i):
                act.wait_ge(sem("oiT_psum"), i + 1)
                nc.scalar.copy(oiT[:].rearrange("p u c s -> p (u c s)"), bank[1][:, 0:2 * P].bitcast(BF16)).then_inc(sem("oiT_ready"), 1)

            pair5(0, None)
            with act.Fori(0, NT // 2 - 1) as i:
                pair5(i + 1, i)
            preload(ACT.Sqrt)
            outputs5(NT // 2 - 1)
            deviation(6)

            def ternary_copy(k):
                act.wait_ge(sem("w6T_psum"), k + 1)
                b16 = bank[2 + k][:].bitcast(BF16)
                dst = fguT[:, k % 2, k // 2, :] if k < 4 else fdT[:, 4 * (k - 4):4 * (k - 4) + 4, :].rearrange("p c n -> p (c n)")
                nc.scalar.copy(dst, b16).then_inc(sem("w6T_ready"), 1)

            for k in range(6):
                ternary_copy(k)
            preload(ACT.Silu)
            act.wait_ge(sem("xn_scaled"), 1)
            for t in range(SCALED_BY_VECTOR, NT):
                nc.scalar.activation(xn[:, t, :], xn[:, t, :], ACT.Copy, bias=ROUND, scale=xsc[:, 2, t:t + 1]).then_inc(sem("xn_scaled"), 1)
            xiT_copy(6)

            def silu(i, u):
                act.wait_ge(sem("fsn_ready"), i * 2 + (u + 1))
                act.wait_ge(sem("gu_psum"), i * 4 + (2 * u + 1))
                for k in range(2):
                    nc.scalar.activation(fg[:, u, 512 * k:512 * k + 512], bank[2 * u + k][:], ACT.Silu, scale=fsn[:, u, 0:1]).then_inc(sem("silu_ready"), 1)

            def rounded(i, u):
                act.wait_ge(sem("f_step"), i * 10 + (5 * u + 5))
                nc.scalar.activation(fq[:, u, :], fh[:, u, :], ACT.Copy, bias=ROUND, scale=fsd[:, u, 2:3]).then_inc(sem("fq_ready"), 1)

            def turned(i, u):
                act.wait_ge(sem("fhT_psum"), i * 2 + (u + 1))
                nc.scalar.copy(fhT[:, u].rearrange("p c s -> p (c s)"), bank[6][:].bitcast(BF16)).then_inc(sem("fhT_ready"), 1)

            silu(0, 0)
            silu(0, 1)
            rounded(0, 0)
            with act.Fori(0, NT // 2 - 1) as i:
                for u in range(2):
                    silu(i + 1, u)
                    rounded(i + u, 1 - u)
                    turned(i, u)
            rounded(NT // 2 - 1, 1)
            turned(NT // 2 - 1, 0)
            turned(NT // 2 - 1, 1)

        @block.vector
        def _(dve):
            own = [0]

            def then(ins):
                own[0] += 1
                ins.then_inc(sem("dve_own"), 1)
                dve.wait_ge(sem("dve_own"), own[0])

            def rsqrt_refined(v, root, r, tmp):
                then(nc.vector.reciprocal(r[:, 0], root))
                then(nc.vector.tensor_tensor(tmp[:, 0], r[:, 0], r[:, 0], ALU.mult))
                then(nc.vector.tensor_tensor(tmp[:, 1], tmp[:, 0], v, ALU.mult))
                then(nc.vector.tensor_scalar(tmp[:, 0], tmp[:, 1], -0.5, 1.5, ALU.mult, ALU.add))
                then(nc.vector.tensor_tensor(r[:, 1], r[:, 0], tmp[:, 0], ALU.mult))

            def stats(s, t):
                x_done(dve, s - 1, t)
                nc.vector.bn_stats(st[:, t, :], x[:, t, :]).then_inc(sem("ln_stats"), 1)

            def layernorm(s):
                for t in range(NT):
                    if s == 1 or (s in (5, 6) and t >= NT - 2):
                        stats(s, t)
                for t in range(NT):
                    dve.wait_ge(sem("ln_stats"), NT * (s - 1) + t + 1)
                    nc.vector.bn_aggr(mv[:, t, :], st[:, t, :]).then_inc(sem("ln_mean"), 1)
                dve.wait_ge(sem("ln_mean"), NT * s)
                nc.vector.tensor_scalar(ve[:], mv[:, :, 1], EPS, None, ALU.add).then_inc(sem("ln_var"), 1)
                dve.wait_ge(sem("ln_sd"), s)
                r2 = rs[:].rearrange("p t k -> p k t")
                rsqrt_refined(ve[:], sd[:], r2, nw)
                for t in range(NT):
                    nc.vector.tensor_scalar(xn[:, t, :], x[:, t, :], mv[:, t, 0:1], rs[:, t, 1:2], ALU.subtract, ALU.mult).then_inc(sem("xn_ready"), 1)

            def xnT_copies(s):
                for half in range(2):
                    dve.wait_ge(sem("xnT_psum"), 4 * (s - 1) + 2 * half + 2)
                    nc.vector.tensor_copy(xnT[:, 1, 4 * half:4 * half + 4, :].rearrange("p t s -> p (t s)"), bank[2 * half + 1][:]).then_inc(sem("xnT_dve"), 1)

            layernorm(1)
            xnT_copies(1)
            def square_sums(t):
                dve.wait_ge(sem("sq_ready"), t + 1)
                nc.vector.tensor_reduce(ss[:, 32 * t:32 * t + 32],
                                        sq[:, t % 2, :].rearrange("p (w a h k) -> p w h a k", w=2, a=2, k=8),
                                        AX.XY, ALU.add).then_inc(sem("ss_done"), 1)

            def inverse_norms(half):
                cols = slice(P * half, P * half + P)
                dve.wait_ge(sem("norm_ready"), half + 1)
                rsqrt_refined(ss[:, cols], sn[:, cols], rn[:, :, cols], nn[:, :, cols])

            def unit_coefficients(t):
                dve.wait_ge(sem("qk_ready"), t + 1)
                for w in range(2):
                    v = qk[:, t, D * w:D * w + D].rearrange("p (a h k) -> p a h k", a=2, k=8)
                    r = rn[:, 1, 32 * t + 16 * w:32 * t + 16 * w + 16].unsqueeze(1).unsqueeze(3).to_broadcast([P, 2, 16, 8])
                    nc.vector.tensor_tensor(v, v, r, ALU.mult).then_inc(sem("qkn_ready"), 1)

            for t in range(4):
                square_sums(t)
            inverse_norms(0)
            for t in range(4, NT):
                square_sums(t)
                unit_coefficients(t - 4)
            inverse_norms(1)
            for t in range(4, NT):
                unit_coefficients(t)

            def add_attention(t):
                dve.wait_ge(sem("attn_psum"), t + 1)
                nc.vector.tensor_tensor(x[:, t, :], x[:, t, :], bank[t % 4][:, 0:D], ALU.add).then_inc(sem("x1_added"), 1)
                stats(2, t)

            for t in range(NT):
                dve.wait_ge(sem("kqT_ready"), t + 1)
                k, w = t % 4, t % 2
                nc.vector.tensor_tensor(pr[:, w, 0:2, :].rearrange("p a s -> p (a s)"), kqT[:, k, 0:256], kqT[:, k, 256:512], ALU.mult)
                nc.vector.tensor_tensor(pr[:, w, 2, :], kqT[:, k, 0:128], kqT[:, k, 384:512], ALU.mult)
                nc.vector.tensor_tensor(pr[:, w, 3, :], kqT[:, k, 128:256], kqT[:, k, 256:384], ALU.mult).then_inc(sem("products_ready"), 1)
                if t >= 1:
                    add_attention(t - 1)
            add_attention(NT - 1)
            layernorm(2)
            dve.wait_ge(sem("s2_loaded"), 16 * (HG + 2))
            for k in range(4):
                two = slice(2 * k, 2 * k + 2)
                dve.wait_ge(sem("xn_ready"), NT + 2 * k + 2)
                nc.vector.scalar_tensor_tensor(wsk[:, two, :], xn[:, two, :], skip[:, 0:1], cx[:, two, :],
                                               ALU.mult, ALU.mult).then_inc(sem("wsk_ready"), 1)
            xnT_copies(2)
            for k in range(4):
                two = slice(2 * k, 2 * k + 2)
                dve.wait_ge(sem("skip_psum"), k + 1)
                then(nc.vector.tensor_tensor(sk2[:, k % 2, :], bank[4 + k][:], cx[:, two, :].rearrange("p t d -> p (t d)"), ALU.mult))
                xt = x[:, two, :].rearrange("p t d -> p (t d)")
                nc.vector.tensor_tensor(xt, xt, sk2[:, k % 2, :], ALU.add).then_inc(sem("skip_added"), 1)
            for h in range(HG):
                g = slice(CH * h, CH * h + CH)
                for lc in range(DC):
                    dve.wait_ge(sem("conv_psum"), 2 * h + lc + 1)
                    b = 2 * (h % 2) + lc
                    if h >= 1:
                        dve.wait_ge(sem("yT_ready"), 2 * (h - 1) + lc + 1)
                    nc.vector.tensor_tensor(yx[:, lc, :].rearrange("p (b j i) -> p b j i", b=NT, j=CH),
                                            bank[b][:].rearrange("p (b i j) -> p b j i", b=NT, i=CH),
                                            cxT[:, lc, :, g].unsqueeze(2).to_broadcast([P, NT, CH, CH]),
                                            ALU.mult).then_inc(sem("yx_ready"), 1)
                for lc in range(DC):
                    dve.wait_ge(sem("yx_ready"), 2 * h + lc + 1)
                    nc.vector.tensor_reduce(yT[:, lc, :, g], yx[:, lc, :].rearrange("p (b j i) -> p b j i", b=NT, j=CH),
                                            AX.X, ALU.add).then_inc(sem("yT_ready"), 1)
            dve.wait_ge(sem("skip_added"), 4)
            for k in range(4):
                dve.wait_ge(sem("conv_out_psum"), k + 1)
                xt = x[:, 2 * k:2 * k + 2, :].rearrange("p t d -> p (t d)")
                nc.vector.tensor_tensor(xt, xt, bank[4 + k][:], ALU.add).then_inc(sem("x2_added"), 1)
                stats(3, 2 * k)
                stats(3, 2 * k + 1)
            layernorm(3)
            xnT_copies(3)
            dve.wait_ge(sem("gate_psum"), 2)
            dve.wait_ge(sem("gate_loaded"), 80)
            bg8 = bg[:].unsqueeze(1).to_broadcast([P, NT, NE])
            then(nc.vector.tensor_tensor(lg[:], bank[7][:, 0:64].rearrange("p (t e) -> p t e", e=NE), bg8, ALU.add))
            then(nc.vector.tensor_reduce(gm[:], lg[:], AX.X, ALU.max))
            nc.vector.tensor_tensor(lg[:], lg[:], gm[:].unsqueeze(2).to_broadcast([P, NT, NE]), ALU.subtract).then_inc(sem("route_ready"), 1)
            dve.wait_ge(sem("gate_act"), 2)
            then(nc.vector.tensor_reduce(gs[:, 0, :], gw[:], AX.X, ALU.add))
            then(nc.vector.reciprocal(gs[:, 1, :], gs[:, 0, :]))
            then(nc.vector.tensor_tensor(gw[:], gw[:], gs[:, 1, :].unsqueeze(2).to_broadcast([P, NT, NE]), ALU.mult))
            def burst(instructions):
                for ins in instructions:
                    own[0] += 1
                    ins.then_inc(sem("dve_own"), 1)
                dve.wait_ge(sem("dve_own"), own[0])

            burst(nc.vector.max(top[:, t, :], gw[:, t, :]) for t in range(NT))
            burst(nc.vector.max_index(topi[:, t, :], top[:, t, :], gw[:, t, :]) for t in range(NT))
            then(nc.vector.tensor_copy(topf[:], topi[:]))
            iota = cst["iota"][:, 0:NE].unsqueeze(1).to_broadcast([P, NT, NE])
            burst(nc.vector.tensor_tensor(pick[:, r], iota, topf[:, :, r:r + 1].to_broadcast([P, NT, NE]), ALU.is_equal) for r in range(2))
            nc.vector.tensor_tensor(sel[:], pick[:, 0], pick[:, 1], ALU.add).then_inc(sem("route_ready"), 1)
            burst(nc.vector.tensor_tensor(pickw[:, r], pick[:, r], top[:, :, r:r + 1].to_broadcast([P, NT, NE]), ALU.mult) for r in range(2))
            nc.vector.tensor_tensor(comb[:], pickw[:, 0], pickw[:, 1], ALU.add).then_inc(sem("route_ready"), 1)
            nc.vector.memset(pre[:, 0, :], 0.0)
            dve.wait_ge(sem("gate_psum"), 3)
            rank = bank[4][:, 0:64].rearrange("p (t e) -> p t e", e=NE)
            count = bank[4][:, 64:128].rearrange("p (t e) -> p t e", e=NE)
            then(nc.vector.tensor_copy(pre[:, 1, :], count[:, 0, :]))
            for t in range(1, NT):
                then(nc.vector.tensor_tensor(pre[:, t + 1, :], pre[:, t, :], count[:, t, :], ALU.add))
            then(nc.vector.tensor_scalar(tl[:, 0, :], pre[:, NT, :], 1.0 / SLOTS, 0.5 - 0.5 / SLOTS, ALU.mult, ALU.add))
            then(nc.vector.tensor_scalar(tl[:, 0, :], tl[:, 0, :], ROUND, None, ALU.add))
            then(nc.vector.tensor_scalar(tl[:, 0, :], tl[:, 0, :], -ROUND, None, ALU.add))
            then(nc.vector.tensor_tensor(tri[:], cst["before"].rearrange("p (e f) -> p e f", e=NE), tl[:, 0, :].unsqueeze(1).to_broadcast([P, NE, NE]), ALU.mult))
            then(nc.vector.tensor_reduce(tl[:, 1, :], tri[:], AX.X, ALU.add))
            then(nc.vector.tensor_tensor(tl[:, 2, :], tl[:, 1, :], tl[:, 0, :], ALU.subtract))
            then(nc.vector.tensor_scalar(tl[:, 2, :], tl[:, 2, :], float(SLOTS), -1.0, ALU.mult, ALU.add))
            then(nc.vector.tensor_tensor(sel[:], rank, pre[:, 0:NT, :], ALU.add))
            then(nc.vector.tensor_tensor(sel[:], sel[:], tl[:, 2, :].unsqueeze(1).to_broadcast([P, NT, NE]), ALU.add))
            burst(nc.vector.tensor_tensor(pick[:, r], pick[:, r], sel[:], ALU.mult) for r in range(2))
            burst(nc.vector.tensor_reduce(posf[:, r], pick[:, r], AX.X, ALU.add) for r in range(2))
            nc.vector.tensor_copy(pos[:], posf[:]).then_inc(sem("route_ready"), 1)
            then(nc.vector.tensor_tensor(eidg[:], cst["iota"].unsqueeze(2).to_broadcast([P, 16, NE - 1]),
                                         tl[:, 1, 0:NE - 1].unsqueeze(1).to_broadcast([P, 16, NE - 1]), ALU.is_ge))
            then(nc.vector.tensor_reduce(eidf[:], eidg[:], AX.X, ALU.add))
            nc.vector.tensor_copy(eid[:], eidf[:]).then_inc(sem("route_ready"), 1)
            def split_low(k):
                cols = slice(2048 * (k % 2), 2048 * (k % 2) + 2048)
                dve.wait_ge(sem("w_hi"), k - POOL_HALVES + 1)
                nc.vector.tensor_tensor(wsp[:, k // 2, 1, cols], wraw[:, k % 2, :], wsp[:, k // 2, 0, cols], ALU.subtract).then_inc(sem("w_split_dve"), 1)

            for k in range(10, 14):
                split_low(k)
            for k in range(4):
                dve.wait_ge(sem("gate_psum"), k + 6)
                xt = x[:, 2 * k:2 * k + 2, :].rearrange("p t d -> p (t d)")
                nc.vector.tensor_tensor(xt, xt, bank[k][:], ALU.add).then_inc(sem("b3_added"), 1)
            split_low(14)
            split_low(15)
            dve.wait_ge(sem("b3_added"), 4)
            dve.sem_inc(sem("h2_lo"), CREDIT)
            dve.sem_inc(sem("xgT_split"), 1)

            def split_rows(i, u):
                dve.wait_ge(sem("xgT_psum"), i * 2 + (u + 1))
                nc.vector.tensor_copy(xgT[:, u, 0].rearrange("p c n -> p (c n)"), bank[6][:]).then_inc(sem("xgT_hi"), 1)
                dve.wait_ge(sem("xgT_hi"), i * 2 + (u + 1))
                nc.vector.tensor_tensor(xgT[:, u, 1].rearrange("p c n -> p (c n)"), bank[6][:], xgT[:, u, 0].rearrange("p c n -> p (c n)"),
                                        ALU.subtract).then_inc(sem("xgT_split"), 1)

            def split_hidden(layer, i, u):
                h = h1 if layer == 1 else h2
                for p in range(2):
                    n = i * 4 + (2 * u + p)
                    hi = h[:, 0, 2 * p:2 * p + 2, :].rearrange("p f n -> p (f n)")
                    dve.wait_ge(sem(f"h{layer}_f32"), n + (1 + CREDIT))
                    nc.vector.tensor_copy(hi, hf[:, p, :]).then_inc(sem("h_hi"), 1)
                    dve.wait_ge(sem("h_hi"), i * 8 + (4 * u + 2 * layer + p - 1))
                    nc.vector.tensor_tensor(h[:, 1, 2 * p:2 * p + 2, :].rearrange("p f n -> p (f n)"), hf[:, p, :], hi, ALU.subtract).then_inc(sem(f"h{layer}_lo"), 1)

            split_rows(0, 0)
            split_rows(0, 1)
            split_hidden(1, 0, 0)
            with dve.Fori(0, ET // 2 - 1) as i:
                for u in range(2):
                    split_hidden(2, i, u)
                    split_hidden(1, i + u, 1 - u)
                    split_rows(i + 1, u)
            last = ET // 2 - 1
            split_hidden(2, last, 0)
            split_hidden(1, last, 1)
            split_rows(last + 1, 0)
            split_hidden(2, last, 1)
            split_hidden(1, last + 1, 0)
            split_hidden(2, last + 1, 0)

            def add_experts():
                for t in range(NT):
                    for r in range(2):
                        dve.wait_ge(sem(f"gathered{t // 4}"), 16 * 8)
                        add = nc.vector.scalar_tensor_tensor(x[:, t, :], yg[:, t, r, :], top[:, t, r:r + 1], x[:, t, :], ALU.mult, ALU.add)
                        if r:
                            add.then_inc(sem("x3_added"), 1)
                            stats(4, t)
                        else:
                            then(add)

            def add_tile(i, u):
                dve.wait_ge(sem("out4_psum"), i * 2 + (u + 1))
                xt = x[:, bass.ds(i * 2 + u, 1), :].rearrange("p t d -> p (t d)")
                nc.vector.tensor_tensor(xt, xt, bank[7][:, 0:D], ALU.add).then_inc(sem("x4_added"), 1)

            def copy_p5T_even(i, j):
                u, g = j // 4, j % 4
                dve.wait_ge(sem("pt5_psum"), i * 8 + (j + 1))
                nc.vector.tensor_copy(p5T[:, u, 4 * g:4 * g + 4, :].rearrange("p h n -> p (h n)"), bank[3][:]).then_inc(sem("p5T_dve"), 1)

            def project(i, u):
                def step(n, ins):
                    ins.then_inc(sem("o5_step"), 1)
                    dve.wait_ge(sem("o5_step"), i * 16 + (7 * u + n))
                dve.wait_ge(sem("pv5_psum"), i * 2 + (u + 1))
                step(1, nc.vector.reciprocal(i5[:, u, :], r5[:, u, :]))
                step(2, nc.vector.tensor_tensor(o5[:, u, :].rearrange("p (h d) -> p h d", h=H4), bank[(7, 0)[u]][:, 0:D].rearrange("p (h d) -> p h d", h=H4),
                                                i5[:, u, :].unsqueeze(2).to_broadcast([P, H4, 16]), ALU.mult))
                step(3, nc.vector.tensor_reduce(osc[:, u, 0:1], o5[:, u, :], AX.X, ALU.max, apply_absolute_value=True))
                step(4, nc.vector.tensor_scalar(osc[:, u, 1:2], osc[:, u, 0:1], 1.0 / 127.0, 1e-8, ALU.mult, ALU.max))
                step(5, nc.vector.reciprocal(osc[:, u, 2:3], osc[:, u, 1:2]))
                step(6, nc.vector.tensor_scalar(oq[:, u, :], o5[:, u, :], osc[:, u, 2:3], ROUND, ALU.mult, ALU.add))
                step(7, nc.vector.tensor_scalar(oq[:, u, :], oq[:, u, :], -ROUND, 127.0, ALU.add, ALU.min))
                nc.vector.tensor_scalar(oi[:, u, :], oq[:, u, :], -127.0, None, ALU.max).then_inc(sem("oi_ready"), 1)

            add_experts()
            layernorm(4)
            xnT_copies(4)
            def scales(dst_scale, dst_inverse, largest, floor):
                then(nc.vector.tensor_scalar(dst_scale, largest, 1.0 / 127.0, 1e-8 if floor else EPS, ALU.mult, ALU.max if floor else ALU.add))
                then(nc.vector.reciprocal(dst_inverse, dst_scale))

            dve.wait_ge(sem("w5_loaded"), 112)
            ew4 = ew[:].rearrange("p w c n -> p (w c) n")
            then(nc.vector.tensor_reduce(esc[:, 0, :], ew4, AX.X, ALU.max, apply_absolute_value=True))
            scales(esc[:, 1, :], esc[:, 2, :], esc[:, 0, :], True)
            for k in range(4):
                then(nc.vector.tensor_scalar(ediag[:, k, :], cst["ident"], esc[:, 1, k:k + 1], None, ALU.mult))
                then(nc.vector.tensor_scalar(eqf[:, k, :], ew4[:, k, :], esc[:, 2, k:k + 1], ROUND, ALU.mult, ALU.add))
            then(nc.vector.tensor_scalar(eqf[:], eqf[:], -ROUND, 127.0, ALU.add, ALU.min))
            nc.vector.tensor_scalar(eqi[:], eqf[:], -127.0, None, ALU.max).then_inc(sem("eqi_ready"), 1)
            dve.sem_inc(sem("s4_masked"), 2)
            dve.sem_inc(sem("pT_ready"), 2)
            dve.sem_inc(sem("x4_added"), 1)

            def rope_k(i, u):
                kv = bank[0][:, P:2 * P]
                pe_ = kv[:, 64:128].rearrange("p (f two) -> p f two", two=2)
                sn_ = cst["sin"].rearrange("p (f two) -> p f two", two=2)
                turned = rk[:, 1].rearrange("p (f two) -> p f two", two=2)
                dve.wait_ge(sem("kvn_psum"), i * 2 + (u + 1))
                nc.vector.tensor_copy(kvr[:, u, 0:64], kv[:, 0:64]).then_inc(sem("rk_step"), 1)
                nc.vector.tensor_tensor(rk[:, 0], kv[:, 64:128], cst["cos"], ALU.mult).then_inc(sem("rk_step"), 1)
                for two in range(2):
                    nc.vector.tensor_tensor(turned[:, :, two], pe_[:, :, 1 - two], sn_[:, :, two], ALU.mult).then_inc(sem("rk_step"), 1)
                dve.wait_ge(sem("rk_step"), i * 8 + (4 * u + 4))
                nc.vector.tensor_tensor(kvr[:, u, 64:128], rk[:, 0], rk[:, 1], ALU.add).then_inc(sem("kvr_ready"), 1)

            causal = cst["causal"].unsqueeze(1).to_broadcast([P, 4, P])
            steps = [(u, g) for u in range(2) for g in range(4)]

            def invert(i, j):
                u, g = steps[j]
                dve.wait_ge(sem("exp_ready"), i * 8 + (j + 1))
                nc.vector.reciprocal(rinv[:, u, 4 * g:4 * g + 4], rsum[:, u, 4 * g:4 * g + 4]).then_inc(sem("r4_ready"), 1)

            def pair4(i, after):
                for j, (u, g) in enumerate(steps):
                    hs = slice(4 * g, 4 * g + 4)
                    dve.wait_ge(sem("s4_psum"), i * 8 + (j + 1))
                    nc.vector.scalar_tensor_tensor(sm[:, u, hs, :], bank[5 + g % 2][:].rearrange("p (h n) -> p h n", h=4), S4, causal,
                                                   ALU.mult, ALU.add).then_inc(sem("s4_masked"), 1)
                    dve.wait_ge(sem("s4_masked"), i * 8 + (j + 3))
                    nc.vector.tensor_reduce(nm[:, u, hs], sm[:, u, hs, :], AX.X, ALU.max, negate=True).then_inc(sem("nm_ready"), 1)
                    if j >= 2:
                        invert(i, j - 2)
                    if j >= 3:
                        copy_pT(i, j - 3)
                invert(i, 6)
                invert(i, 7)
                for j in range(5, 8):
                    copy_pT(i, j)
                if after is None:
                    for t in range(NT - 2):
                        stats(5, t)
                for u in range(2):
                    if after is not None:
                        rope_k(after, u)
                    add_tile(i, u)

            def copy_pT(i, j):
                u, g = steps[j]
                dve.wait_ge(sem("pt4_psum"), i * 8 + (j + 1))
                nc.vector.tensor_copy(pT[:, u, 4 * g:4 * g + 4, :].rearrange("p h n -> p (h n)"), bank[3 + g % 2][:]).then_inc(sem("pT_ready"), 1)

            for u in range(2):
                rope_k(0, u)
            with dve.Fori(0, NT // 2 - 1) as i:
                pair4(i, i + 1)
            pair4(NT // 2 - 1, None)
            layernorm(5)

            def quantise_x(s, low):
                dve.wait_ge(sem("xn_ready"), NT * s)
                then(nc.vector.tensor_reduce(xsc[:, 0, :], xn[:], AX.X, ALU.max, apply_absolute_value=True))
                scales(xsc[:, 1, :], xsc[:, 2, :], xsc[:, 0, :], s == 5)
                if s == 6:
                    dve.sem_inc(sem("xn_scaled"), 1)
                burst(nc.vector.tensor_scalar(xn[:, t, :], xn[:, t, :], xsc[:, 2, t:t + 1], ROUND, ALU.mult, ALU.add)
                      for t in range(SCALED_BY_VECTOR if s == 6 else NT))
                if s == 6:
                    dve.wait_ge(sem("xn_scaled"), 1 + NT - SCALED_BY_VECTOR)
                then(nc.vector.tensor_scalar(xn[:], xn[:], -ROUND, 127.0, ALU.add, ALU.min))
                nc.vector.tensor_scalar(xi[:], xn[:], low, None, ALU.max).then_inc(sem("xi_ready"), 1)

            def xiT_copy(s):
                dve.wait_ge(sem("xiT_psum"), 2 * (s - 5) + 2)
                nc.vector.tensor_copy(xiT[:, 1].rearrange("p t s -> p (t s)"), bank[5 if s == 5 else 1][:].bitcast(BF16)).then_inc(sem("xiT_ready"), 1)

            quantise_x(5, -127.0)
            xiT_copy(5)
            dve.wait_ge(sem("prep5_ready"), 8)
            for t in range(NT):
                dve.wait_ge(sem("q5_psum"), t // 2 + 1)
                then(nc.vector.scalar_tensor_tensor(q5[:, t, :], bank[4 + t // 2][:, D * (t % 2):D * (t % 2) + D], xsc[:, 1, t:t + 1], ewb[:, 0, :],
                                                    ALU.mult, ALU.mult))
                nc.vector.tensor_tensor(q5[:, t, :], q5[:, t, :], bq5[:], ALU.add).then_inc(sem("q5_ready"), 1)
            for k in range(4):
                dve.wait_ge(sem("v5_psum"), k + 1)
                nc.vector.tensor_tensor(v5[:, 2 * k:2 * k + 2, :], bank[k][:].rearrange("p (t n) -> p t n", t=2),
                                        bv5[:].unsqueeze(1).to_broadcast([P, 2, D]), ALU.add).then_inc(sem("v5_ready"), 1)
            dve.wait_ge(sem("prep5_psum"), 9)
            then(nc.vector.tensor_scalar(fws[:, 2, :], bank[0][:, 0:3], 1.0 / (1024 * D), EPS, ALU.mult, ALU.add))
            nc.vector.reciprocal(fws[:, 3, :], fws[:, 2, :]).then_inc(sem("w6_scale"), 1)
            dve.sem_inc(sem("p5T_dve"), 1)
            dve.sem_inc(sem("x5_added"), 1)
            dve.wait_ge(sem("q5T_ready"), 4)
            dve.wait_ge(sem("x_biased"), 1)

            def add_outputs5(i):
                dve.wait_ge(sem("out5_psum"), i + 1)
                for u in range(2):
                    nc.vector.scalar_tensor_tensor(ot[:, u, :], bank[2][:, D * u:D * u + D], osc[:, u, 1:2], ewb[:, 1, :], ALU.mult, ALU.mult).then_inc(sem("o5_step"), 1)
                for u in range(2):
                    dve.wait_ge(sem("o5_step"), i * 16 + (15 + u))
                    xt = x[:, bass.ds(i * 2 + u, 1), :].rearrange("p t d -> p (t d)")
                    nc.vector.tensor_tensor(xt, xt, ot[:, u, :], ALU.add).then_inc(sem("x5_added"), 1)

            def slot_values(i, u):
                nc.vector.tensor_copy(v5s[:, u, :], v5[:, bass.ds(i * 2 + u, 1), :].rearrange("p t d -> p (t d)")).then_inc(sem("v5s_ready"), 1)

            def pair5(i, before):
                for u in range(2):
                    dve.wait_ge(sem("s5_psum"), i * 8 + (4 * u + 4))
                    nc.vector.tensor_copy(q5s[:, u], q5T[:, :, bass.ds(i * 2 + u, 1), :].rearrange("p c t s -> p c (t s)")).then_inc(sem("q5s_ready"), 1)
                slot_values(i, 0)
                for j in range(8):
                    u, g = j // 4, j % 4
                    dve.wait_ge(sem("s5_psum"), i * 8 + (j + 9))
                    nc.vector.tensor_reduce(n5[:, u, 4 * g:4 * g + 4], bank[5 + g % 2][:].rearrange("p (h n) -> p h n", h=4), AX.X, ALU.max,
                                            negate=True).then_inc(sem("n5_ready"), 1)
                    if j == 2:
                        if before is not None:
                            project(before, 1)
                        slot_values(i, 1)
                    if j == 7 and before is not None:
                        add_outputs5(before)
                    if j % 2:
                        copy_p5T_even(i, j - 1)
                project(i, 0)

            pair5(0, None)
            with dve.Fori(0, NT // 2 - 1) as i:
                pair5(i + 1, i)
            project(NT // 2 - 1, 1)

            for t in range(NT - 2):
                stats(6, t)
            add_outputs5(NT // 2 - 1)
            layernorm(6)
            quantise_x(6, -128.0)
            burst(nc.vector.tensor_scalar(fsg[:, :, w], xsc[:, 1, :], fws[:, 2, w:w + 1], None, ALU.mult) for w in range(2))
            xiT_copy(6)
            dve.sem_inc(sem("x6_added"), 2)

            def scales6(i, u):
                nc.vector.tensor_copy(fsn[:, u, :], fsg[:, bass.ds(i * 2 + u, 1), :].rearrange("p t w -> p (t w)")).then_inc(sem("fsn_ready"), 1)

            def gated(i, u):
                def step(n, ins):
                    ins.then_inc(sem("f_step"), 1)
                    dve.wait_ge(sem("f_step"), i * 10 + (5 * u + n))
                dve.wait_ge(sem("fsn_ready"), i * 2 + (u + 1))
                dve.wait_ge(sem("gu_psum"), i * 4 + (2 * u + 2))
                for k in range(2):
                    dve.wait_ge(sem("silu_ready"), i * 4 + (2 * u + k + 1))
                    ins = nc.vector.scalar_tensor_tensor(fh[:, u, 512 * k:512 * k + 512], bank[4 + k][:], fsn[:, u, 1:2], fg[:, u, 512 * k:512 * k + 512],
                                                         ALU.mult, ALU.mult)
                    step(k + 1, ins)
                step(3, nc.vector.tensor_reduce(fsd[:, u, 0:1], fh[:, u, :], AX.X, ALU.max, apply_absolute_value=True))
                step(4, nc.vector.tensor_scalar(fsd[:, u, 1:2], fsd[:, u, 0:1], 1.0 / 127.0, EPS, ALU.mult, ALU.add))
                nc.vector.reciprocal(fsd[:, u, 2:3], fsd[:, u, 1:2]).then_inc(sem("f_step"), 1)

            def quantised(i, u):
                dve.wait_ge(sem("fq_ready"), i * 2 + (u + 1))
                nc.vector.tensor_scalar(fsd[:, u, 3:4], fsd[:, u, 1:2], fws[:, 2, 2:3], None, ALU.mult).then_inc(sem("fq_step"), 1)
                nc.vector.tensor_scalar(fq[:, u, :], fq[:, u, :], -ROUND, 127.0, ALU.add, ALU.min).then_inc(sem("fq_step"), 1)
                dve.wait_ge(sem("fq_step"), i * 4 + (2 * u + 2))
                nc.vector.tensor_scalar(fhi[:, u, :], fq[:, u, :], -128.0, None, ALU.max).then_inc(sem("fhi_ready"), 1)

            def add_down(i, u):
                dve.wait_ge(sem("down_psum"), i * 2 + (u + 1))
                xt = x[:, bass.ds(i * 2 + u, 1), :].rearrange("p t d -> p (t d)")
                nc.vector.scalar_tensor_tensor(xt, bank[7][:, 0:D], fsd[:, u, 3:4], xt, ALU.mult, ALU.add).then_inc(sem("x6_added"), 1)

            last = NT // 2 - 1
            scales6(0, 0)
            scales6(0, 1)
            gated(0, 0)
            scales6(1, 0)
            gated(0, 1)
            quantised(0, 0)
            with dve.Fori(0, last - 1) as i:
                for u in range(2):
                    scales6(i + 1 + u, 1 - u)
                    gated(i + 1, u)
                    add_down(i, u)
                    quantised(i + u, 1 - u)
            scales6(last, 1)
            gated(last, 0)
            add_down(last - 1, 0)
            quantised(last - 1, 1)
            gated(last, 1)
            add_down(last - 1, 1)
            quantised(last, 0)
            quantised(last, 1)
            add_down(last, 0)
            add_down(last, 1)

        @block.tensor
        def _(pe):
            ident = cst["ident"]

            def transposes(s):
                for half in range(2):
                    for c in range(DC):
                        pe.wait_ge(sem("xn_ready"), NT * (s - 1) + 4 * half + 4)
                        for k in range(4):
                            last = nc.tensor.transpose(bank[2 * half + c][:, P * k:P * k + P], xn[:, 4 * half + k, P * c:P * c + P], ident)
                        last.then_inc(sem("xnT_psum"), 1)

            def all_xnT(s):
                pe.wait_ge(sem("xnT_act"), 2 * s)
                pe.wait_ge(sem("xnT_dve"), 2 * s)

            pe.wait_ge(sem("const_loaded"), 32)
            pe.wait_ge(sem("w1_loaded"), 48)
            for oc in range(DC):
                for dc in range(DC):
                    last = nc.tensor.transpose(bank[4][:, D * oc + P * dc:D * oc + P * dc + P], wo[:, dc, P * oc:P * oc + P], ident)
            last.then_inc(sem("prep1_psum"), 1)
            for ic in range(DC):
                for w, src in enumerate((wq, wkv)):
                    for oc in range(DC):
                        last = nc.tensor.matmul(bank[5 + ic][:, D * w:D * w + D], src[:, oc, P * ic:P * ic + P],
                                                cst["fourier"][:, D * oc:D * oc + D], start=(oc == 0), stop=(oc == DC - 1))
                last.then_inc(sem("prep1_psum"), 1)
            transposes(1)
            all_xnT(1)
            pe.wait_ge(sem("prep1_ready"), 3)
            for t in range(NT):
                if t >= 4:
                    pe.wait_ge(sem("qk_ready"), t - 3)
                for c in range(DC):
                    last = nc.tensor.matmul(bank[t % 4][:], xnT[:, c, t, :], toF[:, c, :], start=(c == 0), stop=(c == DC - 1))
                last.then_inc(sem("qk_psum"), 1)
            pe.wait_ge(sem("prep1_ready"), 1)
            for part in range(3):
                dst = (bank[7][:, 0:D], bank[7][:, D:2 * D], bank[4][:, 0:D])[part]
                for oc in range(DC):
                    last = nc.tensor.matmul(dst, cst["inverse"][:, 384 * oc + P * part:384 * oc + P * part + P], woT[:, oc, :],
                                            start=(oc == 0), stop=(oc == DC - 1))
                if part:
                    last.then_inc(sem("prep1_psum"), 1)
            pe.wait_ge(sem("prep1_ready"), 5)

            def attention_out(t):
                pe.wait_ge(sem("products_ready"), t + 1)
                if t >= 4:
                    pe.wait_ge(sem("x1_added"), t - 3)
                for j in range(4):
                    last = nc.tensor.matmul(bank[t % 4][:, 0:D], pr[:, t % 2, j, :], toO[:, min(j, 2), :], start=(j == 0), stop=(j == 3))
                last.then_inc(sem("attn_psum"), 1)

            for t in range(NT):
                b = bank[4 + t % 4]
                pe.wait_ge(sem("qkn_ready"), 2 * t + 2)
                if t >= 4:
                    pe.wait_ge(sem("kqT_ready"), t - 3)
                for part in range(2):
                    nc.tensor.matmul(b[:, P * part:P * part + P], qk[:, t, D + P * part:D + P * part + P], cst["upper"], start=True, stop=True)
                for part in range(2):
                    last = nc.tensor.transpose(b[:, D + P * part:D + P * part + P], qk[:, t, P * part:P * part + P], ident)
                last.then_inc(sem("kq_psum"), 1)
                if t >= 1:
                    attention_out(t - 1)
            attention_out(NT - 1)
            pe.wait_ge(sem("kqT_ready"), NT)
            pe.wait_ge(sem("s2_loaded"), 16 * (HG + 2))
            for k in range(8):
                if k >= 2:
                    pe.wait_ge(sem("tap_ready"), k - 1)
                nc.tensor.matmul(bank[4 + k % 2][:], cst["reverse"], tapR[:, 2 * k:2 * k + 2, :].rearrange("p h n -> p (h n)"),
                                 start=True, stop=True).then_inc(sem("tap_psum"), 1)
            for half in range(2):
                for c in range(DC):
                    if half:
                        pe.wait_ge(sem("cxT_ready"), c + 1)
                    for k in range(4):
                        last = nc.tensor.transpose(bank[6 + c][:, P * k:P * k + P], cx[:, 4 * half + k, P * c:P * c + P], ident)
                    last.then_inc(sem("cxT_psum"), 1)
            transposes(2)
            pe.wait_ge(sem("tap_ready"), 8)
            pe.wait_ge(sem("cxT_ready"), 4)
            for k in range(4):
                pe.wait_ge(sem("wsk_ready"), k + 1)
                nc.tensor.matmul(bank[4 + k][:], cst["group8"], wsk[:, 2 * k:2 * k + 2, :].rearrange("p t d -> p (t d)"),
                                 start=True, stop=True).then_inc(sem("skip_psum"), 1)
            all_xnT(2)
            for h in range(HG):
                pe.wait_ge(sem("kvp_ready"), 2 * h + 2)
                if h >= 2:
                    pe.wait_ge(sem("yx_ready"), 2 * (h - 1))
                nc.tensor.matmul(bank[2 * (h % 2)][:], tap[:, h, 0:P], kvp[:, h % 2, 0, :], start=True, stop=True).then_inc(sem("conv_psum"), 1)
                nc.tensor.matmul(bank[2 * (h % 2) + 1][:], tap[:, h, P:2 * P], kvp[:, h % 2, 0, :], start=True, stop=False)
                nc.tensor.matmul(bank[2 * (h % 2) + 1][:], tap[:, h, 0:P], kvp[:, h % 2, 1, :], start=False, stop=True).then_inc(sem("conv_psum"), 1)
            pe.wait_ge(sem("yT_ready"), 2 * HG)
            pe.wait_ge(sem("skip_added"), 4)
            for k in range(4):
                for tt in range(2):
                    for c in range(DC):
                        last = nc.tensor.transpose(bank[4 + k][:, D * tt + P * c:D * tt + P * c + P], yT[:, c, 2 * k + tt, :], ident)
                last.then_inc(sem("conv_out_psum"), 1)
            pe.wait_ge(sem("gate_loaded"), 80)
            pe.wait_ge(sem("x2_added"), 4)
            nc.tensor.transpose(bank[4][:, 0:64], b12[:, :], ident[0:64, 0:64]).then_inc(sem("gate_psum"), 1)
            transposes(3)
            all_xnT(3)
            for t in range(NT):
                for c in range(DC):
                    last = nc.tensor.matmul(bank[7][:, NE * t:NE * t + NE], xnT[:, c, t, :], wg[:, c, :], start=(c == 0), stop=(c == DC - 1))
            last.then_inc(sem("gate_psum"), 1)
            pe.wait_ge(sem("route_ready"), 2)
            pe.wait_ge(sem("gate_act"), 1)
            for k, m in enumerate(("upper", "ones")):
                last = nc.tensor.matmul(bank[4][:, 64 * k:64 * k + 64], cst[m], sel[:].rearrange("p t e -> p (t e)"), start=True, stop=True)
            last.then_inc(sem("gate_psum"), 1)
            pe.wait_ge(sem("route_ready"), 3)
            for t in range(NT):
                last = nc.tensor.transpose(bank[5 + t // 4][0:NE, P * (t % 4):P * (t % 4) + P], comb[:, t, :], ident)
                if t % 4 == 3:
                    last.then_inc(sem("gate_psum"), 1)
            pe.wait_ge(sem("gate_act"), 4)
            for t in range(NT):
                last = nc.tensor.matmul(bank[t // 2][:, D * (t % 2):D * (t % 2) + D], combT[:, t, :], b3[:, :], start=True, stop=True)
                if t % 2:
                    last.then_inc(sem("gate_psum"), 1)
            pe.wait_ge(sem("b3_added"), 4)
            pe.wait_ge(sem("route_ready"), 5)

            def turn_rows(i, u):
                pe.wait_ge(sem(f"xg{u}_loaded"), i * 16 + 16)
                pe.wait_ge(sem("xgT_split"), i * 2 + (u + 1))
                for c in range(DC):
                    for b in range(2):
                        last = nc.tensor.transpose(bank[6][:, SLOTS * c + P * b:SLOTS * c + P * b + P], xg[:, u, b, P * c:P * c + P], ident)
                last.then_inc(sem("xgT_psum"), 1)

            def expert_weights(e, cols, chunks):
                return [wsp[:, bass.ds(e, 1), part, cols].rearrange("p e (c n) -> p (e c) n", c=chunks) for part in range(2)]

            passes = ((0, 0), (0, 1), (1, 0))

            def layer(n_layer, i, u, e):
                chunks, cols, inp = ((DC, W1, xgT[:, u]), (FC, W2, h1))[n_layer - 1]
                w = expert_weights(e, cols, chunks)
                for p in range(2):
                    n = i * 4 + (2 * u + p)
                    b = bank[2 * (n_layer - 1) + p]
                    pe.wait_ge(sem(f"h{n_layer}_f32"), n + 1)
                    for f in range(2 * p, 2 * p + 2):
                        for c in range(chunks):
                            if n_layer == 1:
                                pe.wait_ge(sem("xgT_split"), i * 2 + (u + 2))
                            elif f == 0:
                                pe.wait_ge(sem("h1_lo"), i * 4 + (2 * u + c // 2 + 1))
                            for a_, b_ in passes:
                                last = nc.tensor.matmul(b[:, SLOTS * (f % 2):SLOTS * (f % 2) + SLOTS], w[a_][:, c, P * f:P * f + P], inp[:, b_, c, :],
                                                        start=(c == 0 and a_ + b_ == 0), stop=(c == chunks - 1 and a_ == 1))
                    last.then_inc(sem(f"l{n_layer}_psum"), 1)

            def layer3(i, u, e):
                w = expert_weights(e, W3, FC)
                pe.wait_ge(sem("y_ready"), i * 2 + (u + 1))
                for b in range(2):
                    for c in range(FC):
                        if b == 0:
                            pe.wait_ge(sem("h2_lo"), i * 4 + (2 * u + c // 2 + 1 + CREDIT))
                        for a_, b_ in passes:
                            last = nc.tensor.matmul(bank[4 + u][:, D * b:D * b + D], h2[:, b_, c, P * b:P * b + P], w[a_][:, c, :],
                                                    start=(c == 0 and a_ + b_ == 0), stop=(c == FC - 1 and a_ == 1))
                last.then_inc(sem("l3_psum"), 1)

            def expert_of(i, u):
                return pe.value_load(eid[0:1, bass.ds(i * 2 + u, 1)], min_val=0, max_val=NE - 1)

            turn_rows(0, 0)
            turn_rows(0, 1)
            pe.wait_ge(sem("w_split"), 10)
            pe.wait_ge(sem("w_split_dve"), 6)
            layer(1, 0, 0, expert_of(0, 0))
            with pe.Fori(0, ET // 2 - 1) as i:
                for u in range(2):
                    e, e_next = expert_of(i, u), expert_of(i + u, 1 - u)
                    layer(2, i, u, e)
                    layer(1, i + u, 1 - u, e_next)
                    layer3(i, u, e)
                    turn_rows(i + 1, u)
            for j in range(ET - 3, ET):
                i, u = j // 2, j % 2
                e = expert_of(i, u)
                layer(2, i, u, e)
                if j + 1 < ET:
                    layer(1, i + u, 1 - u, expert_of(i + u, 1 - u))
                layer3(i, u, e)
                if j + 2 < ET:
                    turn_rows(i + 1, u)
            pe.wait_ge(sem("y_ready"), ET + CREDIT)
            pe.wait_ge(sem("w4_loaded"), 96)

            def prep_copied(n):
                pe.wait_ge(sem("prep4_act"), n)

            i64 = ident[0:64, 0:64]
            for k in range(2):
                for j in range(8):
                    last = nc.tensor.transpose(bank[k][0:64, 64 * j:64 * j + 64], wkvb[:, 8 * k + j, 0:64], i64)
                last.then_inc(sem("prep4_psum"), 1)
            for k in range(2):
                for j in range(8):
                    last = nc.tensor.transpose(bank[2 + k][:, 64 * j:64 * j + 64], wkvb[:, 8 * k + j, 64:192], i64)
                last.then_inc(sem("prep4_psum"), 1)
            for k in range(4):
                for j in range(4):
                    last = nc.tensor.transpose(bank[4 + k][0:64, P * j:P * j + P], wqb[:, 0, 4 * k + j, 0:64], ident)
                last.then_inc(sem("prep4_psum"), 1)
            prep_copied(2)
            for k in range(2):
                for j in range(8):
                    last = nc.tensor.transpose(bank[k][0:64, 64 * j:64 * j + 64], wqb[0:64, 1, 8 * k + j, 0:64], i64)
                last.then_inc(sem("prep4_psum"), 1)
            prep_copied(10)
            for lo, hi, at in ((0, P, 2), (P, QL, 4)):
                for k in range(2):
                    for j in range(8):
                        h = 8 * k + j
                        last = nc.tensor.matmul(bank[at + k][0:hi - lo, 64 * j:64 * j + 64], wqbT[:, h, lo:hi], wkT[:, h, :], start=True, stop=True)
                    last.then_inc(sem("prep4_psum"), 1)
            pe.wait_ge(sem("wo4b_loaded"), 16)
            for k in range(4):
                for j in range(2):
                    for odd in range(2):
                        h = 4 * k + 2 * j + odd
                        last = nc.tensor.matmul(bank[(6, 7, 0, 1)[k]][64 * odd:64 * odd + 64, D * j:D * j + D], wvT[:, h, :], (wo4a, wo4b)[h // 8][:, h % 8, :], start=True, stop=True)
                last.then_inc(sem("prep4_psum"), 1)
            prep_copied(18)
            transposes(4)
            all_xnT(4)

            def latents(i):
                two = bass.ds(i * 2, 2)
                for dst, w in ((bank[0][:, 0:2 * P], wqa[:, :, 0:P]), (bank[0][0:64, 2 * P:4 * P], wqa[:, :, P:QL])):
                    for c in range(DC):
                        last = nc.tensor.matmul(dst, w[:, c, :], xnT[:, c, two, :].rearrange("p t s -> p (t s)"), start=(c == 0), stop=(c == DC - 1))
                last.then_inc(sem("lat_psum"), 1)

            def key_latents(i, u):
                t = bass.ds(i * 2 + u, 1)
                for c in range(DC):
                    last = nc.tensor.matmul(bank[0][:, 0:P], wkva[:, c, :], xnT[:, c, t, :].rearrange("p t s -> p (t s)"), start=(c == 0), stop=(c == DC - 1))
                last.then_inc(sem("kv_psum"), 1)

            def turn_kv(i, u):
                pe.wait_ge(sem("kvT_ready"), i * 2 + (u + 1))
                nc.tensor.transpose(bank[0][:, P:2 * P], kvT[:, u, :], ident).then_inc(sem("kvn_psum"), 1)

            def turn_keys(i):
                pe.wait_ge(sem("kvr_ready"), i * 2 + 2)
                for u in range(2):
                    last = nc.tensor.transpose(bank[0][:, 2 * P + P * u:3 * P + P * u], kvr[:, u, :], ident)
                last.then_inc(sem("kT_psum"), 1)

            def queries(i, j):
                u, g = j // 4, j % 4
                hs = slice(4 * g, 4 * g + 4)
                if j == 0:
                    pe.wait_ge(sem("lat_copied"), i + 1)
                pe.wait_ge(sem("q4_copied"), i * 8 + (j + 1))
                nc.tensor.matmul(bank[1 + g % 2][:], ql0[:, u, :], wqb[:, 0, hs, :].rearrange("p h n -> p (h n)"), start=True, stop=False)
                nc.tensor.matmul(bank[1 + g % 2][:], ql1[:, u, :], wqb[0:64, 1, hs, :].rearrange("p h n -> p (h n)"), start=False, stop=True).then_inc(sem("q4_psum"), 1)

            def turn_q(i, u, g):
                pe.wait_ge(sem("roped"), i * 8 + (4 * u + g + 1))
                j = 4 * u + g
                if j < 2:
                    pe.wait_ge(sem("pT_ready"), i * 8 + (j + 1))
                elif j < 6:
                    pe.wait_ge(sem("qT_ready"), i * 8 + (j - 1))
                else:
                    pe.wait_ge(sem("pT_ready"), i * 8 + (j - 3))
                for k in range(4):
                    last = nc.tensor.transpose(bank[3 + g % 2][:, P * k:P * k + P], qs[:, u, 4 * g + k, :], ident)
                last.then_inc(sem("t4_psum"), 1)

            def scores(i, u, g):
                pe.wait_ge(sem("qT_ready"), i * 8 + (4 * u + g + 1))
                pe.wait_ge(sem("kT_ready"), i + 1)
                pe.wait_ge(sem("s4_masked"), i * 8 + (4 * u + g + 1))
                for k in range(4):
                    last = nc.tensor.matmul(bank[5 + g % 2][:, P * k:P * k + P], qT[:, u, 4 * g + k, :], kT[:, u, :], start=True, stop=True)
                last.then_inc(sem("s4_psum"), 1)

            def turn_p(i, u, g):
                pe.wait_ge(sem("p4_ready"), i * 8 + (4 * u + g + 1))
                if u == 0:
                    pe.wait_ge(sem("qT_ready"), i * 8 + (g + 5))
                else:
                    pe.wait_ge(sem("pT_ready"), i * 8 + (4 * u + g + 1))
                for k in range(4):
                    last = nc.tensor.transpose(bank[3 + g % 2][:, P * k:P * k + P], sm[:, u, 4 * g + k, :], ident)
                last.then_inc(sem("pt4_psum"), 1)

            def values(i, u, after):
                pe.wait_ge(sem("x4_added"), i * 2 + (u + 1))
                if after is None:
                    pe.wait_ge(sem("oT_ready" if u else "kT_ready"), i * 4 + 2 if u else i + 1)
                elif u == 0:
                    pe.wait_ge(sem("lat_copied"), after + 1)
                else:
                    pe.wait_ge(sem("kvr_ready"), after * 2 + 1)
                pe.wait_ge(sem("pT_ready"), i * 8 + (4 * u + 6))
                pairs = pT[:, u].rearrange("p (j odd) s -> p odd j s", odd=2)
                for k in range(2):
                    for odd in range(2):
                        last = nc.tensor.matmul(bank[7 if k == 0 else 0][64 * odd:64 * odd + 64, :], kvr[:, u, 0:64], pairs[:, odd, 4 * k:4 * k + 4, :], start=True, stop=True)
                    last.then_inc(sem("pv_psum"), 1)

            def output(i, u, lo, hi):
                pe.wait_ge(sem("oT_ready"), i * 4 + (2 * u + 1 + (lo >= 4)))
                for j in range(lo, hi):
                    last = nc.tensor.matmul(bank[7][:, 0:D], oT[:, u, j, :], wvo[:, j, :], start=(j == 0), stop=(j == H4 // 2 - 1))
                if hi == H4 // 2:
                    last.then_inc(sem("out4_psum"), 1)

            def pair4(i, after):
                turn_q(i, 0, 0)
                turn_keys(i)
                turn_q(i, 0, 1)
                if after is not None:
                    pe.wait_ge(sem("kT_ready"), i + 1)
                    latents(after)
                for j in range(1, 8):
                    if j >= 2:
                        turn_q(i, j // 4, j % 4)
                    scores(i, (j - 1) // 4, (j - 1) % 4)
                    if after is not None:
                        if j == 1:
                            queries(after, 0)
                        queries(after, j)
                    if j >= 4:
                        turn_p(i, 0, j - 4)
                scores(i, 1, 3)
                turn_p(i, 1, 0)
                values(i, 0, after)
                turn_p(i, 1, 1)
                turn_p(i, 1, 2)
                if after is not None:
                    pe.wait_ge(sem("oT_ready"), i * 4 + 2)
                    key_latents(after, 0)
                turn_p(i, 1, 3)
                if after is not None:
                    turn_kv(after, 0)
                output(i, 0, 0, 4)
                output(i, 0, 4, 8)
                values(i, 1, after)
                output(i, 1, 0, 4)
                if after is not None:
                    pe.wait_ge(sem("oT_ready"), i * 4 + 4)
                    key_latents(after, 1)
                output(i, 1, 4, 6)
                if after is not None:
                    turn_kv(after, 1)
                output(i, 1, 6, 8)

            latents(0)
            queries(0, 0)
            key_latents(0, 0)
            queries(0, 1)
            turn_kv(0, 0)
            for j in range(2, 5):
                queries(0, j)
            pe.wait_ge(sem("kvr_ready"), 1)
            key_latents(0, 1)
            queries(0, 5)
            turn_kv(0, 1)
            for j in range(6, 8):
                queries(0, j)
            with pe.Fori(0, NT // 2 - 1) as i:
                pair4(i, i + 1)
            pair4(NT // 2 - 1, None)
            x_done(pe, 4, NT - 1)
            pe.wait_ge(sem("w5_loaded"), 112)
            for ic in range(DC):
                for oc in range(4):
                    last = nc.tensor.transpose(bank[ic][:, P * oc:P * oc + P], ewkv[:, oc, P * ic:P * ic + P], ident)
                last.then_inc(sem("prep5_psum"), 1)
            pe.wait_ge(sem("prep5_ready"), 2)
            for oc in range(DC):
                for half in range(2):
                    for ic in range(DC):
                        last = nc.tensor.matmul(bank[2 + 2 * oc + half][:], wkvT[:, ic, P * oc:P * oc + P],
                                                cxT[:, ic, 4 * half:4 * half + 4, :].rearrange("p t s -> p (t s)"), start=(ic == 0), stop=(ic == DC - 1))
                    last.then_inc(sem("prep5_psum"), 1)
            pe.wait_ge(sem("prep1_ready"), 6)

            def turn_x(s):
                pe.wait_ge(sem("xi_ready"), s - 4)
                for c in range(DC):
                    b16 = bank[c + (4 if s == 5 else 0)][:].bitcast(BF16)
                    for t in range(NT):
                        last = nc.tensor.transpose(b16[:, P * t:P * t + P], xi[:, t, P * c:P * c + P], identb[:])
                    last.then_inc(sem("xiT_psum"), 1)

            def values_of(k):
                for t in range(2 * k, 2 * k + 2):
                    for ic in range(DC):
                        last = nc.tensor.matmul(bank[k][:, D * (t % 2):D * (t % 2) + D], cxT[:, ic, t, :], wkvT[:, ic, D:2 * D], start=(ic == 0), stop=(ic == DC - 1))
                last.then_inc(sem("v5_psum"), 1)

            pe.wait_ge(sem("eqi_ready"), 1)
            pe.wait_ge(sem("prep5_ready"), 3)
            b16 = bank[2][:].bitcast(BF16)
            for w in range(2):
                for ic in range(DC):
                    for oc in range(DC):
                        at = 512 * w + D * ic + P * oc
                        last = nc.tensor.transpose(b16[:, at:at + P], eqi[:, 2 * w + oc, P * ic:P * ic + P], identb[:])
            last.then_inc(sem("prep5_psum"), 1)
            pe.wait_ge(sem("prep5_ready"), 4)
            nc.tensor.matmul(bank[3][:], cst["ones"], ediag[:].rearrange("p k n -> p (k n)"), start=True, stop=True).then_inc(sem("prep5_psum"), 1)
            values_of(0)
            values_of(1)
            pe.wait_ge(sem("prep5_ready"), 6)
            turn_x(5)
            pe.wait_ge(sem("xiT_ready"), 2)
            pe.wait_ge(sem("prep5_ready"), 8)
            for t in range(NT):
                for ic in range(DC):
                    last = nc.tensor.matmul(bank[4 + t // 2][:, D * (t % 2):D * (t % 2) + D], xiT[:, ic, t, :], ewT[:, 0, ic, :], start=(ic == 0), stop=(ic == DC - 1))
                if t % 2:
                    last.then_inc(sem("q5_psum"), 1)
            values_of(2)
            values_of(3)
            for half in range(2):
                for c in range(DC):
                    pe.wait_ge(sem("q5_ready"), 4 * half + 4)
                    for k in range(4):
                        last = nc.tensor.transpose(bank[4 + 2 * half + c][:, P * k:P * k + P], q5[:, 4 * half + k, P * c:P * c + P], ident)
                    last.then_inc(sem("q5T_psum"), 1)
            pe.wait_ge(sem("prep5_ready"), 11)
            pe.wait_ge(sem("v5_ready"), 4)
            nc.tensor.matmul(bank[0][:, 0:3], cst["ones"], fws[:, 0, :], start=True, stop=True).then_inc(sem("prep5_psum"), 1)
            pe.wait_ge(sem("w6_scale"), 1)
            pe.wait_ge(sem("q5T_ready"), 4)

            def scores5(i, u, g):
                pe.wait_ge(sem("kx_ready"), i * 4 + (2 * u + g // 2 + 1))
                pe.wait_ge(sem("q5s_ready"), i * 2 + (u + 1))
                pe.wait_ge(sem("exp5_ready"), i * 8 + (4 * u + g + 1))
                nc.tensor.matmul(bank[5 + g % 2][:], q5s[:, u, g // 2, :], kx[:, u, g // 2, 4 * (g % 2):4 * (g % 2) + 4, :].rearrange("p h s -> p (h s)"),
                                 start=True, stop=True).then_inc(sem("s5_psum"), 1)

            def turn_p5(i, u, g):
                pe.wait_ge(sem("exp5_ready"), i * 8 + (4 * u + g + 3))
                pe.wait_ge(sem("p5T_act" if g % 2 else "p5T_dve"), i * 4 + (2 * u + g // 2 + 1))
                for k in range(4):
                    last = nc.tensor.transpose(bank[3 + g % 2][:, P * k:P * k + P], s5m[:, u, 4 * g + k, :], ident)
                last.then_inc(sem("pt5_psum"), 1)

            def values5(i, u, g, before):
                if g == 0:
                    pe.wait_ge(sem("v5s_ready"), i * 2 + (u + 1))
                    if u == 0 and before is not None:
                        pe.wait_ge(sem("oi_ready"), before * 2 + 1)
                pe.wait_ge(sem("p5T_act" if g % 2 else "p5T_dve"), i * 4 + (2 * u + g // 2 + 2))
                for h in range(4 * g, 4 * g + 4):
                    last = nc.tensor.matmul(bank[(7, 0)[u]][:, 16 * h:16 * h + 16], p5T[:, u, h, :],
                                            v5s[:, u, 16 * h:16 * h + 16], start=True, stop=True)
                if g == 3:
                    last.then_inc(sem("pv5_psum"), 1)

            def turn_o5(i):
                pe.wait_ge(sem("oi_ready"), i * 2 + 2)
                for u in range(2):
                    for c in range(DC):
                        last = nc.tensor.transpose(bank[1][:, 0:2 * P].bitcast(BF16)[:, D * u + P * c:D * u + P * c + P], oi[:, u, P * c:P * c + P], identb[:])
                last.then_inc(sem("oiT_psum"), 1)

            def output5(i):
                pe.wait_ge(sem("oiT_ready"), i + 1)
                pe.wait_ge(sem("x5_added"), i * 2 + 1)
                for u in range(2):
                    for c in range(DC):
                        last = nc.tensor.matmul(bank[2][:, D * u:D * u + D], oiT[:, u, c, :], ewT[:, 1, c, :], start=(c == 0), stop=(c == DC - 1))
                last.then_inc(sem("out5_psum"), 1)

            def pair5(i, before):
                for j in range(8):
                    scores5(i, j // 4, j % 4)
                    if j >= 1:
                        turn_p5(i, (j - 1) // 4, (j - 1) % 4)
                    if before is not None:
                        if j == 4:
                            turn_o5(before)
                        if j == 6:
                            output5(before)
                    if j >= 2:
                        values5(i, (j - 2) // 4, (j - 2) % 4, before)
                turn_p5(i, 1, 3)
                values5(i, 1, 2, before)
                values5(i, 1, 3, before)

            pair5(0, None)
            with pe.Fori(0, NT // 2 - 1) as i:
                pair5(i + 1, i)
            turn_o5(NT // 2 - 1)
            output5(NT // 2 - 1)
            def turn_ternary(w):
                for ic in range(DC):
                    b16 = bank[2 + 2 * w + ic][:].bitcast(BF16)
                    for oc in range(8):
                        last = nc.tensor.transpose(b16[:, P * oc:P * oc + P], fi[:, w, D * oc + P * ic:D * oc + P * ic + P], identb[:])
                    last.then_inc(sem("w6T_psum"), 1)

            x_done(pe, 5, NT - 1)
            pe.wait_ge(sem("w6_ternary"), 3)
            turn_ternary(0)
            turn_ternary(1)
            for q in range(2):
                b16 = bank[6 + q][:].bitcast(BF16)
                for k in range(4):
                    for oc in range(DC):
                        last = nc.tensor.transpose(b16[:, D * k + P * oc:D * k + P * oc + P], fi[:, 2, 1024 * oc + P * (4 * q + k):1024 * oc + P * (4 * q + k) + P], identb[:])
                last.then_inc(sem("w6T_psum"), 1)
            turn_x(6)
            pe.wait_ge(sem("w6T_ready"), 6)
            pe.wait_ge(sem("xiT_ready"), 4)

            def gate_up(i, u, before):
                for k in range(4):
                    if k == 2 and before is not None:
                        pe.wait_ge(sem("f_step"), before[0] * 10 + (5 * before[1] + 2))
                    for ic in range(DC):
                        last = nc.tensor.matmul(bank[2 * u + k if k < 2 else 2 + k][:], xiT[:, ic, bass.ds(i * 2 + u, 1), :].rearrange("p t s -> p (t s)"),
                                                fguT[:, ic, k // 2, 512 * (k % 2):512 * (k % 2) + 512], start=(ic == 0), stop=(ic == DC - 1))
                    if k % 2:
                        last.then_inc(sem("gu_psum"), 1)

            def down(i, u):
                pe.wait_ge(sem("fhi_ready"), i * 2 + (u + 1))
                b16 = bank[6][:].bitcast(BF16)
                for c in range(8):
                    last = nc.tensor.transpose(b16[:, P * c:P * c + P], fhi[:, u, P * c:P * c + P], identb[:])
                last.then_inc(sem("fhT_psum"), 1)
                pe.wait_ge(sem("fhT_ready"), i * 2 + (u + 1))
                pe.wait_ge(sem("x6_added"), i * 2 + (u + 2))
                for c in range(8):
                    last = nc.tensor.matmul(bank[7][:, 0:D], fhT[:, u, c, :], fdT[:, c, :], start=(c == 0), stop=(c == 7))
                last.then_inc(sem("down_psum"), 1)

            gate_up(0, 0, None)
            gate_up(0, 1, (0, 0))
            with pe.Fori(0, NT // 2 - 1) as i:
                for u in range(2):
                    gate_up(i + 1, u, (i + u, 1 - u))
                    down(i, u)
            for u in range(2):
                down(NT // 2 - 1, u)
    return nc


_INS = ['x', 'fside_S2_0', 'ctx_2048', 'L0_attn_W_q', 'L0_attn_W_kv', 'L0_attn_W_o', 'L0_ffn_W1', 'L0_ffn_b1',
        'L0_ffn_W2', 'L0_ffn_b2', 'L0_ffn_W3', 'L0_ffn_b3', 'L0_ffn_Wg', 'L0_ffn_bg',
        'L1_attn_Wqa', 'L1_attn_Wqb', 'L1_attn_Wkva', 'L1_attn_Wkvb', 'L1_attn_Wo', 'L1_xattn_wq', 'L1_xattn_bq',
        'L1_xattn_wkv', 'L1_xattn_bkv', 'L1_xattn_wp', 'L1_xattn_bp', 'L1_ffn_w_gate', 'L1_ffn_w_up', 'L1_ffn_w_down']


def kernel(**inputs):
    import concourse.bacc as _bacc
    from concourse import mybir as _mybir
    from concourse.bass_utils import run_bass_kernel_spmd as _run

    nc = _bacc.Bacc("TRN2", target_bir_lowering=False, num_devices=1)
    host = {name: np.ascontiguousarray(inputs[name]) for name in _INS}
    taps = inputs["L0_xattn_k"]
    kpad = np.zeros((taps.shape[0], P + D), np.float32)
    kpad[:, P:] = taps
    host["kpad"] = kpad
    host["consts"] = shape_constants()[0]
    arrays, args = {}, {}
    for name, v in host.items():
        arrays[f"in_{name}"] = v
        args[name] = nc.dram_tensor(f"in_{name}", v.shape, _mybir.dt.from_np(v.dtype), kind="ExternalInput").ap()
    out = nc.dram_tensor("out_0", (NT, P, D), F32, kind="ExternalOutput").ap()
    decoder_kernel(nc, args, out)
    r = _run(nc, [arrays], core_ids=[0])
    return r.results[0]["out_0"]
```
